# Optimizing a Trainium2 kernel written in Bass

```python
import numpy as np
import jax
import jax.numpy as jnp

def _softmax(x, axis=-1):
    return jax.nn.softmax(x, axis=axis)

def _gelu(x):
    return jax.nn.gelu(x, approximate=True)

def _silu(x):
    return jax.nn.silu(x)

def _sigmoid(x):
    return jax.nn.sigmoid(x)

def _layernorm(x, axis=-1, eps=1e-05):
    m = jnp.mean(x, axis=axis, keepdims=True)
    v = jnp.var(x, axis=axis, keepdims=True)
    return (x - m) / jnp.sqrt(v + eps)

def _scatter_add(tgt, idx, src, axis=0):
    return tgt.at[idx].add(src)

def _segment_sum(src, seg, n):
    return jax.ops.segment_sum(src, seg, n)
kernel_name = 'mk_sandwich_d1_jaxref_r4_ddfb4d'

def setup_inputs(seed: int=0):
    np.random.seed(seed)
    _w = jnp.asarray

    def _L0_attn_setup():
        import jax, jax.numpy as jnp
        import numpy as np
        H = 256
        NH = 16
        HD = H // NH
        EPS = 1e-05

        def _attn_block(x, ln_gamma, ln_beta, W_qkv, b_qkv, W_out, b_out):
            B, S, _ = x.shape
            mu = jnp.mean(x, axis=-1, keepdims=True)
            var = jnp.mean(jnp.square(x - mu), axis=-1, keepdims=True)
            xn = (x - mu) / jnp.sqrt(var + EPS) * ln_gamma + ln_beta
            qkv = jnp.einsum('bsh,oh->bso', xn, W_qkv) + b_qkv
            qkv = qkv.reshape(B, S, 3, NH, HD).transpose(2, 0, 3, 1, 4)
            q, k, v = (qkv[0], qkv[1], qkv[2])
            scores = jnp.einsum('bhqd,bhkd->bhqk', q, k) / jnp.sqrt(jnp.asarray(HD, x.dtype))
            probs = jax.nn.softmax(scores, axis=-1)
            ctx = jnp.einsum('bhqk,bhkd->bhqd', probs, v)
            ctx = ctx.transpose(0, 2, 1, 3).reshape(B, S, H)
            out = jnp.einsum('bsh,oh->bso', ctx, W_out) + b_out
            return x + out
        key = jax.random.key(seed)
        ks = jax.random.split(key, 5)
        b_qkv = float(np.sqrt(6.0 / (H + 3 * H)))
        b_out = float(np.sqrt(6.0 / (H + H)))
        return {'hidden_states': jax.random.normal(ks[0], (2, 512, H), dtype=jnp.float32), 'ln_gamma': jnp.ones((H,), jnp.float32), 'ln_beta': jnp.zeros((H,), jnp.float32), 'W_qkv': jax.random.uniform(ks[1], (3 * H, H), jnp.float32, -b_qkv, b_qkv), 'b_qkv': jnp.zeros((3 * H,), jnp.float32), 'W_out': jax.random.uniform(ks[2], (H, H), jnp.float32, -b_out, b_out), 'b_out': jnp.zeros((H,), jnp.float32)}
    _L0_attn_in = _L0_attn_setup()

    def _L0_ffn_setup():
        import jax, jax.numpy as jnp
        import numpy as np
        TOP_K = 2
        key = jax.random.key(seed)
        k1, k2, k3, k4, k5 = jax.random.split(key, 5)
        B, S, D, F, E = (2, 256, 256, 512, 8)
        return {'x': jax.random.normal(k1, (B, S, D), dtype=jnp.float32), 'router_kernel_DE': jax.random.normal(k2, (D, E), dtype=jnp.float32) * 0.02, 'kernel_gating_EDF': jax.random.normal(k3, (E, D, F), dtype=jnp.float32) * 0.02, 'kernel_up_EDF': jax.random.normal(k4, (E, D, F), dtype=jnp.float32) * 0.02, 'kernel_down_EFD': jax.random.normal(k5, (E, F, D), dtype=jnp.float32) * 0.02}
    _L0_ffn_in = _L0_ffn_setup()
    _d = {'L0_attn_hidden_states': _L0_attn_in['hidden_states'], 'L0_attn_ln_gamma': _L0_attn_in['ln_gamma'], 'L0_attn_ln_beta': _L0_attn_in['ln_beta'], 'L0_attn_W_qkv': _L0_attn_in['W_qkv'], 'L0_attn_b_qkv': _L0_attn_in['b_qkv'], 'L0_attn_W_out': _L0_attn_in['W_out'], 'L0_attn_b_out': _L0_attn_in['b_out'], 'L0_ffn_router_kernel_DE': _L0_ffn_in['router_kernel_DE'], 'L0_ffn_kernel_gating_EDF': _L0_ffn_in['kernel_gating_EDF'], 'L0_ffn_kernel_up_EDF': _L0_ffn_in['kernel_up_EDF'], 'L0_ffn_kernel_down_EFD': _L0_ffn_in['kernel_down_EFD']}
    _x0 = _d['L0_attn_hidden_states']
    _d['L0_attn_hidden_states'] = jax.random.normal(jax.random.fold_in(jax.random.key(seed), 1), (16, 512, 256), dtype=_x0.dtype)
    del _x0
    return _d

def reference(L0_attn_hidden_states, L0_attn_ln_gamma, L0_attn_ln_beta, L0_attn_W_qkv, L0_attn_b_qkv, L0_attn_W_out, L0_attn_b_out, L0_ffn_router_kernel_DE, L0_ffn_kernel_gating_EDF, L0_ffn_kernel_up_EDF, L0_ffn_kernel_down_EFD):

    def _L0_attn_ref(hidden_states, ln_gamma, ln_beta, W_qkv, b_qkv, W_out, b_out):
        import jax, jax.numpy as jnp
        import numpy as np
        H = 256
        NH = 16
        HD = H // NH
        EPS = 1e-05

        def _attn_block(x, ln_gamma, ln_beta, W_qkv, b_qkv, W_out, b_out):
            B, S, _ = x.shape
            mu = jnp.mean(x, axis=-1, keepdims=True)
            var = jnp.mean(jnp.square(x - mu), axis=-1, keepdims=True)
            xn = (x - mu) / jnp.sqrt(var + EPS) * ln_gamma + ln_beta
            qkv = jnp.einsum('bsh,oh->bso', xn, W_qkv) + b_qkv
            qkv = qkv.reshape(B, S, 3, NH, HD).transpose(2, 0, 3, 1, 4)
            q, k, v = (qkv[0], qkv[1], qkv[2])
            scores = jnp.einsum('bhqd,bhkd->bhqk', q, k) / jnp.sqrt(jnp.asarray(HD, x.dtype))
            probs = jax.nn.softmax(scores, axis=-1)
            ctx = jnp.einsum('bhqk,bhkd->bhqd', probs, v)
            ctx = ctx.transpose(0, 2, 1, 3).reshape(B, S, H)
            out = jnp.einsum('bsh,oh->bso', ctx, W_out) + b_out
            return x + out
        return _attn_block(hidden_states, ln_gamma, ln_beta, W_qkv, b_qkv, W_out, b_out)

    def _L0_ffn_ref(x, router_kernel_DE, kernel_gating_EDF, kernel_up_EDF, kernel_down_EFD):
        import jax, jax.numpy as jnp
        import numpy as np
        TOP_K = 2
        E = router_kernel_DE.shape[-1]
        x = x.astype(jnp.float32)
        logits_BSE = jnp.einsum('BSD,DE->BSE', x, router_kernel_DE)
        probs_BSE = jax.nn.softmax(logits_BSE.astype(jnp.float32), axis=-1)
        weights_BSK, indices_BSK = jax.lax.top_k(probs_BSE, TOP_K)
        norm_weights_BSK = jax.nn.softmax(weights_BSK, axis=-1)
        one_hot_BSKE = jax.nn.one_hot(indices_BSK, num_classes=E, dtype=x.dtype)
        full_weights_BSE = jnp.sum(one_hot_BSKE * norm_weights_BSK[..., None], axis=2)
        gating_BSEF = jnp.einsum('BSD,EDF->BSEF', x, kernel_gating_EDF)
        act_BSEF = jax.nn.silu(gating_BSEF)
        up_BSEF = jnp.einsum('BSD,EDF->BSEF', x, kernel_up_EDF)
        fuse_BSEF = act_BSEF * up_BSEF
        down_BSED = jnp.einsum('BSEF,EFD->BSED', fuse_BSEF, kernel_down_EFD)
        out_BSD = jnp.einsum('BSED,BSE->BSD', down_BSED, full_weights_BSE)
        return out_BSD.astype(jnp.float32)
    x = L0_attn_hidden_states
    x = x + _layernorm(_L0_attn_ref(_layernorm(x, axis=-1), L0_attn_ln_gamma, L0_attn_ln_beta, L0_attn_W_qkv, L0_attn_b_qkv, L0_attn_W_out, L0_attn_b_out), axis=-1)
    x = x + _layernorm(_L0_ffn_ref(_layernorm(x, axis=-1), L0_ffn_router_kernel_DE, L0_ffn_kernel_gating_EDF, L0_ffn_kernel_up_EDF, L0_ffn_kernel_down_EFD), axis=-1)
    return x

_drawn_inputs = setup_inputs


def setup_inputs(seed=0):
    import zlib

    import numpy as np

    out = dict(_drawn_inputs(seed))
    spreads = {'L0_attn_ln_gamma': (1.0, 0.2),
     'L0_attn_ln_beta': (0.0, 0.1),
     'L0_attn_b_qkv': (0.0, 0.1),
     'L0_attn_b_out': (0.0, 0.1)}
    factors = {}
    for name, (base, spread) in spreads.items():
        noise = np.random.default_rng([zlib.crc32(name.encode()), seed]).standard_normal(out[name].shape)
        drawn = base * np.exp(spread * noise) if base else spread * noise
        out[name] = jnp.asarray(drawn.astype(out[name].dtype))
    for name, factor in factors.items():
        out[name] = (out[name] * factor).astype(out[name].dtype)
    return out
```

```python
from contextlib import ExitStack

import concourse.bass as bass
from concourse import mybir

F32 = mybir.dt.float32
F32R = mybir.dt.float32r
BF16 = mybir.dt.bfloat16
I32 = mybir.dt.int32
ALU = mybir.AluOpType
ACT = mybir.ActivationFunctionType
AX_X = mybir.AxisListType.X

P = 128
NH = 16
HD = 16
EPS = 1e-5
G = 4
HG = NH // G
VW = 32
KR = 96
KM = KR + 2


def split3(pe, out, stat_hi, stat_lo, mov_hi, mov_lo):
    n = len(stat_hi)
    for c in range(n):
        pe.matmul(out, stat_hi[c], mov_hi[c], start=(c == 0), stop=False)
        pe.matmul(out, stat_hi[c], mov_lo[c], start=False, stop=False)
        last = pe.matmul(out, stat_lo[c], mov_hi[c], start=False, stop=(c == n - 1))
    return last


def carry(eng, passed):
    eng.sem_inc(passed, 1)


def clears(T):
    return T // 512 + 2 + -(-(E * region(T) // P) // (5 * P))


def prepare_weights(nc, W, w_qkv, b_qkv, w_out, b_out, gamma, beta, acc_d, xn2_d, table_d, cleared):
    with ExitStack() as ctx:
        def sb(name, shape, dt=F32):
            return ctx.enter_context(nc.sbuf_tensor(name, shape, dt))

        def sem(name):
            return ctx.enter_context(nc.semaphore(name))

        wq_in = sb("wq_in", [P, 6, 256])
        wo_in = sb("wo_in", [P, 2, 256])
        wo_t = sb("wo_t", [P, 2, 256])
        beta_rows = sb("beta_rows", [P, 256])
        bo_rows = sb("bo_rows", [P, 256])
        gamma_col = sb("gamma_col", [P, 2])
        bq_col = sb("bq_col", [P, 6])
        wbeta = sb("wbeta", [P, 6, 256])
        wb_col = sb("wb_col", [P, 6])
        bv_wide = sb("bv_wide", [P, 2, P])
        bank = [ctx.enter_context(nc.psum_tensor(f"prep_bank{i}", [P, 512], F32)) for i in range(2)]
        loaded = sem("w_loaded")
        ident0 = sem("w_ident0")
        ident_ready = sem("w_ident_ready")
        turned = sem("w_turned")
        hi_done = sem("w_hi_done")
        raw_done = sem("w_raw_done")
        lo_done = sem("w_lo_done")
        bias_step = sem("w_bias_step")
        bo_ready = sem("w_bo_ready")
        bo_done = sem("w_bo_done")
        ones_done = sem("w_ones_done")

        T = acc_d.shape[0] - P
        zeros = sb("zeros", [P, 4, 256])
        filler = sb("filler", [P, 5, P, 2], I32)
        zeros_ready, filler_step = sem("w_zeros"), sem("w_filler")
        jobs = [("q", o, c) for c in range(2) for o in range(6)] + [("o", o, c) for c in range(2) for o in range(2)]
        with nc.Block() as block:
            @block.sync
            def _(sp):
                with nc.allow_non_contiguous_dma(reason="bias and gamma columns, once"):
                    sp.dma_start(wq_in[:], w_qkv.rearrange("(t p) h -> p t h", p=P)).then_inc(loaded, 16)
                    sp.dma_start(wo_in[:], w_out.rearrange("(t p) h -> p t h", p=P)).then_inc(loaded, 16)
                    sp.dma_start(beta_rows[:], beta.unsqueeze(0).to_broadcast([P, 256])).then_inc(loaded, 16)
                    sp.dma_start(bo_rows[:], b_out.unsqueeze(0).to_broadcast([P, 256])).then_inc(loaded, 16)
                    sp.dma_start(gamma_col[:], gamma.rearrange("(c p) -> p c", p=P)).then_inc(loaded, 16)
                    sp.dma_start(bq_col[:], b_qkv.rearrange("(c p) -> p c", p=P)).then_inc(loaded, 16)

                sp.wait_ge(zeros_ready, 1)
                for n in range(T // 512):
                    sp.dma_start(acc_d[n * 512:(n + 1) * 512, :].rearrange("(p t) h -> p t h", t=4), zeros[:]).then_inc(cleared, 16)
                sp.dma_start(acc_d[T:, :], zeros[:, 0, :]).then_inc(cleared, 16)
                sp.dma_start(xn2_d[T:, :], zeros[:, 0, :]).then_inc(cleared, 16)
                rows = table_d.shape[0] // P
                table = table_d.rearrange("(p r) c -> p (r c)", p=P)
                sp.wait_ge(filler_step, 6)
                for n in range(0, rows, 5 * P):
                    m = min(5 * P, rows - n)
                    sp.dma_start(table[:, 2 * n:2 * (n + m)], filler[:].rearrange("p a q c -> p (a q c)")[:, 0:2 * m]).then_inc(cleared, 16)
                sp.wait_ge(cleared, 16 * clears(T))

            @block.gpsimd
            def _(pool):
                nc.gpsimd.memset(filler[:], 0).then_inc(filler_step, 1)
                pool.wait_ge(filler_step, 1)
                for n in range(5):
                    nc.gpsimd.iota(filler[:, n, :, 0], pattern=[[1, P]], base=T, channel_multiplier=0).then_inc(filler_step, 1)
                    pool.wait_ge(filler_step, n + 2)
                nc.gpsimd.memset(W["ident"][:], 0.0).then_inc(ident0, 1)
                pool.wait_ge(ident0, 1)
                nc.gpsimd.affine_select(out=W["ident"][:], in_=W["ident"][:], compare_op=ALU.not_equal, fill=1.0,
                                        base=0, pattern=[[-1, P]], channel_multiplier=1).then_inc(ident_ready, 1)
                nc.gpsimd.memset(W["v_aug"][:], 0.0).then_inc(ones_done, 1)
                nc.gpsimd.memset(W["q_st"][:].bitcast(F32), 0.0).then_inc(ones_done, 1)
                nc.gpsimd.memset(W["k_st"][:].bitcast(F32), 0.0).then_inc(ones_done, 1)
                nc.gpsimd.memset(W["neg_half"][:], -0.5).then_inc(ones_done, 1)
                pool.wait_ge(ones_done, 4)
                nc.gpsimd.memset(W["v_aug"][:, :, :, HD:HD + 1], 1.0).then_inc(ones_done, 1)
                pool.wait_ge(ones_done, 5)
                nc.gpsimd.memset(W["k_st"][KR:KM].bitcast(F32), 1.0).then_inc(ones_done, 1)
                pool.wait_ge(ones_done, 6)

            @block.tensor
            def _(pe):
                pe.wait_ge(loaded, 96)
                pe.wait_ge(ident_ready, 1)
                for n, (kind, o, c) in enumerate(jobs):
                    if n >= 2:
                        pe.wait_ge(lo_done, n - 1)
                    src = wq_in if kind == "q" else wo_in
                    nc.tensor.transpose(bank[n % 2][:, 0:P], src[:, o, c * P:(c + 1) * P], W["ident"][:]).then_inc(turned, 1)
                pe.wait_ge(bias_step, 4)
                pe.wait_ge(raw_done, 4)
                pe.wait_ge(lo_done, len(jobs))
                for c in range(2):
                    last = nc.tensor.matmul(bank[0][:, 0:256], bv_wide[:, c, :], wo_t[:, c, :], start=(c == 0), stop=(c == 1))
                last.then_inc(bo_ready, 1)

            @block.scalar
            def _(act):
                act.wait_ge(loaded, 96)
                for n, (kind, o, c) in enumerate(jobs):
                    act.wait_ge(turned, n + 1)
                    cols = slice(o * P, (o + 1) * P)
                    if kind == "q":
                        nc.scalar.activation(W["wq_hi"][:, c, cols], bank[n % 2][:, 0:P], ACT.Copy,
                                             scale=gamma_col[:, c:c + 1]).then_inc(hi_done, 1)
                    else:
                        nc.scalar.activation(wo_t[:, c, cols], bank[n % 2][:, 0:P], ACT.Copy).then_inc(raw_done, 1)
                        nc.scalar.activation(W["wo_hi"][:, c, cols], bank[n % 2][:, 0:P], ACT.Copy).then_inc(hi_done, 1)

            @block.vector
            def _(dve):
                nc.vector.memset(zeros[:], 0.0).then_inc(zeros_ready, 1)
                dve.wait_ge(loaded, 96)
                nc.vector.tensor_tensor(wbeta[:], wq_in[:], beta_rows[:].unsqueeze(1).to_broadcast([P, 6, 256]), ALU.mult).then_inc(bias_step, 1)
                dve.wait_ge(bias_step, 1)
                nc.vector.reduce_sum(wb_col[:], wbeta[:], AX_X).then_inc(bias_step, 1)
                dve.wait_ge(bias_step, 2)
                nc.vector.tensor_tensor(W["b_col"][:], wb_col[:], bq_col[:], ALU.add).then_inc(bias_step, 1)
                dve.wait_ge(bias_step, 3)
                nc.vector.tensor_copy(bv_wide[:], W["b_col"][:, 4:6].unsqueeze(2).to_broadcast([P, 2, P])).then_inc(bias_step, 1)
                for n, (kind, o, c) in enumerate(jobs):
                    dve.wait_ge(hi_done, n + 1)
                    cols = slice(o * P, (o + 1) * P)
                    if kind == "q":
                        nc.vector.scalar_tensor_tensor(out=W["wq_lo"][:, c, cols], in0=bank[n % 2][:, 0:P],
                                                       scalar=gamma_col[:, c:c + 1], in1=W["wq_hi"][:, c, cols].bitcast(F32),
                                                       op0=ALU.mult, op1=ALU.subtract).then_inc(lo_done, 1)
                    else:
                        nc.vector.tensor_tensor(W["wo_lo"][:, c, cols], bank[n % 2][:, 0:P],
                                                W["wo_hi"][:, c, cols].bitcast(F32), ALU.subtract).then_inc(lo_done, 1)
                dve.wait_ge(bo_ready, 1)
                nc.vector.tensor_tensor(W["bo"][:], bank[0][:, 0:256], bo_rows[:], ALU.add).then_inc(bo_done, 1)
                dve.wait_ge(bo_done, 1)


USES = [
    (0, "mt", 1, 0),
    (1, "v", 1, 0), (1, "cx", 3, -1),
    (2, "zt", 0, 1),
    (3, "zt", 1, 1), (3, "cn", 0, -1),
    (4, "mt", 2, 0), (4, "qk", 0, 1), (4, "cn", 1, -1),
    (5, "qk", 1, 1), (5, "cx", 0, 0),
    (6, "qk", 2, 1), (6, "xt", 0, -2),
    (7, "qk", 3, 1), (7, "xt", 1, -2),
    (8, "mt", 3, 0), (8, "out", 0, -1),
    (9, "cx", 1, 0), (9, "out", 1, -1),
    (10, "lg", 0, -2),
    (12, "mt", 0, 1),
    (13, "cx", 2, 0),
    (15, "v", 0, 1),
]
PER = {"mt": 4, "v": 2, "cx": 4, "zt": 2, "cn": 2, "qk": 4, "xt": 2, "out": 2, "lg": 1}
NB = 3
BANK = {(kind, i): n % NB for n, (_, kind, i, _) in enumerate(USES)}


def attention(nc, W, x, y_d, x2_d, xn2_d, lg_d, qk_d, mt_d, router):
    B = x.shape[0]
    with ExitStack() as ctx:
        def sb(name, shape, dt=F32):
            return ctx.enter_context(nc.sbuf_tensor("a_" + name, shape, dt))

        def sem(name):
            return ctx.enter_context(nc.semaphore("a_" + name))

        v_aug, q_st, k_st, ident = W["v_aug"], W["q_st"], W["k_st"], W["ident"]
        xa = sb("xa", [P, 4, 256])
        y = sb("y", [P, 4, 256])
        z = sb("z", [P, 4, 256])
        z_hi = sb("z_hi", [P, 2, 512], F32R)
        z_lo = sb("z_lo", [P, 2, 512], F32R)
        qk_hi = sb("qk_hi", [P, 4, 512], F32R)
        qk_lo = sb("qk_lo", [P, 4, 512], F32R)
        probs = sb("probs", [P, 2, HG, 512])
        mx = sb("mx", [P, 2, 16])
        mt = sb("mt", [16, 2, 2, P], F32R)
        ctx_t = sb("ctx_t", [P, 2, 512])
        rsum = sb("rsum", [P, 16])
        cn = sb("cn", [P, 4, 256])
        c_hi = sb("c_hi", [P, 2, 512], F32R)
        c_lo = sb("c_lo", [P, 2, 512], F32R)
        xp = sb("xp", [P, 4, 256])
        yp = sb("yp", [P, 4, 256])
        a = sb("a", [P, 4, 256])
        x2 = sb("x2", [P, 4, 256])
        xn2 = sb("xn2", [P, 4, 256])
        x_t = sb("x_t", [P, 2, 512])
        lgt = sb("lgt", [8, 512])
        wr = sb("wr", [P, 2, 8])
        st = {k: sb(f"st{k}", [P, 4, 2]) for k in (1, 3, 4)}
        bst = {k: sb(f"bst{k}", [P, 4, 6]) for k in (1, 3, 4)}
        rs = {k: sb(f"rs{k}", [P, 4]) for k in (1, 3, 4)}
        r2 = sb("r2", [P, 4])
        t2 = sb("t2", [P, 4])

        misc = [ctx.enter_context(nc.psum_tensor(f"misc{i}", [P, 512], F32)) for i in range(NB)]
        sm = [ctx.enter_context(nc.psum_tensor(f"sm{i}", [P, 512], F32)) for i in range(2)]
        stp = [ctx.enter_context(nc.psum_tensor(f"stp{i}", [P, 512], F32)) for i in range(2)]
        cacc = ctx.enter_context(nc.psum_tensor("cacc", [P, 512], F32))

        wr_in = sem("wr_in")
        sp_passed, pool_passed, dve_passed = sem("sp_passed"), sem("pool_passed"), sem("dve_passed")
        x_in, xp_in, yp_in = sem("x_in"), sem("xp_in"), sem("yp_in")
        y_out, x2_out, xn2_out, lg_out = sem("y_out"), sem("x2_out"), sem("xn2_out"), sem("lg_out")
        qk_w = [sem(f"qk_w{c}") for c in range(2)]
        stack_in = [sem(f"stack_in{g}") for g in range(G)]
        mt_w = sem("mt_w")
        m_in = [sem(f"m_in{g}") for g in range(G)]
        full = {k: sem(f"{k}_full") for k in PER}
        zt_hi, qkh, cnh, mth = sem("zt_hi"), sem("qk_hi"), sem("cn_hi"), sem("mt_hi")
        free = {k: sem(f"{k}_free") for k in PER}
        sm_full = sem("sm_full")
        max_done = [sem(f"max_done{k}") for k in range(2)]
        st_full, exp_done = sem("st_full"), sem("exp_done")
        pv_done, ctx_full, ctx_evac = sem("pv_done"), sem("ctx_full"), sem("ctx_evac")
        bn = {k: sem(f"bn{k}") for k in (1, 3, 4)}
        agg = {k: sem(f"agg{k}") for k in (1, 3, 4)}
        rstd = {k: sem(f"rstd{k}") for k in (1, 3, 4)}
        y_done, z_done = sem("y_done"), sem("z_done")
        recip = sem("recip")
        yp_done, lna_done, x2_done, xn2_done = sem("yp_done"), sem("lna_done"), sem("x2_done"), sem("xn2_done")

        def wait(eng, s, value):
            if not (isinstance(value, int) and value <= 0):
                eng.wait_ge(s, value)

        def there(b, lag):
            return not isinstance(b, int) or 0 <= b + lag < B

        def before(b, kind, i):
            at = [(k, j) for _, k, j, _ in USES].index((kind, i))
            for back in range(1, 4 * len(USES)):
                pos = at - back
                _, k, j, lag = USES[pos % len(USES)]
                it = b + pos // len(USES)
                if BANK[k, j] == BANK[kind, i] and there(it, lag):
                    return k, (it + lag) * PER[k] + j + 1
            return None

        def iterations(eng, body):
            for b in range(-2, 2):
                body(b)
            if B > 4:
                with eng.Fori(2, B - 2) as b:
                    body(b)
            for b in range(max(B - 2, 2), B + 2):
                body(b)

        with nc.Block() as block:
            @block.sync
            def _(sp):
                sp.dma_start(wr[:], router.rearrange("(c p) e -> p c e", p=P)).then_inc(wr_in, 16)

                def write_qk(i, c):
                    wait(sp, free["qk"], 4 * i + 2 * c + 2)
                    carry(sp, sp_passed)
                    wait(sp, stack_in[2 * c], 96 * i)
                    wait(sp, stack_in[2 * c + 1], 96 * i)
                    for part, src in enumerate((qk_hi, qk_lo)):
                        for k in range(2):
                            sp.dma_start(qk_d[2 * k + part, c * P:(c + 1) * P, :], src[:, 2 * c + k, :].bitcast(F32)).then_inc(qk_w[c], 16)

                def stack(i, g, old):
                    c = g // 2
                    wait(sp, qk_w[c], 64 * (i + 1))
                    carry(sp, sp_passed)
                    wait(sp, st_full, old)
                    for st_, parts in ((q_st, (0, 0, 1)), (k_st, (2, 3, 2))):
                        for r, part in enumerate(parts):
                            src = qk_d[part, g * 64:(g + 1) * 64, :].rearrange("(h d) n -> d h n", d=HD)
                            sp.dma_start(st_[r * HD:(r + 1) * HD, g, :, :].bitcast(F32), src).then_inc(stack_in[g], 16)

                def max_rows(i, g, n):
                    wait(sp, free["mt"], n + 1)
                    wait(sp, m_in[(g - 1) % 4], 16 * (i + (g > 0)))
                    sp.dma_start(mt_d.rearrange("r (k n) -> k r n", n=P), mt[:, g % 2, :, :].bitcast(F32)).then_inc(mt_w, 16)
                    wait(sp, mt_w, 16 * (n + 1))
                    sp.dma_start(q_st[KR:KM, g, :, :].rearrange("r h n -> r (h n)").bitcast(F32), mt_d).then_inc(m_in[g], 16)

                def body(b):
                    n = 4 * b
                    if there(b, 0):
                        max_rows(b, 1, n + 1)
                        stack(b, 3, 64 * b)
                        max_rows(b, 2, n + 2)
                    if there(b, 1):
                        write_qk(b + 1, 0)
                        stack(b + 1, 0, 16 * (n + 1))
                        write_qk(b + 1, 1)
                        stack(b + 1, 1, 16 * (n + 2))
                    if there(b, 0):
                        max_rows(b, 3, n + 3)
                    if there(b, 1):
                        stack(b + 1, 2, 16 * (n + 3))
                        max_rows(b + 1, 0, n + 4)
                iterations(sp, body)

            @block.gpsimd
            def _(pool):
                def rsqrt(k, i, steps, first, src, dst):
                    carry(pool, pool_passed)
                    nc.gpsimd.tensor_scalar(dst, src, EPS, None, ALU.add).then_inc(rstd[k], 1)
                    wait(pool, rstd[k], steps * i + first + 1)
                    nc.gpsimd.tensor_tensor(dst, dst, W["neg_half"][:, 0:4], ALU.pow).then_inc(rstd[k], 1)
                    wait(pool, rstd[k], steps * i + first + 2)

                def rows(dram, i):
                    return dram[bass.ts(i, 512), :].rearrange("(t p) h -> p t h", p=P)

                def body(b):
                    if there(b, 2):
                        i = b + 2
                        wait(pool, y_done, 4 * i)
                        carry(pool, pool_passed)
                        pool.dma_start(xa[:], rows(x.rearrange("b s h -> (b s) h"), i)).then_inc(x_in, 16)
                    if there(b, -2):
                        i = b - 2
                        wait(pool, xn2_done, 4 * (i + 1))
                        carry(pool, pool_passed)
                        pool.dma_start(rows(xn2_d, i), xn2[:]).then_inc(xn2_out, 16)
                    if there(b, -1):
                        i = b - 1
                        wait(pool, x2_done, i)
                        carry(pool, pool_passed)
                        pool.dma_start(xp[:], rows(x.rearrange("b s h -> (b s) h"), i)).then_inc(xp_in, 16)
                        wait(pool, free["out"], 2 * i)
                        wait(pool, y_out, 16 * (i + 1))
                        carry(pool, pool_passed)
                        pool.dma_start(yp[:], rows(y_d, i)).then_inc(yp_in, 16)
                        wait(pool, yp_in, 16 * (i + 1))
                        nc.gpsimd.tensor_tensor(yp[:], yp[:], W["bo"][:].unsqueeze(1).to_broadcast([P, 4, 256]), ALU.add).then_inc(yp_done, 1)
                        wait(pool, agg[3], 4 * (i + 1))
                        rsqrt(3, i, 2, 0, st[3][:, :, 1], rs[3][:])
                    if there(b, 2):
                        i = b + 2
                        wait(pool, agg[1], 4 * (i + 1))
                        rsqrt(1, i, 6, 0, st[1][:, :, 1], rs[1][:])
                        nc.gpsimd.tensor_tensor(t2[:], rs[1][:], rs[1][:], ALU.mult).then_inc(rstd[1], 1)
                        wait(pool, rstd[1], 6 * i + 3)
                        nc.gpsimd.tensor_tensor(t2[:], t2[:], st[1][:, :, 1], ALU.mult).then_inc(rstd[1], 1)
                        wait(pool, rstd[1], 6 * i + 4)
                        wait(pool, z_done, 4 * i)
                        rsqrt(1, i, 6, 4, t2[:], r2[:])
                    if there(b, -1):
                        i = b - 1
                        wait(pool, lna_done, 4 * (i + 1))
                        wait(pool, xp_in, 16 * (i + 1))
                        wait(pool, x2_out, 16 * i)
                        wait(pool, xn2_done, 4 * i)
                        nc.gpsimd.tensor_tensor(x2[:], xp[:], a[:], ALU.add).then_inc(x2_done, 1)
                        wait(pool, agg[4], 4 * (i + 1))
                        rsqrt(4, i, 2, 0, st[4][:, :, 1], rs[4][:])
                        wait(pool, x2_done, i + 1)
                        carry(pool, pool_passed)
                        pool.dma_start(rows(x2_d, i), x2[:]).then_inc(x2_out, 16)
                    if there(b, -2):
                        i = b - 2
                        wait(pool, free["lg"], i + 1)
                        carry(pool, pool_passed)
                        pool.dma_start(lg_d[:, bass.ts(i, 512)], lgt[:]).then_inc(lg_out, 16)
                    if there(b, 2):
                        i = b + 2
                        wait(pool, y_done, 4 * (i + 1))
                        carry(pool, pool_passed)
                        pool.dma_start(rows(y_d, i), y[:]).then_inc(y_out, 16)
                iterations(pool, body)
                for s in (y_out, x2_out, xn2_out, lg_out):
                    pool.wait_ge(s, 16 * B)

            @block.tensor
            def _(pe):
                te = nc.tensor

                def bank_for(b, kind, i):
                    prev = before(b, kind, i)
                    if prev is not None:
                        wait(pe, free[prev[0]], prev[1])
                    return misc[BANK[kind, i]]

                def turn(bank, src, c):
                    for t in range(4):
                        last = te.transpose(bank[:, t * P:(t + 1) * P], src[:, t, c * P:(c + 1) * P], ident[:])
                    return last

                def use(b, kind, i, d):
                    bank = bank_for(b, kind, i)
                    if kind == "zt":
                        wait(pe, z_done, 4 * (d + 1))
                        last = turn(bank, z, i)
                    elif kind == "qk":
                        wait(pe, free["zt"], 2 * (d + 1))
                        col = (i % 2) * 256 + (i // 2) * P
                        last = split3(te, bank[:], [W["wq_hi"][:, c, col:col + P] for c in range(2)],
                                      [W["wq_lo"][:, c, col:col + P] for c in range(2)],
                                      [z_hi[:, c, :] for c in range(2)], [z_lo[:, c, :] for c in range(2)])
                    elif kind == "v":
                        wait(pe, free["zt"], 2 * (d + 1))
                        for half in range(2):
                            tk = slice((2 * i + half) * P, (2 * i + half + 1) * P)
                            last = split3(te, bank[:, half * 256:(half + 1) * 256],
                                          [z_hi[:, c, tk] for c in range(2)], [z_lo[:, c, tk] for c in range(2)],
                                          [W["wq_hi"][:, c, 512:768] for c in range(2)],
                                          [W["wq_lo"][:, c, 512:768] for c in range(2)])
                    elif kind == "mt":
                        wait(pe, max_done[1], 8 * (4 * d + i + 1))
                        last = te.transpose(bank[0:16, 0:P], mx[:, i % 2, :], ident[:])
                    elif kind == "cx":
                        wait(pe, ctx_evac, 4 * d + i + 1)
                        for t in range(4):
                            last = te.transpose(bank[:, t * P:(t + 1) * P], ctx_t[:, i % 2, t * P:(t + 1) * P], ident[:])
                    elif kind == "cn":
                        wait(pe, free["cx"], 4 * (d + 1))
                        last = turn(bank, cn, i)
                    elif kind == "out":
                        wait(pe, free["cn"], 2 * (d + 1))
                        for half in range(2):
                            tk = slice((2 * i + half) * P, (2 * i + half + 1) * P)
                            last = split3(te, bank[:, half * 256:(half + 1) * 256],
                                          [c_hi[:, c, tk] for c in range(2)], [c_lo[:, c, tk] for c in range(2)],
                                          [W["wo_hi"][:, c, :] for c in range(2)], [W["wo_lo"][:, c, :] for c in range(2)])
                    elif kind == "xt":
                        wait(pe, xn2_done, 4 * (d + 1))
                        last = turn(bank, xn2, i)
                    else:
                        wait(pe, free["xt"], 2 * (d + 1))
                        for c in range(2):
                            last = te.matmul(bank[0:8, :], wr[:, c, :], x_t[:, c, :], start=(c == 0), stop=(c == 1))
                    last.then_inc(full[kind], 1)

                def body(b):
                    for s in range(16):
                        g, j = s // 4, s % 4
                        da, ga = b + (g >= 2), (g + 2) % 4
                        for r in range(4):
                            if there(b, int(g >= 2)):
                                if j == 0 and r == 0:
                                    wait(pe, stack_in[ga], 96 * (da + 1))
                                wait(pe, max_done[r % 2], 32 * da + 8 * ga + 2 * j + r // 2)
                                te.matmul(sm[r % 2][:], q_st[0:KR, ga, j, r * P:(r + 1) * P], k_st[0:KR, ga, j, :],
                                          start=True, stop=True).then_inc(sm_full, 1)
                            if there(b, 0):
                                if j == 0 and r == 0:
                                    wait(pe, m_in[g], 16 * (b + 1))
                                wait(pe, exp_done, 64 * b + 4 * s + r - 1)
                                te.matmul(stp[r % 2][:], k_st[0:KM, g, r, j * P:(j + 1) * P], q_st[0:KM, g, r, :],
                                          start=True, stop=True).then_inc(st_full, 1)
                        lag = -1 if s == 0 else 0
                        if there(b, lag):
                            q = 16 * b + s - 1
                            gq, jq = (s - 1) % 16 // 4, (s - 1) % 4
                            wait(pe, exp_done, 4 * (q + 1))
                            if jq % 2 == 0:
                                wait(pe, free["v"], 2 * (b + lag) + jq // 2 + 1)
                            if jq == 0:
                                wait(pe, ctx_evac, 4 * b + gq)
                            for h in range(HG):
                                last = te.matmul(cacc[32 * h:32 * h + 32, :], v_aug[:, jq, HG * gq + h, :],
                                                 probs[:, jq % 2, h, :], start=(jq == 0), stop=(jq == 3),
                                                 skip_group_check=True)
                            last.then_inc(pv_done, 1)
                        for slot, kind, i, lag in USES:
                            if slot == s and there(b, lag):
                                use(b, kind, i, b + lag)
                pe.wait_ge(wr_in, 16)
                iterations(pe, body)

            @block.scalar
            def _(act):
                sc = nc.scalar

                def extra(b, kind, i, lag):
                    if not there(b, lag):
                        return
                    d = b + lag
                    bank = misc[BANK[kind, i]] if (kind, i) in BANK else None
                    if kind in PER:
                        wait(act, full[kind], PER[kind] * d + i + 1)
                    if kind == "zt":
                        wait(act, full["v"], 2 * d)
                        sc.activation(z_hi[:, i, :], bank[:], ACT.Copy).then_inc(zt_hi, 1)
                    elif kind == "qk":
                        wait(act, qk_w[i // 2], 64 * d)
                        sc.activation(qk_hi[:, i, :], bank[:], ACT.Identity,
                                      bias=W["b_col"][:, (i % 2) * 2 + i // 2:(i % 2) * 2 + i // 2 + 1]).then_inc(qkh, 1)
                    elif kind == "v":
                        wait(act, pv_done, 16 * d + (0 if i else -2))
                        sc.activation(v_aug[:, 2 * i:2 * i + 2, :, 0:HD],
                                      bank[:].rearrange("p (t h d) -> p t h d", t=2, h=NH), ACT.Copy).then_inc(free["v"], 1)
                    elif kind == "ctx":
                        n = 4 * d + i
                        wait(act, pv_done, 4 * (n + 1))
                        wait(act, full["cx"], n - 1)
                        sc.activation(ctx_t[:, i % 2, :], cacc[:], ACT.Copy).then_inc(ctx_evac, 1)
                    elif kind == "cn":
                        wait(act, full["out"], 2 * d)
                        sc.activation(c_hi[:, i, :], bank[:], ACT.Copy).then_inc(cnh, 1)
                    elif kind == "xt":
                        wait(act, full["lg"], d)
                        sc.activation(x_t[:, i, :], bank[:], ACT.Copy).then_inc(free["xt"], 1)
                    elif kind == "lg":
                        wait(act, lg_out, 16 * d)
                        sc.activation(lgt[:], bank[0:8, :], ACT.Copy).then_inc(free["lg"], 1)
                    elif kind == "z":
                        wait(act, y_done, 4 * (d + 1))
                        wait(act, rstd[1], 6 * (d + 1))
                        wait(act, full["zt"], 2 * d)
                        for t in range(4):
                            sc.activation(z[:, t, :], y[:, t, :], ACT.Copy, scale=r2[:, t:t + 1]).then_inc(z_done, 1)

                extras = {
                    0: [("v", 0, 0)], 1: [("ctx", 3, -1)], 2: [("v", 1, 0)], 3: [("zt", 0, 1)],
                    4: [("zt", 1, 1), ("cn", 0, -1)], 5: [("qk", 0, 1), ("cn", 1, -1), ("ctx", 0, 0)],
                    6: [("qk", 1, 1)], 7: [("qk", 2, 1), ("xt", 0, -2)], 8: [("qk", 3, 1), ("xt", 1, -2)],
                    9: [("ctx", 1, 0)], 11: [("lg", 0, -2)], 13: [("ctx", 2, 0)], 15: [("z", 0, 2)],
                }

                def body(b):
                    for s in range(16):
                        j = s % 4
                        for r in range(4):
                            if there(b, 0):
                                q = 16 * b + s
                                if r == 0:
                                    wait(act, pv_done, q - 1)
                                wait(act, st_full, 4 * q + r + 1)
                                sc.activation(probs[:, j % 2, r, :], stp[r % 2][:], ACT.Exp, scale=HD ** -0.5).then_inc(exp_done, 1)
                            if r == 0:
                                for kind, i, lag in extras.get(s, []):
                                    extra(b, kind, i, lag)
                iterations(act, body)

            @block.vector
            def _(dve):
                ve = nc.vector

                def stats(k, src, i):
                    for t in range(4):
                        ve.bn_stats(bst[k][:, t, :], src[:, t, :]).then_inc(bn[k], 1)
                    for t in range(4):
                        wait(dve, bn[k], 4 * i + t + 1)
                        carry(dve, dve_passed)
                        ve.bn_aggr(st[k][:, t, :], bst[k][:, t, :]).then_inc(agg[k], 1)

                def normal(k, dst, src, done):
                    for t in range(4):
                        ve.tensor_scalar(dst[:, t, :], src[:, t, :], st[k][:, t, 0:1], rs[k][:, t:t + 1],
                                         ALU.subtract, ALU.mult).then_inc(done, 1)

                def extra(b, kind, i, lag):
                    if not there(b, lag):
                        return
                    d = b + lag
                    bank = misc[BANK[kind, i]] if (kind, i) in BANK else None
                    n = 4 * d + i
                    if kind == "mt":
                        wait(dve, full["mt"], n + 1)
                        wait(dve, mt_w, 16 * (n - 1))
                        ve.tensor_scalar(mt[:, i % 2, 0, :], bank[0:16, 0:P], -1.0, None, ALU.mult).then_inc(mth, 1)
                        wait(dve, mth, n + 1)
                        ve.scalar_tensor_tensor(out=mt[:, i % 2, 1, :], in0=bank[0:16, 0:P], scalar=-1.0,
                                                in1=mt[:, i % 2, 0, :].bitcast(F32), op0=ALU.mult,
                                                op1=ALU.subtract).then_inc(free["mt"], 1)
                    elif kind == "cx":
                        wait(dve, full["cx"], n + 1)
                        wait(dve, full["cn"], 2 * d)
                        v = bank[:].rearrange("p (t h d) -> p t h d", t=4, h=HG)
                        ve.reciprocal(rsum[:].rearrange("p (t h) -> p t h", t=4), v[:, :, :, HD]).then_inc(recip, 1)
                        wait(dve, recip, n + 1)
                        ve.tensor_tensor(cn[:, :, i * 64:(i + 1) * 64].rearrange("p t (h d) -> p t h d", h=HG),
                                         v[:, :, :, 0:HD],
                                         rsum[:].rearrange("p (t h) -> p t h", t=4).unsqueeze(3).to_broadcast([P, 4, HG, HD]),
                                         ALU.mult).then_inc(free["cx"], 1)
                    elif kind == "zt":
                        wait(dve, zt_hi, 2 * d + i + 1)
                        ve.tensor_tensor(z_lo[:, i, :], bank[:], z_hi[:, i, :].bitcast(F32), ALU.subtract).then_inc(free["zt"], 1)
                    elif kind == "cn":
                        wait(dve, cnh, 2 * d + i + 1)
                        ve.tensor_tensor(c_lo[:, i, :], bank[:], c_hi[:, i, :].bitcast(F32), ALU.subtract).then_inc(free["cn"], 1)
                    elif kind == "qk":
                        wait(dve, qkh, n + 1)
                        col = (i % 2) * 2 + i // 2
                        ve.scalar_tensor_tensor(out=qk_lo[:, i, :], in0=bank[:], scalar=W["b_col"][:, col:col + 1],
                                                in1=qk_hi[:, i, :].bitcast(F32), op0=ALU.add,
                                                op1=ALU.subtract).then_inc(free["qk"], 1)
                    elif kind == "out":
                        wait(dve, full["out"], 2 * d + i + 1)
                        wait(dve, yp_done, d + 1)
                        wait(dve, x2_done, d)
                        ve.tensor_tensor(a[:, 2 * i:2 * i + 2, :], bank[:].rearrange("p (t h) -> p t h", t=2),
                                         yp[:, 2 * i:2 * i + 2, :], ALU.add).then_inc(free["out"], 1)
                    elif kind == "stats3":
                        wait(dve, free["out"], 2 * (d + 1))
                        stats(3, a, d)
                    elif kind == "lna":
                        wait(dve, rstd[3], 2 * (d + 1))
                        normal(3, a, a, lna_done)
                    elif kind == "stats4":
                        wait(dve, x2_done, d + 1)
                        stats(4, x2, d)
                    elif kind == "xn2":
                        wait(dve, rstd[4], 2 * (d + 1))
                        wait(dve, full["xt"], 2 * d)
                        wait(dve, xn2_out, 16 * d)
                        normal(4, xn2, x2, xn2_done)
                    elif kind == "stats1":
                        wait(dve, x_in, 16 * (d + 1))
                        wait(dve, rstd[1], 6 * d)
                        stats(1, xa, d)
                    elif kind == "y":
                        wait(dve, rstd[1], 6 * d + 2)
                        wait(dve, z_done, 4 * d)
                        wait(dve, y_out, 16 * d)
                        normal(1, y, xa, y_done)

                extras = {
                    0: [("xn2", 0, -2)], 1: [("mt", 1, 0)], 2: [("cx", 3, -1)], 3: [("zt", 0, 1)],
                    4: [("zt", 1, 1), ("cn", 0, -1)], 5: [("mt", 2, 0), ("qk", 0, 1), ("cn", 1, -1)],
                    6: [("qk", 1, 1), ("cx", 0, 0)], 7: [("qk", 2, 1)], 8: [("qk", 3, 1)],
                    9: [("mt", 3, 0), ("out", 0, -1)], 10: [("cx", 1, 0), ("out", 1, -1), ("stats3", 0, -1)],
                    11: [("stats1", 0, 2)], 12: [("lna", 0, -1)], 13: [("mt", 0, 1)],
                    14: [("cx", 2, 0), ("stats4", 0, -1)], 15: [("y", 0, 2)],
                }

                def body(b):
                    for s in range(16):
                        g, j = s // 4, s % 4
                        da, ga = b + (g >= 2), (g + 2) % 4
                        for r in range(4):
                            if there(b, int(g >= 2)):
                                if j == 0 and r == 0:
                                    wait(dve, full["mt"], 4 * da + ga - 1)
                                wait(dve, sm_full, 64 * da + 16 * ga + 4 * j + r + 1)
                                ve.reduce_max(mx[:, ga % 2, 4 * j + r:4 * j + r + 1], sm[r % 2][:], AX_X).then_inc(max_done[r % 2], 1)
                            if r == 1:
                                for kind, i, lag in extras.get(s, []):
                                    extra(b, kind, i, lag)
                iterations(dve, body)


def shared(nc, ctx):
    def sb(name, shape, dt=F32):
        return ctx.enter_context(nc.sbuf_tensor(name, shape, dt))
    return {
        "wq_hi": sb("wq_hi", [P, 2, 768], F32R), "wq_lo": sb("wq_lo", [P, 2, 768], F32R),
        "wo_hi": sb("wo_hi", [P, 2, 256], F32R), "wo_lo": sb("wo_lo", [P, 2, 256], F32R),
        "b_col": sb("b_col", [P, 6]), "bo": sb("bo", [P, 256]), 
        "v_aug": sb("v_aug", [P, 4, NH, VW]),
        "q_st": sb("q_st", [KM, G, HG, 512], F32R), "k_st": sb("k_st", [KM, G, HG, 512], F32R),
    }


E = 8
F = 512
KE = 2
WD = mybir.dt.bfloat16
U = 8


def tiles_of(T):
    n = KE * T // P + E - 1
    return -(-n // U) * U


def region(T):
    return -(-(T // P + E) // 16) * 16 * P


def route(nc, R, lg_d, table_d, T, w_loader, cleared):
    NT = T // P
    RT = region(T)
    with ExitStack() as ctx:
        def sb(name, shape, dt=F32):
            return ctx.enter_context(nc.sbuf_tensor("r_" + name, shape, dt))

        def sem(name):
            return ctx.enter_context(nc.semaphore("r_" + name))

        lgs = sb("lgs", [E, T])
        logits = sb("logits", [P, NT, E])
        col = {k: sb(k, [P, NT]) for k in ("m", "s", "p0", "p1", "ed", "w0", "w1")}
        work = sb("work", [P, NT, E])
        prob = sb("prob", [P, NT, E])
        hot = [sb(f"hot{k}", [P, NT, E]) for k in range(KE)]
        both = sb("both", [P, NT, E])
        scan = [sb(f"scan{k}", [P, NT, E]) for k in range(2)]
        total = sb("total", [P, NT, E])
        slot = sb("slot", [P, NT, KE])
        slot_i = sb("slot_i", [P, NT, KE], I32)
        pay = sb("pay", [P, NT, KE, 2], I32)
        before = sb("before", [P, P])
        ones = sb("ones", [P, P])
        iota_i = sb("iota_i", [P, E + E + tiles_of(T)], I32)
        iota = sb("iota", [P, E + E + tiles_of(T)])
        cnt_i = sb("cnt_i", [P, E], I32)
        ntile = sb("ntile", [P, E])
        tb = sb("tb", [P, E])
        jump = sb("jump", [P, E])
        e_f, off_f, tmp_f = (sb(n, [P, tiles_of(T)]) for n in ("e_f", "off_f", "tmp_f"))
        bank = [ctx.enter_context(nc.psum_tensor(f"r_bank{i}", [P, 512], F32)) for i in range(3)]

        lg_in, const, turned = sem("lg_in"), sem("const"), sem("turned")
        step = sem("step")
        exp_in, exp_out = sem("exp_in"), sem("exp_out")
        hot_ready, counted = sem("hot_ready"), sem("counted")
        slots_ready, scattered = sem("slots_ready"), sem("scattered")
        w_in, w_hi, w_lo = sem("w_in"), sem("w_hi"), sem("w_lo")

        w_src, raw = w_loader
        parts = [(e, k) for e in range(E) for k in range(3)]

        with nc.Block() as block:
            @block.sync
            def _(sp):
                sp.dma_start(lgs[:], lg_d).then_inc(lg_in, 16)
                for n, (e, k) in enumerate(parts):
                    if n >= 3:
                        sp.wait_ge(w_lo, n - 2)
                    if n:
                        sp.wait_ge(w_in, 16 * n)
                    sp.dma_start(raw[:, n % 3, :].rearrange("p (c f) -> p c f", c=2 if k < 2 else 4), w_src[k][e]).then_inc(w_in, 16)

            @block.gpsimd
            def _(pool):
                nc.gpsimd.memset(before[:], 1.0).then_inc(const, 1)
                pool.wait_ge(const, 1)
                nc.gpsimd.affine_select(out=before[:], in_=before[:], compare_op=ALU.is_gt, fill=0.0,
                                        base=0, pattern=[[1, P]], channel_multiplier=-1).then_inc(const, 1)
                pool.wait_ge(const, 2)
                nc.gpsimd.memset(ones[:], 1.0).then_inc(const, 1)
                pool.wait_ge(const, 3)
                nc.gpsimd.iota(iota_i[:, 0:E], pattern=[[-1, E]], base=E, channel_multiplier=0).then_inc(const, 1)
                pool.wait_ge(const, 4)
                nc.gpsimd.iota(iota_i[:, E:2 * E], pattern=[[RT, E]], base=0, channel_multiplier=0).then_inc(const, 1)
                pool.wait_ge(const, 5)
                nc.gpsimd.iota(iota_i[:, 2 * E:], pattern=[[1, tiles_of(T)]], base=0, channel_multiplier=0).then_inc(const, 1)
                pool.wait_ge(const, 6)
                for k in range(KE):
                    nc.gpsimd.iota(pay[:, :, k, 0], pattern=[[P, NT]], base=0, channel_multiplier=1).then_inc(const, 1)
                    pool.wait_ge(const, 7 + k)
                pool.wait_ge(slots_ready, 1)
                pool.wait_ge(cleared[0], cleared[1])
                for t in range(NT):
                    for k in range(KE):
                        pool.indirect_dma_start(table_d, bass.IndirectOffsetOnAxis(ap=slot_i[:, t, k:k + 1], axis=0),
                                                pay[:, t, k, :], None).then_inc(scattered, 16)
                pool.wait_ge(scattered, 16 * NT * KE)

            @block.tensor
            def _(pe):
                pe.wait_ge(lg_in, 16)
                for t in range(NT):
                    last = nc.tensor.transpose(bank[0][:, t * E:(t + 1) * E], lgs[:, t * P:(t + 1) * P], R["ident"][0:E, 0:E])
                last.then_inc(turned, 1)
                pe.wait_ge(hot_ready, 1)
                pe.wait_ge(const, 3)
                n = NT * E
                nc.tensor.matmul(bank[1][:, 0:n], before[:], both[:].rearrange("p t e -> p (t e)"), start=True, stop=True)
                nc.tensor.matmul(bank[2][:, 0:n], ones[:], both[:].rearrange("p t e -> p (t e)"), start=True, stop=True).then_inc(counted, 1)

            @block.scalar
            def _(act):
                def split_hi(n):
                    e, k = parts[n]
                    act.wait_ge(w_in, 16 * (n + 1))
                    nc.scalar.activation(R["hi"][:, e, k, :], raw[:, n % 3, :], ACT.Copy).then_inc(w_hi, 1)
                act.wait_ge(exp_in, 1)
                nc.scalar.activation(prob[:], work[:], ACT.Exp).then_inc(exp_out, 1)
                for n in range(4):
                    split_hi(n)
                act.wait_ge(exp_in, 2)
                nc.scalar.activation(col["ed"][:], col["s"][:], ACT.Exp).then_inc(exp_out, 1)
                for n in range(4, len(parts)):
                    split_hi(n)

            @block.vector
            def _(dve):
                ve = nc.vector
                done = [0]

                def chain(ins):
                    done[0] += 1
                    ins.then_inc(step, 1)
                    dve.wait_ge(step, done[0])

                def wide(v):
                    return v.unsqueeze(2).to_broadcast([P, NT, E])

                def over(v):
                    return v.unsqueeze(1).to_broadcast([P, NT, E])

                def split_lo(n):
                    e, k = parts[n]
                    dve.wait_ge(w_hi, n + 1)
                    ve.tensor_tensor(R["lo"][:, e, k, :], raw[:, n % 3, :], R["hi"][:, e, k, :], ALU.subtract).then_inc(w_lo, 1)

                dve.wait_ge(const, 8)
                chain(ve.tensor_copy(iota[:], iota_i[:]))
                dve.wait_ge(turned, 1)
                chain(ve.tensor_copy(logits[:].rearrange("p t e -> p (t e)"), bank[0][:, 0:NT * E]))
                chain(ve.reduce_max(col["m"][:], logits[:], AX_X))
                ve.tensor_tensor(work[:], logits[:], wide(col["m"][:]), ALU.subtract).then_inc(exp_in, 1)
                dve.wait_ge(exp_out, 1)
                chain(ve.reduce_sum(col["s"][:], prob[:], AX_X))
                chain(ve.reciprocal(col["m"][:], col["s"][:]))
                chain(ve.tensor_tensor(prob[:], prob[:], wide(col["m"][:]), ALU.mult))
                for k in range(KE):
                    chain(ve.reduce_max(col[f"p{k}"][:], prob[:], AX_X))
                    chain(ve.tensor_tensor(work[:], prob[:], wide(col[f"p{k}"][:]), ALU.is_equal))
                    chain(ve.tensor_tensor(work[:], work[:], over(iota[:, 0:E]), ALU.mult))
                    chain(ve.reduce_max(col["m"][:], work[:], AX_X))
                    chain(ve.tensor_tensor(hot[k][:], work[:], wide(col["m"][:]), ALU.is_equal))
                    if k == 0:
                        chain(ve.scalar_tensor_tensor(out=prob[:], in0=hot[0][:], scalar=-2.0, in1=prob[:], op0=ALU.mult, op1=ALU.add))
                ve.tensor_tensor(both[:], hot[0][:], hot[1][:], ALU.add).then_inc(hot_ready, 1)
                ve.tensor_tensor(col["s"][:], col["p1"][:], col["p0"][:], ALU.subtract).then_inc(exp_in, 1)
                for n in range(4):
                    split_lo(n)
                dve.wait_ge(exp_out, 2)
                chain(ve.tensor_scalar(col["m"][:], col["ed"][:], 1.0, None, ALU.add))
                chain(ve.reciprocal(col["w0"][:], col["m"][:]))
                chain(ve.tensor_tensor(col["w1"][:], col["ed"][:], col["w0"][:], ALU.mult))
                for k in range(KE):
                    chain(ve.tensor_copy(pay[:, :, k, 1].bitcast(F32), col[f"w{k}"][:]))
                dve.wait_ge(counted, 1)
                chain(ve.tensor_copy(total[:].rearrange("p t e -> p (t e)"), bank[2][:, 0:NT * E]))
                src = total
                shift, n = 1, 0
                while shift < NT:
                    dst = scan[n % 2]
                    chain(ve.tensor_copy(dst[:, 0:shift, :], src[:, 0:shift, :]))
                    chain(ve.tensor_tensor(dst[:, shift:, :], src[:, shift:, :], src[:, 0:NT - shift, :], ALU.add))
                    src, shift, n = dst, shift * 2, n + 1
                count = src[:, NT - 1, :]
                chain(ve.tensor_tensor(total[:], src[:], total[:], ALU.subtract))
                chain(ve.tensor_tensor(total[:], bank[1][:, 0:NT * E].rearrange("p (t e) -> p t e", e=E), total[:], ALU.add))
                chain(ve.tensor_tensor(total[:], total[:], over(iota[:, E:2 * E]), ALU.add))
                for k in range(KE):
                    chain(ve.tensor_tensor(work[:], total[:], hot[k][:], ALU.mult))
                    chain(ve.reduce_sum(slot[:, :, k], work[:], AX_X))
                ve.tensor_copy(slot_i[:], slot[:]).then_inc(slots_ready, 1)
                chain(ve.tensor_scalar(ntile[:], count, float(P - 1), None, ALU.add))
                chain(ve.tensor_copy(cnt_i[:], ntile[:]))
                chain(ve.tensor_scalar(cnt_i[:], cnt_i[:], 7, None, ALU.arith_shift_right))
                chain(ve.tensor_copy(ntile[:], cnt_i[:]))
                chain(ve.memset(tb[:, 0:1], 0.0))
                for e in range(1, E):
                    chain(ve.tensor_tensor(tb[:, e:e + 1], tb[:, e - 1:e], ntile[:, e - 1:e], ALU.add))
                chain(ve.tensor_scalar(jump[:], ntile[:], float(-P), float(RT), ALU.mult, ALU.add))
                chain(ve.memset(e_f[:], 0.0))
                it = iota[:, 2 * E:]
                chain(ve.tensor_scalar(off_f[:], it, float(P), None, ALU.mult))
                for e in range(1, E):
                    chain(ve.scalar_tensor_tensor(out=e_f[:], in0=it, scalar=tb[:, e:e + 1], in1=e_f[:], op0=ALU.is_ge, op1=ALU.add))
                    chain(ve.tensor_scalar(tmp_f[:], it, tb[:, e:e + 1], jump[:, e - 1:e], ALU.is_ge, ALU.mult))
                    chain(ve.tensor_tensor(off_f[:], off_f[:], tmp_f[:], ALU.add))
                chain(ve.tensor_copy(R["tile_e"][:], e_f[:]))
                chain(ve.tensor_copy(R["tile_off"][:], off_f[:]))
                for n in range(4, len(parts)):
                    split_lo(n)
                dve.wait_ge(w_lo, len(parts))


def experts(nc, R, table_d, xn2_d, acc_d, T):
    NTL = tiles_of(T)
    RT = region(T)
    with ExitStack() as ctx:
        def sb(name, shape, dt=F32):
            return ctx.enter_context(nc.sbuf_tensor("e_" + name, shape, dt))

        def sem(name):
            return ctx.enter_context(nc.semaphore("e_" + name))

        pair = sb("pair", [P, U, 2], I32)
        xg = sb("xg", [P, 4, 256])
        x_hi, x_lo = sb("x_hi", [P, 2, 256], WD), sb("x_lo", [P, 2, 256], WD)
        sg = sb("sg", [P, 2, F])
        h = sb("h", [P, 2, F])
        h_hi, h_lo = sb("h_hi", [P, 2, F], WD), sb("h_lo", [P, 2, F], WD)
        yw = sb("yw", [P, 2, 256])
        ps_x = ctx.enter_context(nc.psum_tensor("ps_x", [P, 512], F32))
        ps_g = [ctx.enter_context(nc.psum_tensor(f"ps_g{i}", [P, 512], F32)) for i in range(2)]
        ps_u = [ctx.enter_context(nc.psum_tensor(f"ps_u{i}", [P, 512], F32)) for i in range(2)]
        ps_h = ctx.enter_context(nc.psum_tensor("ps_h", [P, 512], F32))
        ps_y = [ctx.enter_context(nc.psum_tensor(f"ps_y{i}", [P, 512], F32)) for i in range(2)]

        pair_in = [sem(f"pair_in{k}") for k in range(U)]
        x_in, added = [sem(f"x_in{k}") for k in range(4)], sem("added")
        xt_full, xh, xt_free = sem("xt_full"), sem("xh"), sem("xt_free")
        g_full, u_full, sg_done, h_done = sem("g_full"), sem("u_full"), sem("sg_done"), sem("h_done")
        passed = sem("passed")
        ht_full, hh, ht_free = sem("ht_full"), sem("hh"), sem("ht_free")
        y_full, yw_done = sem("y_full"), sem("yw_done")

        def wait(eng, s, value):
            if not (isinstance(value, int) and value <= 0):
                eng.wait_ge(s, value)

        def steps(eng, body):
            for k in range(U):
                body(k, k)
            with eng.Fori(1, NTL // U - 1) as o:
                for k in range(U):
                    body(o * U + k, k)
            for k in range(U):
                body(NTL - U + k, k)

        def no(i, past):
            return isinstance(i, int) and not 0 <= past < NTL

        with nc.Block() as block:
            @block.sync
            def _(sp):
                def body(i, k):
                    off = sp.value_load(R["tile_off"][0:1, bass.ds(i, 1)], min_val=0, max_val=E * RT - P)
                    wait(sp, added, 16 * (i - U + 1))
                    sp.dma_start(pair[:, k, :], table_d[bass.ds(off, P), :]).then_inc(pair_in[k], 16)
                steps(sp, body)

            @block.gpsimd
            def _(pool):
                def gather(i, k, o):
                    pool.wait_ge(pair_in[k], 16 * (o + 1))
                    wait(pool, xt_full, i - 3)
                    carry(pool, passed)
                    pool.indirect_dma_start(xg[:, k % 4, :], None, xn2_d,
                                            bass.IndirectOffsetOnAxis(ap=pair[:, k, 0:1], axis=0)).then_inc(x_in[k % 4], 16)

                def body(o):
                    i = o * U
                    for k in range(U):
                        if not no(i, i + k + 3 if isinstance(i, int) else 0):
                            gather(i + k + 3, (k + 3) % U, o + (k + 3) // U)
                        pool.wait_ge(yw_done, i + k + 1)
                        wait(pool, added, 16 * (i + k))
                        carry(pool, passed)
                        pool.indirect_dma_start(acc_d, bass.IndirectOffsetOnAxis(ap=pair[:, k, 0:1], axis=0), yw[:, k % 2, :], None,
                                                compute_op=ALU.add).then_inc(added, 16)
                for k in range(3):
                    gather(k, k, 0)
                body(0)
                with pool.Fori(1, NTL // U - 1) as o:
                    body(o)
                body(NTL // U - 1)
                pool.wait_ge(added, 16 * NTL)

            @block.tensor
            def _(pe):
                te = nc.tensor

                def x_turn(i, k, o):
                    pe.wait_ge(x_in[k % 4], 16 * (2 * o + k // 4 + 1))
                    wait(pe, xt_free, i)
                    for c in range(2):
                        last = te.transpose(ps_x[:, c * P:(c + 1) * P], xg[:, k % 4, c * P:(c + 1) * P], R["ident"][:])
                    last.then_inc(xt_full, 1)

                def weight(part, e, which, cols):
                    return R[part][:, bass.ds(e, 1), which, cols].rearrange("p a f -> p (a f)")

                def up(i, k):
                    e = pe.value_load(R["tile_e"][0:1, bass.ds(i, 1)], min_val=0, max_val=E - 1)
                    pe.wait_ge(xt_free, i + 1)
                    for which, (ps, full, used) in enumerate(((ps_g, g_full, sg_done), (ps_u, u_full, h_done))):
                        wait(pe, used, i - 1)
                        out = ps[k % 2][:]
                        for c in range(2):
                            xh_, xl_ = x_hi[:, k % 2, c * P:(c + 1) * P], x_lo[:, k % 2, c * P:(c + 1) * P]
                            cols = slice(c * F, (c + 1) * F)
                            te.matmul(out, xh_, weight("hi", e, which, cols), start=(c == 0), stop=False)
                            te.matmul(out, xh_, weight("lo", e, which, cols), start=False, stop=False)
                            last = te.matmul(out, xl_, weight("hi", e, which, cols), start=False, stop=(c == 1))
                        last.then_inc(full, 1)

                def h_turn(i, k):
                    pe.wait_ge(h_done, i + 1)
                    wait(pe, ht_free, i)
                    for c in range(4):
                        last = te.transpose(ps_h[:, c * P:(c + 1) * P], h[:, k % 2, c * P:(c + 1) * P], R["ident"][:])
                    last.then_inc(ht_full, 1)

                def down(i, k):
                    e = pe.value_load(R["tile_e"][0:1, bass.ds(i, 1)], min_val=0, max_val=E - 1)
                    pe.wait_ge(ht_free, i + 1)
                    wait(pe, yw_done, i - 1)
                    out = ps_y[k % 2][:, 0:256]
                    for c in range(4):
                        hh_, hl_ = h_hi[:, k % 2, c * P:(c + 1) * P], h_lo[:, k % 2, c * P:(c + 1) * P]
                        cols = slice(c * 256, (c + 1) * 256)
                        te.matmul(out, hh_, weight("hi", e, 2, cols), start=(c == 0), stop=False)
                        te.matmul(out, hh_, weight("lo", e, 2, cols), start=False, stop=False)
                        last = te.matmul(out, hl_, weight("hi", e, 2, cols), start=False, stop=(c == 3))
                    last.then_inc(y_full, 1)

                def body(o):
                    i = o * U
                    for k in range(U):
                        if not no(i, i + k + 1 if isinstance(i, int) else 0):
                            x_turn(i + k + 1, (k + 1) % U, o + (k + 1) // U)
                        up(i + k, k)
                        if not no(i, i + k - 1 if isinstance(i, int) else 0):
                            down(i + k - 1, (k - 1) % U)
                        h_turn(i + k, k)
                x_turn(0, 0, 0)
                body(0)
                with pe.Fori(1, NTL // U - 1) as o:
                    body(o)
                body(NTL // U - 1)
                down(NTL - 1, U - 1)

            @block.scalar
            def _(act):
                sc = nc.scalar

                def x_high(i, k):
                    act.wait_ge(xt_full, i + 1)
                    wait(act, u_full, i - 1)
                    sc.activation(x_hi[:, k % 2, :], ps_x[:, 0:256], ACT.Copy).then_inc(xh, 1)

                def scaled(i, k):
                    act.wait_ge(y_full, i + 1)
                    wait(act, added, 16 * (i - 1))
                    sc.activation(yw[:, k % 2, :], ps_y[k % 2][:, 0:256], ACT.Copy,
                                  scale=pair[:, k, 1:2].bitcast(F32)).then_inc(yw_done, 1)

                def body(i, k):
                    if not no(i, i + 1 if isinstance(i, int) else 0):
                        x_high(i + 1, (k + 1) % U)
                    act.wait_ge(g_full, i + 1)
                    wait(act, h_done, i - 1)
                    sc.activation(sg[:, k % 2, :], ps_g[k % 2][:], ACT.Silu).then_inc(sg_done, 1)
                    if not no(i, i - 1 if isinstance(i, int) else 0):
                        scaled(i - 1, (k - 1) % U)
                    act.wait_ge(ht_full, i + 1)
                    wait(act, y_full, i - 1)
                    sc.activation(h_hi[:, k % 2, :], ps_h[:], ACT.Copy).then_inc(hh, 1)
                x_high(0, 0)
                steps(act, body)
                scaled(NTL - 1, U - 1)

            @block.vector
            def _(dve):
                ve = nc.vector

                def x_low(i, k):
                    dve.wait_ge(xh, i + 1)
                    ve.tensor_tensor(x_lo[:, k % 2, :], ps_x[:, 0:256], x_hi[:, k % 2, :], ALU.subtract).then_inc(xt_free, 1)

                def body(i, k):
                    if not no(i, i + 1 if isinstance(i, int) else 0):
                        x_low(i + 1, (k + 1) % U)
                    dve.wait_ge(u_full, i + 1)
                    dve.wait_ge(sg_done, i + 1)
                    wait(dve, ht_full, i - 1)
                    ve.tensor_tensor(h[:, k % 2, :], ps_u[k % 2][:], sg[:, k % 2, :], ALU.mult).then_inc(h_done, 1)
                    dve.wait_ge(hh, i + 1)
                    ve.tensor_tensor(h_lo[:, k % 2, :], ps_h[:], h_hi[:, k % 2, :], ALU.subtract).then_inc(ht_free, 1)
                x_low(0, 0)
                steps(dve, body)


def finish(nc, R, acc_d, x2_d, out, T):
    N, D = T // 512, 3
    with ExitStack() as ctx:
        def sb(name, shape, dt=F32):
            return ctx.enter_context(nc.sbuf_tensor("f_" + name, shape, dt))

        def sem(name):
            return ctx.enter_context(nc.semaphore("f_" + name))

        acc, xs = sb("acc", [P, D, 4, 256]), sb("xs", [P, D, 4, 256])
        raw, st, rs = sb("raw", [P, 2, 4, 6]), sb("st", [P, 2, 4, 2]), sb("rs", [P, 2, 4])
        acc_in, xs_in = [sem(f"acc_in{k}") for k in range(D)], [sem(f"xs_in{k}") for k in range(D)]
        out_done = [sem(f"out_done{k}") for k in range(D)]
        bn, agg, rstd, normed, summed = sem("bn"), sem("agg"), sem("rstd"), sem("normed"), sem("summed")

        def rows(dram, i):
            return dram[i * 512:(i + 1) * 512, :].rearrange("(t p) h -> p t h", p=P)

        with nc.Block() as block:
            @block.sync
            def _(sp):
                for i in range(N):
                    if i >= D:
                        sp.wait_ge(out_done[i % D], 16 * (i // D))
                    sp.dma_start(acc[:, i % D], rows(acc_d, i)).then_inc(acc_in[i % D], 16)
                    sp.dma_start(xs[:, i % D], rows(x2_d, i)).then_inc(xs_in[i % D], 16)

            @block.gpsimd
            def _(pool):
                for i in range(N):
                    pool.wait_ge(agg, 4 * (i + 1))
                    nc.gpsimd.tensor_scalar(rs[:, i % 2, :], st[:, i % 2, :, 1], EPS, None, ALU.add).then_inc(rstd, 1)
                    pool.wait_ge(rstd, 2 * i + 1)
                    nc.gpsimd.tensor_tensor(rs[:, i % 2, :], rs[:, i % 2, :], R["neg_half"][:], ALU.pow).then_inc(rstd, 1)

            @block.vector
            def _(dve):
                def normal(i):
                    dve.wait_ge(rstd, 2 * (i + 1))
                    for t in range(4):
                        nc.vector.tensor_scalar(acc[:, i % D, t, :], acc[:, i % D, t, :], st[:, i % 2, t, 0:1],
                                                rs[:, i % 2, t:t + 1], ALU.subtract, ALU.mult).then_inc(normed, 1)
                    dve.wait_ge(xs_in[i % D], 16 * (i // D + 1))
                    dve.wait_ge(normed, 4 * (i + 1))
                    nc.vector.tensor_tensor(acc[:, i % D], acc[:, i % D], xs[:, i % D], ALU.add).then_inc(summed, 1)

                for i in range(N):
                    dve.wait_ge(acc_in[i % D], 16 * (i // D + 1))
                    for t in range(4):
                        nc.vector.bn_stats(raw[:, i % 2, t, :], acc[:, i % D, t, :]).then_inc(bn, 1)
                    for t in range(4):
                        dve.wait_ge(bn, 4 * i + t + 1)
                        nc.vector.bn_aggr(st[:, i % 2, t, :], raw[:, i % 2, t, :]).then_inc(agg, 1)
                    if i >= 1:
                        normal(i - 1)
                normal(N - 1)

            @block.scalar
            def _(act):
                for i in range(N):
                    act.wait_ge(summed, i + 1)
                    act.dma_start(rows(out, i), acc[:, i % D]).then_inc(out_done[i % D], 16)
                for k in range(D):
                    act.wait_ge(out_done[k], 16 * len(range(k, N, D)))


def build(nc, x, gamma, beta, w_qkv, b_qkv, w_out, b_out, router, w_gate, w_up, w_down, out):
    B, S, H = x.shape
    T = B * S
    RT = region(T)

    def dram(name, shape, dt=F32):
        return nc.dram_tensor(name, shape, dt).ap()

    y_d, x2_d = dram("y_d", [T, H]), dram("x2_d", [T, H])
    xn2_d, acc_d = dram("xn2_d", [T + P, H]), dram("acc_d", [T + P, H])
    lg_d = dram("lg_d", [E, T])
    qk_d, mt_d = dram("qk_d", [4, H, S]), dram("mt_d", [2, HG * S])
    table_d = dram("table_d", [E * RT, 2], I32)

    with ExitStack() as outer:
        def sb(name, shape, dt=F32):
            return outer.enter_context(nc.sbuf_tensor(name, shape, dt))
        ident, neg_half = sb("ident", [P, P]), sb("neg_half", [P, 4])
        cleared = outer.enter_context(nc.semaphore("cleared"))
        with ExitStack() as ctx:
            W = shared(nc, ctx)
            W["ident"], W["neg_half"] = ident, neg_half
            prepare_weights(nc, W, w_qkv, b_qkv, w_out, b_out, gamma, beta, acc_d, xn2_d, table_d, cleared)
            attention(nc, W, x, y_d, x2_d, xn2_d, lg_d, qk_d, mt_d, router)
        with ExitStack() as ctx:
            def sc(name, shape, dt=F32):
                return ctx.enter_context(nc.sbuf_tensor(name, shape, dt))
            R = {"ident": ident, "neg_half": neg_half,
                 "hi": sc("we_hi", [P, E, 3, 1024], WD), "lo": sc("we_lo", [P, E, 3, 1024], WD),
                 "tile_e": sc("tile_e", [P, tiles_of(T)], I32), "tile_off": sc("tile_off", [P, tiles_of(T)], I32)}
            with ExitStack() as inner:
                raw = inner.enter_context(nc.sbuf_tensor("we_raw", [P, 3, 1024], F32))
                src = [[w[e].rearrange("(c p) f -> p c f", p=P) for e in range(E)] for w in (w_gate, w_up, w_down)]
                route(nc, R, lg_d, table_d, T, (src, raw), (cleared, clears(T) * 16))
            experts(nc, R, table_d, xn2_d, acc_d, T)
            finish(nc, R, acc_d, x2_d, out, T)


_INS = ["hidden_states", "ln_gamma", "ln_beta", "W_qkv", "b_qkv", "W_out", "b_out"]
_NAMES = ["L0_attn_" + n for n in _INS] + ["L0_ffn_router_kernel_DE", "L0_ffn_kernel_gating_EDF",
                                          "L0_ffn_kernel_up_EDF", "L0_ffn_kernel_down_EFD"]


def kernel(**inputs):
    import numpy as _np
    import concourse.bacc as _bacc
    from concourse import mybir as _mybir
    from concourse.bass_utils import run_bass_kernel_spmd as _run

    nc = _bacc.Bacc("TRN2", target_bir_lowering=False, num_devices=1)
    arrays, args = {}, []
    for name in _NAMES:
        a = _np.ascontiguousarray(inputs[name])
        arrays[f"in_{name}"] = a
        args.append(nc.dram_tensor(f"in_{name}", a.shape, _mybir.dt.from_np(a.dtype), kind="ExternalInput").ap())
    x = args[0]
    out = nc.dram_tensor("out", [x.shape[0] * x.shape[1], x.shape[2]], _mybir.dt.float32, kind="ExternalOutput").ap()
    x, gamma, beta, w_qkv, b_qkv, w_out, b_out, router, w_gate, w_up, w_down = args
    build(nc, x, gamma, beta, w_qkv, b_qkv, w_out, b_out, router, w_gate, w_up, w_down, out)
    r = _run(nc, [arrays], core_ids=[0])
    return r.results[0]["out"].reshape(inputs[_NAMES[0]].shape)
```

```python
from contextlib import ExitStack

import concourse.bass as bass
from concourse import mybir

F32 = mybir.dt.float32
F32R = mybir.dt.float32r
F16 = mybir.dt.float16
I32 = mybir.dt.int32
ALU = mybir.AluOpType
ACT = mybir.ActivationFunctionType
AX_X = mybir.AxisListType.X

P = 128
NH = 16
HD = 16
EPS = 1e-5
G = 4
HG = NH // G
VW = 32
KR = 96
KM = KR + 2


def split3(pe, out, stat_hi, stat_lo, mov_hi, mov_lo):
    n = len(stat_hi)
    for c in range(n):
        pe.matmul(out, stat_hi[c], mov_hi[c], start=(c == 0), stop=False)
        pe.matmul(out, stat_hi[c], mov_lo[c], start=False, stop=False)
        last = pe.matmul(out, stat_lo[c], mov_hi[c], start=False, stop=(c == n - 1))
    return last


def carry(eng, passed):
    eng.sem_inc(passed, 1)


def clears(T):
    return 1 + -(-(E * region(T) // P) // (5 * P))


def prepare_weights(nc, W, w_qkv, b_qkv, w_out, b_out, gamma, beta, xn2_d, table_d, cleared):
    with ExitStack() as ctx:
        def sb(name, shape, dt=F32):
            return ctx.enter_context(nc.sbuf_tensor(name, shape, dt))

        def sem(name):
            return ctx.enter_context(nc.semaphore(name))

        wq_in = sb("wq_in", [P, 6, 256])
        wo_in = sb("wo_in", [P, 2, 256])
        wo_t = sb("wo_t", [P, 2, 256])
        beta_rows = sb("beta_rows", [P, 256])
        bo_rows = sb("bo_rows", [P, 256])
        gamma_col = sb("gamma_col", [P, 2])
        bq_col = sb("bq_col", [P, 6])
        wbeta = sb("wbeta", [P, 6, 256])
        wb_col = sb("wb_col", [P, 6])
        bv_wide = sb("bv_wide", [P, 2, P])
        bank = [ctx.enter_context(nc.psum_tensor(f"prep_bank{i}", [P, 512], F32)) for i in range(2)]
        loaded = sem("w_loaded")
        ident0 = sem("w_ident0")
        ident_ready = sem("w_ident_ready")
        turned = sem("w_turned")
        hi_done = sem("w_hi_done")
        raw_done = sem("w_raw_done")
        lo_done = sem("w_lo_done")
        bias_step = sem("w_bias_step")
        bo_ready = sem("w_bo_ready")
        bo_done = sem("w_bo_done")
        ones_done = sem("w_ones_done")

        T = xn2_d.shape[0] - P
        rows = table_d.shape[0] // P
        zeros = sb("zeros", [P, 512], F16)
        filler = sb("filler", [P, 5, P, 4], I32)
        dest_base, dest_first = sb("dest_base", [P, 1], I32), sb("dest_first", [P, 1])
        zeros_ready, filler_step = sem("w_zeros"), sem("w_filler")
        jobs = [("q", o, c) for c in range(2) for o in range(6)] + [("o", o, c) for c in range(2) for o in range(2)]
        with nc.Block() as block:
            @block.sync
            def _(sp):
                with nc.allow_non_contiguous_dma(reason="bias and gamma columns, once"):
                    sp.dma_start(wq_in[:], w_qkv.rearrange("(t p) h -> p t h", p=P)).then_inc(loaded, 16)
                    sp.dma_start(wo_in[:], w_out.rearrange("(t p) h -> p t h", p=P)).then_inc(loaded, 16)
                    sp.dma_start(beta_rows[:], beta.unsqueeze(0).to_broadcast([P, 256])).then_inc(loaded, 16)
                    sp.dma_start(bo_rows[:], b_out.unsqueeze(0).to_broadcast([P, 256])).then_inc(loaded, 16)
                    sp.dma_start(gamma_col[:], gamma.rearrange("(c p) -> p c", p=P)).then_inc(loaded, 16)
                    sp.dma_start(bq_col[:], b_qkv.rearrange("(c p) -> p c", p=P)).then_inc(loaded, 16)

                sp.wait_ge(zeros_ready, 1)
                sp.dma_start(xn2_d[T:, :], zeros[:]).then_inc(cleared, 16)
                table = table_d.rearrange("(p r) c -> p (r c)", p=P)
                sp.wait_ge(filler_step, 13)
                for n in range(0, rows, 5 * P):
                    m = min(5 * P, rows - n)
                    sp.dma_start(table[:, 4 * n:4 * (n + m)], filler[:].rearrange("p a q c -> p (a q c)")[:, 0:4 * m]).then_inc(cleared, 16)
                sp.wait_ge(cleared, 16 * clears(T))

            @block.gpsimd
            def _(pool):
                nc.gpsimd.memset(filler[:], 0).then_inc(filler_step, 1)
                pool.wait_ge(filler_step, 1)
                for n in range(5):
                    nc.gpsimd.iota(filler[:, n, :, 0], pattern=[[1, P]], base=T, channel_multiplier=0).then_inc(filler_step, 1)
                    pool.wait_ge(filler_step, n + 2)
                nc.gpsimd.iota(filler[:, :, :, 2], pattern=[[P, 5], [1, P]], base=0, channel_multiplier=rows).then_inc(filler_step, 1)
                pool.wait_ge(filler_step, 7)
                nc.gpsimd.iota(dest_base[:], pattern=[[0, 1]], base=0, channel_multiplier=1).then_inc(filler_step, 1)
                pool.wait_ge(filler_step, 8)
                nc.gpsimd.memset(W["ident"][:], 0.0).then_inc(ident0, 1)
                pool.wait_ge(ident0, 1)
                nc.gpsimd.affine_select(out=W["ident"][:], in_=W["ident"][:], compare_op=ALU.not_equal, fill=1.0,
                                        base=0, pattern=[[-1, P]], channel_multiplier=1).then_inc(ident_ready, 1)
                nc.gpsimd.memset(W["v_aug"][:], 0.0).then_inc(ones_done, 1)
                nc.gpsimd.memset(W["q_st"][:].bitcast(F32), 0.0).then_inc(ones_done, 1)
                nc.gpsimd.memset(W["k_st"][:].bitcast(F32), 0.0).then_inc(ones_done, 1)
                nc.gpsimd.memset(W["neg_half"][:], -0.5).then_inc(ones_done, 1)
                pool.wait_ge(ones_done, 4)
                nc.gpsimd.memset(W["v_aug"][:, :, :, HD:HD + 1], 1.0).then_inc(ones_done, 1)
                pool.wait_ge(ones_done, 5)
                nc.gpsimd.memset(W["k_st"][KR:KM].bitcast(F32), 1.0).then_inc(ones_done, 1)
                pool.wait_ge(ones_done, 6)

            @block.tensor
            def _(pe):
                pe.wait_ge(loaded, 96)
                pe.wait_ge(ident_ready, 1)
                for n, (kind, o, c) in enumerate(jobs):
                    if n >= 2:
                        pe.wait_ge(lo_done, n - 1)
                    src = wq_in if kind == "q" else wo_in
                    nc.tensor.transpose(bank[n % 2][:, 0:P], src[:, o, c * P:(c + 1) * P], W["ident"][:]).then_inc(turned, 1)
                pe.wait_ge(bias_step, 4)
                pe.wait_ge(raw_done, 4)
                pe.wait_ge(lo_done, len(jobs))
                for c in range(2):
                    last = nc.tensor.matmul(bank[0][:, 0:256], bv_wide[:, c, :], wo_t[:, c, :], start=(c == 0), stop=(c == 1))
                last.then_inc(bo_ready, 1)

            @block.scalar
            def _(act):
                act.wait_ge(loaded, 96)
                for n, (kind, o, c) in enumerate(jobs):
                    act.wait_ge(turned, n + 1)
                    cols = slice(o * P, (o + 1) * P)
                    if kind == "q":
                        nc.scalar.activation(W["wq_hi"][:, c, cols], bank[n % 2][:, 0:P], ACT.Copy,
                                             scale=gamma_col[:, c:c + 1]).then_inc(hi_done, 1)
                    else:
                        nc.scalar.activation(wo_t[:, c, cols], bank[n % 2][:, 0:P], ACT.Copy).then_inc(raw_done, 1)
                        nc.scalar.activation(W["wo_hi"][:, c, cols], bank[n % 2][:, 0:P], ACT.Copy).then_inc(hi_done, 1)

            @block.vector
            def _(dve):
                nc.vector.memset(zeros[:], 0.0).then_inc(zeros_ready, 1)
                dve.wait_ge(filler_step, 8)
                nc.vector.tensor_scalar(filler[:, :, :, 2], filler[:, :, :, 2], 511, None, ALU.bitwise_and).then_inc(filler_step, 1)
                nc.vector.tensor_scalar(dest_base[:], dest_base[:], 4, None, ALU.arith_shift_right).then_inc(filler_step, 1)
                dve.wait_ge(filler_step, 10)
                nc.vector.tensor_copy(dest_first[:], dest_base[:]).then_inc(filler_step, 1)
                dve.wait_ge(filler_step, 11)
                nc.vector.tensor_scalar(dest_first[:], dest_first[:], 512.0, float(KE * T), ALU.mult, ALU.add).then_inc(filler_step, 1)
                dve.wait_ge(filler_step, 12)
                nc.vector.tensor_scalar(filler[:, :, :, 2], filler[:, :, :, 2], dest_first[:], None, ALU.add).then_inc(filler_step, 1)
                dve.wait_ge(loaded, 96)
                nc.vector.tensor_tensor(wbeta[:], wq_in[:], beta_rows[:].unsqueeze(1).to_broadcast([P, 6, 256]), ALU.mult).then_inc(bias_step, 1)
                dve.wait_ge(bias_step, 1)
                nc.vector.reduce_sum(wb_col[:], wbeta[:], AX_X).then_inc(bias_step, 1)
                dve.wait_ge(bias_step, 2)
                nc.vector.tensor_tensor(W["b_col"][:], wb_col[:], bq_col[:], ALU.add).then_inc(bias_step, 1)
                dve.wait_ge(bias_step, 3)
                nc.vector.tensor_copy(bv_wide[:], W["b_col"][:, 4:6].unsqueeze(2).to_broadcast([P, 2, P])).then_inc(bias_step, 1)
                for n, (kind, o, c) in enumerate(jobs):
                    dve.wait_ge(hi_done, n + 1)
                    cols = slice(o * P, (o + 1) * P)
                    if kind == "q":
                        nc.vector.scalar_tensor_tensor(out=W["wq_lo"][:, c, cols], in0=bank[n % 2][:, 0:P],
                                                       scalar=gamma_col[:, c:c + 1], in1=W["wq_hi"][:, c, cols].bitcast(F32),
                                                       op0=ALU.mult, op1=ALU.subtract).then_inc(lo_done, 1)
                    else:
                        nc.vector.tensor_tensor(W["wo_lo"][:, c, cols], bank[n % 2][:, 0:P],
                                                W["wo_hi"][:, c, cols].bitcast(F32), ALU.subtract).then_inc(lo_done, 1)
                dve.wait_ge(bo_ready, 1)
                nc.vector.tensor_tensor(W["bo"][:], bank[0][:, 0:256], bo_rows[:], ALU.add).then_inc(bo_done, 1)
                dve.wait_ge(bo_done, 1)


USES = [
    (0, "mt", 1, 0), (0, "v", 1, 0),
    (1, "cx", 3, -1), (1, "zt", 0, 1),
    (2, "zt", 1, 1),
    (3, "qk", 0, 1), (3, "cn", 0, -1),
    (4, "mt", 2, 0), (4, "qk", 1, 1), (4, "cn", 1, -1),
    (5, "qk", 2, 1), (5, "cx", 0, 0),
    (6, "qk", 3, 1), (6, "xt", 0, -2),
    (7, "xt", 1, -2), (7, "out", 0, -1),
    (8, "mt", 3, 0), (8, "out", 1, -1),
    (9, "cx", 1, 0),
    (10, "lg", 0, -2),
    (12, "mt", 0, 1),
    (13, "cx", 2, 0),
    (15, "v", 0, 1),
]
PER = {"mt": 4, "v": 2, "cx": 4, "zt": 2, "cn": 2, "qk": 4, "xt": 2, "out": 2, "lg": 1}
NB = 3
PV_AT = 2
AT = {"pe": {}, "act": {}, "dve": {}}
DEF = {"pe": (3, 3, 3), "act": (1, 1, 1), "dve": (1, 2, 3)}


def at(engine, kind, i, n):
    if (kind, i) in AT[engine]:
        return AT[engine][kind, i]
    if kind == "ctx":
        return 0
    return DEF[engine][min(n, 2)]
BANK = {(kind, i): n % NB for n, (_, kind, i, _) in enumerate(USES)}


def attention(nc, W, x, y_d, x2_d, xn2_d, lg_d, qk_d, mt_d, router, w_src, w_max):
    B = x.shape[0]
    with ExitStack() as ctx:
        def sb(name, shape, dt=F32):
            return ctx.enter_context(nc.sbuf_tensor("a_" + name, shape, dt))

        def sem(name):
            return ctx.enter_context(nc.semaphore("a_" + name))

        v_aug, q_st, k_st, ident = W["v_aug"], W["q_st"], W["k_st"], W["ident"]
        xa = sb("xa", [P, 4, 256])
        y = sb("y", [P, 4, 256])
        z = sb("z", [P, 4, 256])
        z_hi = sb("z_hi", [P, 2, 512], F32R)
        z_lo = sb("z_lo", [P, 2, 512], F32R)
        qk_hi = sb("qk_hi", [P, 4, 512], F32R)
        qk_lo = sb("qk_lo", [P, 4, 512], F32R)
        probs = sb("probs", [P, 2, HG, 512])
        mx = sb("mx", [P, 2, 16])
        mt = sb("mt", [16, 2, 2, P], F32R)
        ctx_t = sb("ctx_t", [P, 2, 512])
        rsum = sb("rsum", [P, 16])
        cn = sb("cn", [P, 4, 256])
        c_hi = sb("c_hi", [P, 2, 512], F32R)
        c_lo = sb("c_lo", [P, 2, 512], F32R)
        xp = sb("xp", [P, 4, 256])
        yp = sb("yp", [P, 4, 256])
        a = sb("a", [P, 4, 256])
        x2 = sb("x2", [P, 4, 256])
        xn2 = sb("xn2", [P, 4, 256])
        xn_s = sb("xn_s", [P, 4, 2, 256], F16)
        w_raw = sb("w_raw", [P, 2, 2048])
        x_t = sb("x_t", [P, 2, 512])
        lgt = sb("lgt", [8, 512])
        wr = sb("wr", [P, 2, 8])
        st = {k: sb(f"st{k}", [P, 4, 2]) for k in (1, 3, 4)}
        bst = {k: sb(f"bst{k}", [P, 4, 6]) for k in (1, 3, 4)}
        rs = {k: sb(f"rs{k}", [P, 4]) for k in (1, 3, 4)}
        r2 = sb("r2", [P, 4])
        t2 = sb("t2", [P, 4])

        misc = [ctx.enter_context(nc.psum_tensor(f"misc{i}", [P, 512], F32)) for i in range(NB)]
        sm = [ctx.enter_context(nc.psum_tensor(f"sm{i}", [P, 512], F32)) for i in range(2)]
        stp = [ctx.enter_context(nc.psum_tensor(f"stp{i}", [P, 512], F32)) for i in range(2)]
        cacc = ctx.enter_context(nc.psum_tensor("cacc", [P, 512], F32))

        wr_in = sem("wr_in")
        sp_passed, pool_passed, dve_passed = sem("sp_passed"), sem("pool_passed"), sem("dve_passed")
        x_in, xp_in, yp_in = sem("x_in"), sem("xp_in"), sem("yp_in")
        y_out, x2_out, xn2_out, lg_out = sem("y_out"), sem("x2_out"), sem("xn2_out"), sem("lg_out")
        qk_w = [sem(f"qk_w{c}") for c in range(2)]
        stack_in = [sem(f"stack_in{g}") for g in range(G)]
        mt_w = sem("mt_w")
        m_in = [sem(f"m_in{g}") for g in range(G)]
        full = {k: sem(f"{k}_full") for k in PER}
        zt_hi, qkh, cnh, mth = sem("zt_hi"), sem("qk_hi"), sem("cn_hi"), sem("mt_hi")
        free = {k: sem(f"{k}_free") for k in PER}
        sm_full = sem("sm_full")
        max_done = [sem(f"max_done{k}") for k in range(2)]
        st_full, exp_done = sem("st_full"), sem("exp_done")
        pv_done, ctx_full, ctx_evac = sem("pv_done"), sem("ctx_full"), sem("ctx_evac")
        bn = {k: sem(f"bn{k}") for k in (1, 3, 4)}
        agg = {k: sem(f"agg{k}") for k in (1, 3, 4)}
        rstd = {k: sem(f"rstd{k}") for k in (1, 3, 4)}
        y_done, z_done = sem("y_done"), sem("z_done")
        xn_hi, xn_lo = sem("xn_hi"), sem("xn_lo")
        w_in, w_red = [sem(f"w_in{k}") for k in range(2)], sem("w_red")
        recip = sem("recip")
        yp_done, lna_done, x2_done, xn2_done = sem("yp_done"), sem("lna_done"), sem("x2_done"), sem("xn2_done")

        def wait(eng, s, value):
            if not (isinstance(value, int) and value <= 0):
                eng.wait_ge(s, value)

        def there(b, lag):
            return not isinstance(b, int) or 0 <= b + lag < B

        def before(b, kind, i):
            at = [(k, j) for _, k, j, _ in USES].index((kind, i))
            for back in range(1, 4 * len(USES)):
                pos = at - back
                _, k, j, lag = USES[pos % len(USES)]
                it = b + pos // len(USES)
                if BANK[k, j] == BANK[kind, i] and there(it, lag):
                    return k, (it + lag) * PER[k] + j + 1
            return None

        def iterations(eng, body):
            for b in range(-2, 2):
                body(b)
            if B > 4:
                with eng.Fori(2, B - 2) as b:
                    body(b)
            for b in range(max(B - 2, 2), B + 2):
                body(b)

        with nc.Block() as block:
            @block.sync
            def _(sp):
                sp.dma_start(wr[:], router.rearrange("(c p) e -> p c e", p=P)).then_inc(wr_in, 16)

                def write_qk(i, c):
                    wait(sp, free["qk"], 4 * i + 2 * c + 2)
                    carry(sp, sp_passed)
                    wait(sp, stack_in[2 * c], 96 * i)
                    wait(sp, stack_in[2 * c + 1], 96 * i)
                    for part, src in enumerate((qk_hi, qk_lo)):
                        for k in range(2):
                            sp.dma_start(qk_d[2 * k + part, c * P:(c + 1) * P, :], src[:, 2 * c + k, :].bitcast(F32)).then_inc(qk_w[c], 16)

                def stack(i, g, old):
                    c = g // 2
                    wait(sp, qk_w[c], 64 * (i + 1))
                    carry(sp, sp_passed)
                    wait(sp, st_full, old)
                    for st_, parts in ((q_st, (0, 0, 1)), (k_st, (2, 3, 2))):
                        for r, part in enumerate(parts):
                            src = qk_d[part, g * 64:(g + 1) * 64, :].rearrange("(h d) n -> d h n", d=HD)
                            sp.dma_start(st_[r * HD:(r + 1) * HD, g, :, :].bitcast(F32), src).then_inc(stack_in[g], 16)

                def max_rows(i, g, n):
                    wait(sp, free["mt"], n + 1)
                    wait(sp, m_in[(g - 1) % 4], 16 * (i + (g > 0)))
                    sp.dma_start(mt_d.rearrange("r (k n) -> k r n", n=P), mt[:, g % 2, :, :].bitcast(F32)).then_inc(mt_w, 16)
                    wait(sp, mt_w, 16 * (n + 1))
                    sp.dma_start(q_st[KR:KM, g, :, :].rearrange("r h n -> r (h n)").bitcast(F32), mt_d).then_inc(m_in[g], 16)

                def body(b):
                    n = 4 * b
                    if there(b, 0):
                        max_rows(b, 1, n + 1)
                        stack(b, 3, 64 * b)
                        max_rows(b, 2, n + 2)
                    if there(b, 1):
                        write_qk(b + 1, 0)
                        stack(b + 1, 0, 16 * (n + 1))
                        write_qk(b + 1, 1)
                        stack(b + 1, 1, 16 * (n + 2))
                    if there(b, 0):
                        max_rows(b, 3, n + 3)
                    if there(b, 1):
                        stack(b + 1, 2, 16 * (n + 3))
                        max_rows(b + 1, 0, n + 4)
                iterations(sp, body)

            @block.gpsimd
            def _(pool):
                def rsqrt(k, i, steps, first, src, dst):
                    carry(pool, pool_passed)
                    nc.gpsimd.tensor_scalar(dst, src, EPS, None, ALU.add).then_inc(rstd[k], 1)
                    wait(pool, rstd[k], steps * i + first + 1)
                    nc.gpsimd.tensor_tensor(dst, dst, W["neg_half"][:, 0:4], ALU.pow).then_inc(rstd[k], 1)
                    wait(pool, rstd[k], steps * i + first + 2)

                def rows(dram, i):
                    return dram[bass.ts(i, 512), :].rearrange("(t p) h -> p t h", p=P)

                def body(b):
                    if there(b, 2):
                        i = b + 2
                        wait(pool, y_done, 4 * i)
                        carry(pool, pool_passed)
                        pool.dma_start(xa[:], rows(x.rearrange("b s h -> (b s) h"), i)).then_inc(x_in, 16)
                    if there(b, -2):
                        i = b - 2
                        wait(pool, xn_lo, i + 1)
                        carry(pool, pool_passed)
                        pool.dma_start(rows(xn2_d, i), xn_s[:].rearrange("p t a h -> p t (a h)")).then_inc(xn2_out, 16)
                    if there(b, -1):
                        i = b - 1
                        wait(pool, x2_done, i)
                        carry(pool, pool_passed)
                        pool.dma_start(xp[:], rows(x.rearrange("b s h -> (b s) h"), i)).then_inc(xp_in, 16)
                        wait(pool, free["out"], 2 * i)
                        wait(pool, y_out, 16 * (i + 1))
                        carry(pool, pool_passed)
                        pool.dma_start(yp[:], rows(y_d, i)).then_inc(yp_in, 16)
                        wait(pool, yp_in, 16 * (i + 1))
                        nc.gpsimd.tensor_tensor(yp[:], yp[:], W["bo"][:].unsqueeze(1).to_broadcast([P, 4, 256]), ALU.add).then_inc(yp_done, 1)
                        wait(pool, agg[3], 4 * (i + 1))
                        rsqrt(3, i, 2, 0, st[3][:, :, 1], rs[3][:])
                    if there(b, 2):
                        i = b + 2
                        wait(pool, agg[1], 4 * (i + 1))
                        rsqrt(1, i, 6, 0, st[1][:, :, 1], rs[1][:])
                        nc.gpsimd.tensor_tensor(t2[:], rs[1][:], rs[1][:], ALU.mult).then_inc(rstd[1], 1)
                        wait(pool, rstd[1], 6 * i + 3)
                        nc.gpsimd.tensor_tensor(t2[:], t2[:], st[1][:, :, 1], ALU.mult).then_inc(rstd[1], 1)
                        wait(pool, rstd[1], 6 * i + 4)
                        wait(pool, z_done, 4 * i)
                        rsqrt(1, i, 6, 4, t2[:], r2[:])
                    if there(b, -1):
                        i = b - 1
                        wait(pool, lna_done, 4 * (i + 1))
                        wait(pool, xp_in, 16 * (i + 1))
                        wait(pool, x2_out, 16 * i)
                        wait(pool, xn2_done, 4 * i)
                        nc.gpsimd.tensor_tensor(x2[:], xp[:], a[:], ALU.add).then_inc(x2_done, 1)
                        wait(pool, agg[4], 4 * (i + 1))
                        rsqrt(4, i, 2, 0, st[4][:, :, 1], rs[4][:])
                        wait(pool, x2_done, i + 1)
                        carry(pool, pool_passed)
                        pool.dma_start(rows(x2_d, i), x2[:]).then_inc(x2_out, 16)
                    if there(b, -2):
                        i = b - 2
                        wait(pool, free["lg"], i + 1)
                        carry(pool, pool_passed)
                        pool.dma_start(lg_d[:, bass.ts(i, 512)], lgt[:]).then_inc(lg_out, 16)
                    if there(b, 2):
                        i = b + 2
                        wait(pool, y_done, 4 * (i + 1))
                        carry(pool, pool_passed)
                        pool.dma_start(rows(y_d, i), y[:]).then_inc(y_out, 16)
                iterations(pool, body)
                for s in (y_out, x2_out, xn2_out, lg_out):
                    pool.wait_ge(s, 16 * B)

            @block.tensor
            def _(pe):
                te = nc.tensor

                def bank_for(b, kind, i):
                    prev = before(b, kind, i)
                    if prev is not None:
                        wait(pe, free[prev[0]], prev[1])
                    return misc[BANK[kind, i]]

                def turn(bank, src, c):
                    for t in range(4):
                        last = te.transpose(bank[:, t * P:(t + 1) * P], src[:, t, c * P:(c + 1) * P], ident[:])
                    return last

                def use(b, kind, i, d):
                    bank = bank_for(b, kind, i)
                    if kind == "zt":
                        wait(pe, z_done, 4 * (d + 1))
                        last = turn(bank, z, i)
                    elif kind == "qk":
                        wait(pe, free["zt"], 2 * (d + 1))
                        col = (i % 2) * 256 + (i // 2) * P
                        last = split3(te, bank[:], [W["wq_hi"][:, c, col:col + P] for c in range(2)],
                                      [W["wq_lo"][:, c, col:col + P] for c in range(2)],
                                      [z_hi[:, c, :] for c in range(2)], [z_lo[:, c, :] for c in range(2)])
                    elif kind == "v":
                        wait(pe, free["zt"], 2 * (d + 1))
                        for half in range(2):
                            tk = slice((2 * i + half) * P, (2 * i + half + 1) * P)
                            last = split3(te, bank[:, half * 256:(half + 1) * 256],
                                          [z_hi[:, c, tk] for c in range(2)], [z_lo[:, c, tk] for c in range(2)],
                                          [W["wq_hi"][:, c, 512:768] for c in range(2)],
                                          [W["wq_lo"][:, c, 512:768] for c in range(2)])
                    elif kind == "mt":
                        wait(pe, max_done[1], 8 * (4 * d + i + 1))
                        last = te.transpose(bank[0:16, 0:P], mx[:, i % 2, :], ident[:])
                    elif kind == "cx":
                        wait(pe, ctx_evac, 4 * d + i + 1)
                        for t in range(4):
                            last = te.transpose(bank[:, t * P:(t + 1) * P], ctx_t[:, i % 2, t * P:(t + 1) * P], ident[:])
                    elif kind == "cn":
                        wait(pe, free["cx"], 4 * (d + 1))
                        last = turn(bank, cn, i)
                    elif kind == "out":
                        wait(pe, free["cn"], 2 * (d + 1))
                        for half in range(2):
                            tk = slice((2 * i + half) * P, (2 * i + half + 1) * P)
                            last = split3(te, bank[:, half * 256:(half + 1) * 256],
                                          [c_hi[:, c, tk] for c in range(2)], [c_lo[:, c, tk] for c in range(2)],
                                          [W["wo_hi"][:, c, :] for c in range(2)], [W["wo_lo"][:, c, :] for c in range(2)])
                    elif kind == "xt":
                        wait(pe, xn2_done, 4 * (d + 1))
                        last = turn(bank, xn2, i)
                    else:
                        wait(pe, free["xt"], 2 * (d + 1))
                        for c in range(2):
                            last = te.matmul(bank[0:8, :], wr[:, c, :], x_t[:, c, :], start=(c == 0), stop=(c == 1))
                    last.then_inc(full[kind], 1)

                def context_part(b, s):
                    lag = -1 if s == 0 else 0
                    if there(b, lag):
                        q = 16 * b + s - 1
                        gq, jq = (s - 1) % 16 // 4, (s - 1) % 4
                        wait(pe, exp_done, 4 * (q + 1))
                        if jq % 2 == 0:
                            wait(pe, free["v"], 2 * (b + lag) + jq // 2 + 1)
                        if jq == 0:
                            wait(pe, ctx_evac, 4 * b + gq)
                        for h in range(HG):
                            last = te.matmul(cacc[32 * h:32 * h + 32, :], v_aug[:, jq, HG * gq + h, :],
                                             probs[:, jq % 2, h, :], start=(jq == 0), stop=(jq == 3),
                                             skip_group_check=True)
                        last.then_inc(pv_done, 1)

                def beside(b, s, r):
                    uses = [u for u in USES if u[0] == s]
                    for n, (_, kind, i, lag) in enumerate(uses):
                        if r == at("pe", kind, i, n) and there(b, lag):
                            use(b, kind, i, b + lag)

                def body(b):
                    for s in range(16):
                        g, j = s // 4, s % 4
                        da, ga = b + (g >= 2), (g + 2) % 4
                        for r in range(4):
                            if there(b, int(g >= 2)):
                                if j == 0 and r == 0:
                                    wait(pe, stack_in[ga], 96 * (da + 1))
                                wait(pe, max_done[r % 2], 32 * da + 8 * ga + 2 * j + r // 2)
                                te.matmul(sm[r % 2][:], q_st[0:KR, ga, j, r * P:(r + 1) * P], k_st[0:KR, ga, j, :],
                                          start=True, stop=True).then_inc(sm_full, 1)
                            if there(b, 0):
                                if j == 0 and r == 0:
                                    wait(pe, m_in[g], 16 * (b + 1))
                                wait(pe, exp_done, 64 * b + 4 * s + r - 1)
                                te.matmul(stp[r % 2][:], k_st[0:KM, g, r, j * P:(j + 1) * P], q_st[0:KM, g, r, :],
                                          start=True, stop=True).then_inc(st_full, 1)
                            if r == PV_AT:
                                context_part(b, s)
                            beside(b, s, r)
                pe.wait_ge(wr_in, 16)
                iterations(pe, body)

            @block.scalar
            def _(act):
                sc = nc.scalar

                def extra(b, kind, i, lag):
                    if not there(b, lag):
                        return
                    d = b + lag
                    bank = misc[BANK[kind, i]] if (kind, i) in BANK else None
                    if kind in PER:
                        wait(act, full[kind], PER[kind] * d + i + 1)
                    if kind == "zt":
                        wait(act, full["v"], 2 * d)
                        sc.activation(z_hi[:, i, :], bank[:], ACT.Copy).then_inc(zt_hi, 1)
                    elif kind == "qk":
                        wait(act, qk_w[i // 2], 64 * d)
                        sc.activation(qk_hi[:, i, :], bank[:], ACT.Identity,
                                      bias=W["b_col"][:, (i % 2) * 2 + i // 2:(i % 2) * 2 + i // 2 + 1]).then_inc(qkh, 1)
                    elif kind == "v":
                        wait(act, pv_done, 16 * d + (0 if i else -2))
                        sc.activation(v_aug[:, 2 * i:2 * i + 2, :, 0:HD],
                                      bank[:].rearrange("p (t h d) -> p t h d", t=2, h=NH), ACT.Copy).then_inc(free["v"], 1)
                    elif kind == "ctx":
                        n = 4 * d + i
                        wait(act, pv_done, 4 * (n + 1))
                        wait(act, full["cx"], n - 1)
                        sc.activation(ctx_t[:, i % 2, :], cacc[:], ACT.Copy).then_inc(ctx_evac, 1)
                    elif kind == "cn":
                        wait(act, full["out"], 2 * d)
                        sc.activation(c_hi[:, i, :], bank[:], ACT.Copy).then_inc(cnh, 1)
                    elif kind == "xt":
                        wait(act, full["lg"], d)
                        sc.activation(x_t[:, i, :], bank[:], ACT.Copy).then_inc(free["xt"], 1)
                    elif kind == "lg":
                        wait(act, lg_out, 16 * d)
                        sc.activation(lgt[:], bank[0:8, :], ACT.Copy).then_inc(free["lg"], 1)
                    elif kind == "xn_hi":
                        wait(act, xn2_done, 4 * (d + 1))
                        wait(act, xn2_out, 16 * d)
                        sc.activation(xn_s[:, :, 0, :], xn2[:], ACT.Copy, scale=XS).then_inc(xn_hi, 1)
                    elif kind == "w_load":
                        load_w(i)
                    elif kind == "z":
                        wait(act, y_done, 4 * (d + 1))
                        wait(act, rstd[1], 6 * (d + 1))
                        wait(act, full["zt"], 2 * d)
                        for t in range(4):
                            sc.activation(z[:, t, :], y[:, t, :], ACT.Copy, scale=r2[:, t:t + 1]).then_inc(z_done, 1)

                def load_w(n):
                    if n < 12:
                        if n >= 2:
                            act.wait_ge(w_red, n - 1)
                        for e in range(2):
                            act.dma_start(w_raw[:, n % 2, e * 1024:(e + 1) * 1024].rearrange("p (c f) -> p c f", c=2 if n < 8 else 4),
                                          w_src[n // 4][n % 4 * 2 + e]).then_inc(w_in[n % 2], 16)

                extras = {
                    0: [("v", 0, 0)], 1: [("ctx", 3, -1), ("v", 1, 0)], 2: [("zt", 0, 1), ("xn_hi", 0, -2)], 3: [("zt", 1, 1)],
                    4: [("qk", 0, 1), ("cn", 0, -1)], 5: [("ctx", 0, 0), ("qk", 1, 1), ("cn", 1, -1)],
                    6: [("qk", 2, 1)], 7: [("qk", 3, 1), ("xt", 0, -2)], 8: [("xt", 1, -2)],
                    9: [("ctx", 1, 0)], 11: [("lg", 0, -2)], 13: [("ctx", 2, 0)], 15: [("z", 0, 2)],
                }

                def body(b):
                    for s in range(16):
                        j = s % 4
                        if isinstance(b, int) and b == -1:
                            load_w(s)
                        for r in range(4):
                            if there(b, 0):
                                q = 16 * b + s
                                if r == 0:
                                    wait(act, pv_done, q - 1)
                                wait(act, st_full, 4 * q + r + 1)
                                sc.activation(probs[:, j % 2, r, :], stp[r % 2][:], ACT.Exp, scale=HD ** -0.5).then_inc(exp_done, 1)
                            for n, (kind, i, lag) in enumerate(extras.get(s, [])):
                                if r == at("act", kind, i, n):
                                    extra(b, kind, i, lag)
                iterations(act, body)

            @block.vector
            def _(dve):
                ve = nc.vector

                def stats(k, src, i):
                    for t in range(4):
                        ve.bn_stats(bst[k][:, t, :], src[:, t, :]).then_inc(bn[k], 1)
                    for t in range(4):
                        wait(dve, bn[k], 4 * i + t + 1)
                        carry(dve, dve_passed)
                        ve.bn_aggr(st[k][:, t, :], bst[k][:, t, :]).then_inc(agg[k], 1)

                def normal(k, dst, src, done):
                    for t in range(4):
                        ve.tensor_scalar(dst[:, t, :], src[:, t, :], st[k][:, t, 0:1], rs[k][:, t:t + 1],
                                         ALU.subtract, ALU.mult).then_inc(done, 1)

                def extra(b, kind, i, lag):
                    if not there(b, lag):
                        return
                    d = b + lag
                    bank = misc[BANK[kind, i]] if (kind, i) in BANK else None
                    n = 4 * d + i
                    if kind == "mt":
                        wait(dve, full["mt"], n + 1)
                        wait(dve, mt_w, 16 * (n - 1))
                        ve.tensor_scalar(mt[:, i % 2, 0, :], bank[0:16, 0:P], -1.0, None, ALU.mult).then_inc(mth, 1)
                        wait(dve, mth, n + 1)
                        ve.scalar_tensor_tensor(out=mt[:, i % 2, 1, :], in0=bank[0:16, 0:P], scalar=-1.0,
                                                in1=mt[:, i % 2, 0, :].bitcast(F32), op0=ALU.mult,
                                                op1=ALU.subtract).then_inc(free["mt"], 1)
                    elif kind == "cx":
                        wait(dve, full["cx"], n + 1)
                        wait(dve, full["cn"], 2 * d)
                        v = bank[:].rearrange("p (t h d) -> p t h d", t=4, h=HG)
                        ve.reciprocal(rsum[:].rearrange("p (t h) -> p t h", t=4), v[:, :, :, HD]).then_inc(recip, 1)
                        wait(dve, recip, n + 1)
                        ve.tensor_tensor(cn[:, :, i * 64:(i + 1) * 64].rearrange("p t (h d) -> p t h d", h=HG),
                                         v[:, :, :, 0:HD],
                                         rsum[:].rearrange("p (t h) -> p t h", t=4).unsqueeze(3).to_broadcast([P, 4, HG, HD]),
                                         ALU.mult).then_inc(free["cx"], 1)
                    elif kind == "zt":
                        wait(dve, zt_hi, 2 * d + i + 1)
                        ve.tensor_tensor(z_lo[:, i, :], bank[:], z_hi[:, i, :].bitcast(F32), ALU.subtract).then_inc(free["zt"], 1)
                    elif kind == "cn":
                        wait(dve, cnh, 2 * d + i + 1)
                        ve.tensor_tensor(c_lo[:, i, :], bank[:], c_hi[:, i, :].bitcast(F32), ALU.subtract).then_inc(free["cn"], 1)
                    elif kind == "qk":
                        wait(dve, qkh, n + 1)
                        col = (i % 2) * 2 + i // 2
                        ve.scalar_tensor_tensor(out=qk_lo[:, i, :], in0=bank[:], scalar=W["b_col"][:, col:col + 1],
                                                in1=qk_hi[:, i, :].bitcast(F32), op0=ALU.add,
                                                op1=ALU.subtract).then_inc(free["qk"], 1)
                    elif kind == "out":
                        wait(dve, full["out"], 2 * d + i + 1)
                        wait(dve, yp_done, d + 1)
                        wait(dve, x2_done, d)
                        ve.tensor_tensor(a[:, 2 * i:2 * i + 2, :], bank[:].rearrange("p (t h) -> p t h", t=2),
                                         yp[:, 2 * i:2 * i + 2, :], ALU.add).then_inc(free["out"], 1)
                    elif kind == "stats3":
                        wait(dve, free["out"], 2 * (d + 1))
                        stats(3, a, d)
                    elif kind == "lna":
                        wait(dve, rstd[3], 2 * (d + 1))
                        normal(3, a, a, lna_done)
                    elif kind == "stats4":
                        wait(dve, x2_done, d + 1)
                        stats(4, x2, d)
                    elif kind == "xn2":
                        wait(dve, rstd[4], 2 * (d + 1))
                        wait(dve, full["xt"], 2 * d)
                        wait(dve, xn_lo, d)
                        normal(4, xn2, x2, xn2_done)
                    elif kind == "xn_lo":
                        wait(dve, xn_hi, d + 1)
                        ve.scalar_tensor_tensor(out=xn_s[:, :, 1, :], in0=xn2[:], scalar=XS, in1=xn_s[:, :, 0, :],
                                                op0=ALU.mult, op1=ALU.subtract).then_inc(xn_lo, 1)
                    elif kind == "stats1":
                        wait(dve, x_in, 16 * (d + 1))
                        wait(dve, rstd[1], 6 * d)
                        stats(1, xa, d)
                    elif kind == "y":
                        wait(dve, rstd[1], 6 * d + 2)
                        wait(dve, z_done, 4 * d)
                        wait(dve, y_out, 16 * d)
                        normal(1, y, xa, y_done)

                extras = {
                    0: [("xn2", 0, -2)], 1: [("mt", 1, 0)], 2: [("cx", 3, -1), ("zt", 0, 1)],
                    3: [("zt", 1, 1), ("xn_lo", 0, -2)], 4: [("qk", 0, 1), ("cn", 0, -1)],
                    5: [("mt", 2, 0), ("qk", 1, 1), ("cn", 1, -1)], 6: [("qk", 2, 1), ("cx", 0, 0)],
                    7: [("qk", 3, 1)], 8: [("out", 0, -1)], 9: [("mt", 3, 0), ("out", 1, -1)],
                    10: [("cx", 1, 0), ("stats3", 0, -1)], 11: [("stats1", 0, 2)], 12: [("lna", 0, -1)],
                    13: [("mt", 0, 1)], 14: [("cx", 2, 0), ("stats4", 0, -1)], 15: [("y", 0, 2)],
                }

                def body(b):
                    for s in range(16):
                        g, j = s // 4, s % 4
                        da, ga = b + (g >= 2), (g + 2) % 4
                        if isinstance(b, int) and b == -1 and s < 12:
                            dve.wait_ge(w_in[s % 2], 32 * (s // 2 + 1))
                            ve.reduce_max(w_max[:, s:s + 1], w_raw[:, s % 2, :], AX_X, apply_absolute_value=True).then_inc(w_red, 1)
                        for r in range(4):
                            if there(b, int(g >= 2)):
                                if j == 0 and r == 0:
                                    wait(dve, full["mt"], 4 * da + ga - 1)
                                wait(dve, sm_full, 64 * da + 16 * ga + 4 * j + r + 1)
                                ve.reduce_max(mx[:, ga % 2, 4 * j + r:4 * j + r + 1], sm[r % 2][:], AX_X).then_inc(max_done[r % 2], 1)
                            for n, (kind, i, lag) in enumerate(extras.get(s, [])):
                                if r == at("dve", kind, i, n):
                                    extra(b, kind, i, lag)
                iterations(dve, body)


def shared(nc, ctx):
    def sb(name, shape, dt=F32):
        return ctx.enter_context(nc.sbuf_tensor(name, shape, dt))
    return {
        "wq_hi": sb("wq_hi", [P, 2, 768], F32R), "wq_lo": sb("wq_lo", [P, 2, 768], F32R),
        "wo_hi": sb("wo_hi", [P, 2, 256], F32R), "wo_lo": sb("wo_lo", [P, 2, 256], F32R),
        "b_col": sb("b_col", [P, 6]), "bo": sb("bo", [P, 256]), 
        "v_aug": sb("v_aug", [P, 4, NH, VW]),
        "q_st": sb("q_st", [KM, G, HG, 512], F32R), "k_st": sb("k_st", [KM, G, HG, 512], F32R),
    }


E = 8
F = 512
KE = 2
WE = 3 * 1024
XS = 1024.0
U = 8
UP = 4


def tiles_of(T):
    n = KE * T // P + E - 1
    return -(-n // U) * U


def region(T):
    return -(-(T // P + E) // 16) * 16 * P


def route(nc, R, lg_d, table_d, T, w_loader, cleared):
    NT = T // P
    RT = region(T)
    with ExitStack() as ctx:
        def sb(name, shape, dt=F32):
            return ctx.enter_context(nc.sbuf_tensor("r_" + name, shape, dt))

        def sem(name):
            return ctx.enter_context(nc.semaphore("r_" + name))

        lgs = sb("lgs", [E, T])
        logits = sb("logits", [P, NT, E])
        col = {k: sb(k, [P, NT]) for k in ("m", "s", "p0", "p1", "ed", "w0", "w1")}
        work = sb("work", [P, NT, E])
        prob = sb("prob", [P, NT, E])
        hot = [sb(f"hot{k}", [P, NT, E]) for k in range(KE)]
        both = sb("both", [P, NT, E])
        scan = [sb(f"scan{k}", [P, NT, E]) for k in range(2)]
        total = sb("total", [P, NT, E])
        slot = sb("slot", [P, NT, KE])
        slot_i = sb("slot_i", [P, NT, KE], I32)
        pay = sb("pay", [P, NT, KE, 4], I32)
        before = sb("before", [P, P])
        ones = sb("ones", [P, P])
        iota_i = sb("iota_i", [P, E + E + tiles_of(T)], I32)
        iota = sb("iota", [P, E + E + tiles_of(T)])
        cnt_i = sb("cnt_i", [P, E], I32)
        ntile = sb("ntile", [P, E])
        tb = sb("tb", [P, E])
        jump = sb("jump", [P, E])
        e_f, off_f, tmp_f = (sb(n, [P, tiles_of(T)]) for n in ("e_f", "off_f", "tmp_f"))
        bank = [ctx.enter_context(nc.psum_tensor(f"r_bank{i}", [P, 512], F32)) for i in range(3)]

        lg_in, const, turned = sem("lg_in"), sem("const"), sem("turned")
        step = sem("step")
        exp_in, exp_out = sem("exp_in"), sem("exp_out")
        hot_ready, counted = sem("hot_ready"), sem("counted")
        slots_ready, scattered = sem("slots_ready"), sem("scattered")
        w_in, w_hi, w_lo = sem("w_in"), sem("w_hi"), sem("w_lo")
        pay_clear, wm_turned, wm_diag, wm_wide, scaled = sem("pay_clear"), sem("wm_turned"), sem("wm_diag"), sem("wm_wide"), sem("scaled")
        wm = sb("wm", [P, 3])
        wm_col = sb("wm_col", [3, 1])
        diag = sb("diag", [3, 3])
        sbank = ctx.enter_context(nc.psum_tensor("r_sbank", [P, 512], F32))

        w_src, raw = w_loader
        parts = [(e, k) for e in range(E) for k in range(3)]

        def part_of(which, e, k):
            return R[which][:, e * WE + k * 1024:e * WE + (k + 1) * 1024]

        with nc.Block() as block:
            @block.sync
            def _(sp):
                sp.dma_start(lgs[:], lg_d).then_inc(lg_in, 16)
                for n, (e, k) in enumerate(parts):
                    if n >= 3:
                        sp.wait_ge(w_lo, n - 2)
                    if n:
                        sp.wait_ge(w_in, 16 * n)
                    sp.dma_start(raw[:, n % 3, :].rearrange("p (c f) -> p c f", c=2 if k < 2 else 4), w_src[k][e]).then_inc(w_in, 16)

            @block.gpsimd
            def _(pool):
                nc.gpsimd.memset(pay[:], 0).then_inc(pay_clear, 1)
                pool.wait_ge(pay_clear, 1)
                nc.gpsimd.memset(before[:], 1.0).then_inc(const, 1)
                pool.wait_ge(const, 1)
                nc.gpsimd.affine_select(out=before[:], in_=before[:], compare_op=ALU.is_gt, fill=0.0,
                                        base=0, pattern=[[1, P]], channel_multiplier=-1).then_inc(const, 1)
                pool.wait_ge(const, 2)
                nc.gpsimd.memset(ones[:], 1.0).then_inc(const, 1)
                pool.wait_ge(const, 3)
                nc.gpsimd.iota(iota_i[:, 0:E], pattern=[[-1, E]], base=E, channel_multiplier=0).then_inc(const, 1)
                pool.wait_ge(const, 4)
                nc.gpsimd.iota(iota_i[:, E:2 * E], pattern=[[RT, E]], base=0, channel_multiplier=0).then_inc(const, 1)
                pool.wait_ge(const, 5)
                nc.gpsimd.iota(iota_i[:, 2 * E:], pattern=[[1, tiles_of(T)]], base=0, channel_multiplier=0).then_inc(const, 1)
                pool.wait_ge(const, 6)
                for k in range(KE):
                    nc.gpsimd.iota(pay[:, :, k, 0], pattern=[[P, NT]], base=0, channel_multiplier=1).then_inc(const, 1)
                    pool.wait_ge(const, 7 + 2 * k)
                    nc.gpsimd.iota(pay[:, :, k, 2], pattern=[[P, NT]], base=k * T, channel_multiplier=1).then_inc(const, 1)
                    pool.wait_ge(const, 8 + 2 * k)
                pool.wait_ge(slots_ready, 1)
                pool.wait_ge(cleared[0], cleared[1])
                for t in range(NT):
                    for k in range(KE):
                        pool.indirect_dma_start(table_d, bass.IndirectOffsetOnAxis(ap=slot_i[:, t, k:k + 1], axis=0),
                                                pay[:, t, k, :], None).then_inc(scattered, 16)
                pool.wait_ge(scattered, 16 * NT * KE)

            @block.tensor
            def _(pe):
                pe.wait_ge(wm_diag, 1)
                nc.tensor.transpose(sbank[0:3, 0:P], wm[:], R["ident"][:]).then_inc(wm_turned, 1)
                pe.wait_ge(wm_diag, 2)
                pe.wait_ge(const, 3)
                nc.tensor.matmul(sbank[:, P:P + 3], ones[0:3, :], diag[:], start=True, stop=True).then_inc(wm_wide, 1)
                pe.wait_ge(lg_in, 16)
                for t in range(NT):
                    last = nc.tensor.transpose(bank[0][:, t * E:(t + 1) * E], lgs[:, t * P:(t + 1) * P], R["ident"][0:E, 0:E])
                last.then_inc(turned, 1)
                pe.wait_ge(hot_ready, 1)
                pe.wait_ge(const, 3)
                n = NT * E
                nc.tensor.matmul(bank[1][:, 0:n], before[:], both[:].rearrange("p t e -> p (t e)"), start=True, stop=True)
                nc.tensor.matmul(bank[2][:, 0:n], ones[:], both[:].rearrange("p t e -> p (t e)"), start=True, stop=True).then_inc(counted, 1)

            @block.scalar
            def _(act):
                def split_hi(n):
                    e, k = parts[n]
                    act.wait_ge(w_in, 16 * (n + 1))
                    nc.scalar.activation(part_of("hi", e, k), raw[:, n % 3, :], ACT.Copy, scale=R["w_scale"][:, k:k + 1]).then_inc(w_hi, 1)
                act.wait_ge(scaled, 1)
                act.wait_ge(exp_in, 1)
                nc.scalar.activation(prob[:], work[:], ACT.Exp).then_inc(exp_out, 1)
                for n in range(4):
                    split_hi(n)
                act.wait_ge(exp_in, 2)
                nc.scalar.activation(col["ed"][:], col["s"][:], ACT.Exp).then_inc(exp_out, 1)
                for n in range(4, len(parts)):
                    split_hi(n)

            @block.vector
            def _(dve):
                ve = nc.vector
                done = [0]

                def chain(ins):
                    done[0] += 1
                    ins.then_inc(step, 1)
                    dve.wait_ge(step, done[0])

                def wide(v):
                    return v.unsqueeze(2).to_broadcast([P, NT, E])

                def over(v):
                    return v.unsqueeze(1).to_broadcast([P, NT, E])

                def split_lo(n):
                    e, k = parts[n]
                    dve.wait_ge(w_hi, n + 1)
                    ve.scalar_tensor_tensor(out=part_of("lo", e, k), in0=raw[:, n % 3, :], scalar=R["w_scale"][:, k:k + 1],
                                            in1=part_of("hi", e, k), op0=ALU.mult, op1=ALU.subtract).then_inc(w_lo, 1)

                chain(ve.reduce_max(wm[:], R["w_max"][:].rearrange("p (k n) -> p k n", k=3), AX_X))
                ve.tensor_scalar(wm[:], wm[:], 2.0 ** -100, None, ALU.max).then_inc(wm_diag, 1)
                dve.wait_ge(wm_turned, 1)
                chain(ve.reduce_max(wm_col[:], sbank[0:3, 0:P], AX_X))
                ve.tensor_scalar(diag[:], R["ident"][0:3, 0:3], wm_col[:], None, ALU.mult).then_inc(wm_diag, 1)
                dve.wait_ge(wm_wide, 1)
                chain(ve.tensor_copy(wm[:], sbank[:, P:P + 3]))
                chain(ve.tensor_scalar(wm[:].bitcast(I32), wm[:].bitcast(I32), 23, None, ALU.arith_shift_right))
                chain(ve.tensor_scalar(wm[:].bitcast(I32), wm[:].bitcast(I32), 23, None, ALU.logical_shift_left))
                chain(ve.reciprocal(R["w_scale"][:], wm[:]))
                inv = R["w_scale"]
                chain(ve.tensor_scalar(R["g_scale"][:], wm[:, 0:1], 2.0 ** -13 / XS, None, ALU.mult))
                chain(ve.tensor_scalar(R["u_scale"][:], inv[:, 0:1], 2.0 ** -16 / XS, None, ALU.mult))
                chain(ve.tensor_scalar(R["y_scale"][:], wm[:, 0:1], wm[:, 1:2], 2.0 ** -10, ALU.mult, ALU.mult))
                chain(ve.tensor_scalar(R["y_scale"][:], R["y_scale"][:], wm[:, 2:3], None, ALU.mult))
                chain(ve.tensor_tensor(R["y_scale2"][:], R["y_scale"][:], R["y_scale"][:], ALU.mult))
                ve.tensor_scalar(inv[:], inv[:], 2.0 ** 13, None, ALU.mult).then_inc(scaled, 1)
                dve.wait_ge(const, 10)
                chain(ve.tensor_copy(iota[:], iota_i[:]))
                dve.wait_ge(turned, 1)
                chain(ve.tensor_copy(logits[:].rearrange("p t e -> p (t e)"), bank[0][:, 0:NT * E]))
                chain(ve.reduce_max(col["m"][:], logits[:], AX_X))
                ve.tensor_tensor(work[:], logits[:], wide(col["m"][:]), ALU.subtract).then_inc(exp_in, 1)
                dve.wait_ge(exp_out, 1)
                chain(ve.reduce_sum(col["s"][:], prob[:], AX_X))
                chain(ve.reciprocal(col["m"][:], col["s"][:]))
                chain(ve.tensor_tensor(prob[:], prob[:], wide(col["m"][:]), ALU.mult))
                for k in range(KE):
                    chain(ve.reduce_max(col[f"p{k}"][:], prob[:], AX_X))
                    chain(ve.tensor_tensor(work[:], prob[:], wide(col[f"p{k}"][:]), ALU.is_equal))
                    chain(ve.tensor_tensor(work[:], work[:], over(iota[:, 0:E]), ALU.mult))
                    chain(ve.reduce_max(col["m"][:], work[:], AX_X))
                    chain(ve.tensor_tensor(hot[k][:], work[:], wide(col["m"][:]), ALU.is_equal))
                    if k == 0:
                        chain(ve.scalar_tensor_tensor(out=prob[:], in0=hot[0][:], scalar=-2.0, in1=prob[:], op0=ALU.mult, op1=ALU.add))
                ve.tensor_tensor(both[:], hot[0][:], hot[1][:], ALU.add).then_inc(hot_ready, 1)
                ve.tensor_tensor(col["s"][:], col["p1"][:], col["p0"][:], ALU.subtract).then_inc(exp_in, 1)
                for n in range(4):
                    split_lo(n)
                dve.wait_ge(exp_out, 2)
                chain(ve.tensor_scalar(col["m"][:], col["ed"][:], 1.0, None, ALU.add))
                chain(ve.reciprocal(col["w0"][:], col["m"][:]))
                chain(ve.tensor_tensor(col["w1"][:], col["ed"][:], col["w0"][:], ALU.mult))
                for k in range(KE):
                    chain(ve.tensor_copy(pay[:, :, k, 1].bitcast(F32), col[f"w{k}"][:]))
                dve.wait_ge(counted, 1)
                chain(ve.tensor_copy(total[:].rearrange("p t e -> p (t e)"), bank[2][:, 0:NT * E]))
                src = total
                shift, n = 1, 0
                while shift < NT:
                    dst = scan[n % 2]
                    chain(ve.tensor_copy(dst[:, 0:shift, :], src[:, 0:shift, :]))
                    chain(ve.tensor_tensor(dst[:, shift:, :], src[:, shift:, :], src[:, 0:NT - shift, :], ALU.add))
                    src, shift, n = dst, shift * 2, n + 1
                count = src[:, NT - 1, :]
                chain(ve.tensor_tensor(total[:], src[:], total[:], ALU.subtract))
                chain(ve.tensor_tensor(total[:], bank[1][:, 0:NT * E].rearrange("p (t e) -> p t e", e=E), total[:], ALU.add))
                chain(ve.tensor_tensor(total[:], total[:], over(iota[:, E:2 * E]), ALU.add))
                for k in range(KE):
                    chain(ve.tensor_tensor(work[:], total[:], hot[k][:], ALU.mult))
                    chain(ve.reduce_sum(slot[:, :, k], work[:], AX_X))
                ve.tensor_copy(slot_i[:], slot[:]).then_inc(slots_ready, 1)
                chain(ve.tensor_scalar(ntile[:], count, float(P - 1), None, ALU.add))
                chain(ve.tensor_copy(cnt_i[:], ntile[:]))
                chain(ve.tensor_scalar(cnt_i[:], cnt_i[:], 7, None, ALU.arith_shift_right))
                chain(ve.tensor_copy(ntile[:], cnt_i[:]))
                chain(ve.memset(tb[:, 0:1], 0.0))
                for e in range(1, E):
                    chain(ve.tensor_tensor(tb[:, e:e + 1], tb[:, e - 1:e], ntile[:, e - 1:e], ALU.add))
                chain(ve.tensor_scalar(jump[:], ntile[:], float(-P), float(RT), ALU.mult, ALU.add))
                chain(ve.memset(e_f[:], 0.0))
                it = iota[:, 2 * E:]
                chain(ve.tensor_scalar(off_f[:], it, float(P), None, ALU.mult))
                for e in range(1, E):
                    chain(ve.scalar_tensor_tensor(out=e_f[:], in0=it, scalar=tb[:, e:e + 1], in1=e_f[:], op0=ALU.is_ge, op1=ALU.add))
                    chain(ve.tensor_scalar(tmp_f[:], it, tb[:, e:e + 1], jump[:, e - 1:e], ALU.is_ge, ALU.mult))
                    chain(ve.tensor_tensor(off_f[:], off_f[:], tmp_f[:], ALU.add))
                chain(ve.tensor_scalar(R["tile_e"][:], e_f[:], float(WE), None, ALU.mult))
                chain(ve.tensor_copy(R["tile_off"][:], off_f[:]))
                for n in range(4, len(parts)):
                    split_lo(n)
                dve.wait_ge(w_lo, len(parts))


def experts(nc, R, table_d, xn2_d, pair_d, T):
    NTL = tiles_of(T)
    RT = region(T)
    with ExitStack() as ctx:
        def sb(name, shape, dt=F32):
            return ctx.enter_context(nc.sbuf_tensor("e_" + name, shape, dt))

        def sem(name):
            return ctx.enter_context(nc.semaphore("e_" + name))

        pair = sb("pair", [P, U, 4], I32)
        xg = sb("xg", [P, 4, 512], F16)
        x_t = sb("x_t", [P, 2, 512], F16)
        sg = sb("sg", [P, 2, F])
        h = sb("h", [P, 2, F])
        h_s = sb("h_s", [P, 2, 2, F], F16)
        h_t = sb("h_t", [P, 2, 2, F], F16)
        yw = sb("yw", [P, 4, 256])
        ident16 = sb("ident16", [P, P], F16)
        ps_x = ctx.enter_context(nc.psum_tensor("ps_x", [P, 2, 512], F16))
        ps_h = ctx.enter_context(nc.psum_tensor("ps_h", [P, 2 * F], F16))
        ps_g = [ctx.enter_context(nc.psum_tensor(f"ps_g{i}", [P, 512], F32)) for i in range(2)]
        ps_u = [ctx.enter_context(nc.psum_tensor(f"ps_u{i}", [P, 512], F32)) for i in range(2)]
        ps_y = [ctx.enter_context(nc.psum_tensor(f"ps_y{i}", [P, 512], F32)) for i in range(2)]

        pair_in = [sem(f"pair_in{k}") for k in range(U)]
        x_in, stored = [sem(f"x_in{k}") for k in range(4)], [sem(f"stored{k}") for k in range(4)]
        xt_full, xt_free = sem("xt_full"), sem("xt_free")
        g_full, u_full, sg_done, h_done = sem("g_full"), sem("u_full"), sem("sg_done"), sem("h_done")
        passed, ident_done = sem("passed"), sem("ident_done")
        h_hi, h_lo, ht_full, ht_done = sem("h_hi"), sem("h_lo"), sem("ht_full"), sem("ht_done")
        y_full, yw_done = sem("y_full"), sem("yw_done")

        def wait(eng, s, value):
            if not (isinstance(value, int) and value <= 0):
                eng.wait_ge(s, value)

        def steps(eng, body):
            for k in range(U):
                body(k, k, 0)
            with eng.Fori(1, NTL // U - 1) as o:
                for k in range(U):
                    body(o * U + k, k, o)
            for k in range(U):
                body(NTL - U + k, k, NTL // U - 1)

        def no(i, past):
            return isinstance(i, int) and not 0 <= past < NTL

        with nc.Block() as block:
            @block.sync
            def _(sp):
                def body(i, k, o):
                    off = sp.value_load(R["tile_off"][0:1, bass.ds(i, 1)], min_val=0, max_val=E * RT - P)
                    wait(sp, stored[k % 4], 16 * (2 * o + k // 4 - 1))
                    sp.dma_start(pair[:, k, :], table_d[bass.ds(off, P), :]).then_inc(pair_in[k], 16)
                steps(sp, body)

            @block.gpsimd
            def _(pool):
                def gather(i, k, o):
                    pool.wait_ge(pair_in[k], 16 * (o + 1))
                    wait(pool, xt_full, i - 3)
                    carry(pool, passed)
                    pool.indirect_dma_start(xg[:, k % 4, :], None, xn2_d,
                                            bass.IndirectOffsetOnAxis(ap=pair[:, k, 0:1], axis=0)).then_inc(x_in[k % 4], 16)

                def body(o):
                    i = o * U
                    for k in range(U):
                        if not no(i, i + k + 3 if isinstance(i, int) else 0):
                            gather(i + k + 3, (k + 3) % U, o + (k + 3) // U)
                        pool.wait_ge(yw_done, i + k + 1)
                        carry(pool, passed)
                        pool.indirect_dma_start(pair_d, bass.IndirectOffsetOnAxis(ap=pair[:, k, 2:3], axis=0),
                                                yw[:, k % 4, :], None).then_inc(stored[k % 4], 16)
                for k in range(3):
                    gather(k, k, 0)
                body(0)
                with pool.Fori(1, NTL // U - 1) as o:
                    body(o)
                body(NTL // U - 1)
                for k in range(4):
                    pool.wait_ge(stored[k], 16 * NTL // 4)

            @block.tensor
            def _(pe):
                te = nc.tensor

                def x_turn(i, k, o):
                    pe.wait_ge(x_in[k], 16 * (o + 1))
                    wait(pe, xt_free, i)
                    for c in range(4):
                        last = te.transpose(ps_x[:, k % 2, c * P:(c + 1) * P], xg[:, k, c * P:(c + 1) * P], ident16[:])
                    last.then_inc(xt_full, 1)

                def weight(part, e, which, cols):
                    return R[part][:, bass.ds(e + (which * 1024 + cols.start), cols.stop - cols.start)]

                def project(i, k, e, which, ps, full, used):
                    wait(pe, used, i - 1)
                    out = ps[k % 2][:]
                    for c in range(2):
                        x_hi, x_lo = (x_t[:, k % 2, (2 * a + c) * P:(2 * a + c + 1) * P] for a in range(2))
                        cols = slice(c * F, (c + 1) * F)
                        te.matmul(out, x_hi, weight("hi", e, which, cols), start=(c == 0), stop=False)
                        te.matmul(out, x_lo, weight("hi", e, which, cols), start=False, stop=False)
                        last = te.matmul(out, x_hi, weight("lo", e, which, cols), start=False, stop=(c == 1))
                    last.then_inc(full, 1)

                def h_turn(i, k):
                    pe.wait_ge(h_lo, i + 1)
                    wait(pe, ht_done, i)
                    for a in range(2):
                        for c in range(4):
                            last = te.transpose(ps_h[:, a * F + c * P:a * F + (c + 1) * P], h_s[:, k % 2, a, c * P:(c + 1) * P], ident16[:])
                    last.then_inc(ht_full, 1)

                def down(i, k):
                    e = pe.value_load(R["tile_e"][0:1, bass.ds(i, 1)], min_val=0, max_val=(E - 1) * WE)
                    pe.wait_ge(ht_done, i + 1)
                    wait(pe, yw_done, i - 1)
                    out = ps_y[k % 2][:, 0:256]
                    for c in range(4):
                        hh_, hl_ = (h_t[:, k % 2, a, c * P:(c + 1) * P] for a in range(2))
                        cols = slice(c * 256, (c + 1) * 256)
                        te.matmul(out, hh_, weight("hi", e, 2, cols), start=(c == 0), stop=False)
                        te.matmul(out, hl_, weight("hi", e, 2, cols), start=False, stop=False)
                        last = te.matmul(out, hh_, weight("lo", e, 2, cols), start=False, stop=(c == 3))
                    last.then_inc(y_full, 1)

                def body(o):
                    i = o * UP
                    for k in range(UP):
                        past = not no(i, i + k - 1 if isinstance(i, int) else 0)
                        if not no(i, i + k + 1 if isinstance(i, int) else 0):
                            x_turn(i + k + 1, (k + 1) % UP, o + (k + 1) // UP)
                        e = pe.value_load(R["tile_e"][0:1, bass.ds(i + k, 1)], min_val=0, max_val=(E - 1) * WE)
                        pe.wait_ge(xt_free, i + k + 1)
                        project(i + k, k, e, 0, ps_g, g_full, sg_done)
                        if past:
                            h_turn(i + k - 1, (k - 1) % UP)
                        project(i + k, k, e, 1, ps_u, u_full, h_done)
                        if past:
                            down(i + k - 1, (k - 1) % UP)
                pe.wait_ge(ident_done, 1)
                x_turn(0, 0, 0)
                body(0)
                with pe.Fori(1, NTL // UP - 1) as o:
                    body(o)
                body(NTL // UP - 1)
                h_turn(NTL - 1, UP - 1)
                down(NTL - 1, UP - 1)

            @block.scalar
            def _(act):
                sc = nc.scalar

                def x_copy(i, k):
                    act.wait_ge(xt_full, i + 1)
                    wait(act, u_full, i - 1)
                    sc.activation(x_t[:, k % 2, :], ps_x[:, k % 2, :], ACT.Copy).then_inc(xt_free, 1)

                def weighted(i, k, o):
                    act.wait_ge(y_full, i + 1)
                    wait(act, stored[k % 4], 16 * (2 * o + k // 4))
                    sc.activation(yw[:, k % 4, :], ps_y[k % 2][:, 0:256], ACT.Copy,
                                  scale=pair[:, k, 1:2].bitcast(F32)).then_inc(yw_done, 1)

                def high(i, k):
                    act.wait_ge(h_done, i + 1)
                    wait(act, ht_full, i - 1)
                    sc.activation(h_s[:, k % 2, 0, :], h[:, k % 2, :], ACT.Copy).then_inc(h_hi, 1)

                def body(i, k, o):
                    if not no(i, i - 1 if isinstance(i, int) else 0):
                        high(i - 1, (k - 1) % U)
                    if not no(i, i - 2 if isinstance(i, int) else 0):
                        weighted(i - 2, (k - 2) % U, o if k >= 2 else o - 1)
                    if not no(i, i + 1 if isinstance(i, int) else 0):
                        x_copy(i + 1, (k + 1) % U)
                    act.wait_ge(g_full, i + 1)
                    wait(act, h_done, i - 1)
                    sc.activation(sg[:, k % 2, :], ps_g[k % 2][:], ACT.Silu, scale=R["g_scale"][:]).then_inc(sg_done, 1)
                x_copy(0, 0)
                steps(act, body)
                high(NTL - 1, U - 1)
                for k in (U - 2, U - 1):
                    weighted(NTL - U + k, k, NTL // U - 1)

            @block.vector
            def _(dve):
                ve = nc.vector
                ve.tensor_copy(ident16[:], R["ident"][:]).then_inc(ident_done, 1)

                def hidden(i, k):
                    dve.wait_ge(u_full, i + 1)
                    dve.wait_ge(sg_done, i + 1)
                    wait(dve, h_lo, i - 1)
                    ve.scalar_tensor_tensor(out=h[:, k % 2, :], in0=ps_u[k % 2][:], scalar=R["u_scale"][:], in1=sg[:, k % 2, :],
                                            op0=ALU.mult, op1=ALU.mult).then_inc(h_done, 1)
                    dve.wait_ge(h_hi, i + 1)
                    ve.tensor_tensor(h_s[:, k % 2, 1, :], h[:, k % 2, :], h_s[:, k % 2, 0, :], ALU.subtract).then_inc(h_lo, 1)
                    dve.wait_ge(ht_full, i + 1)
                    wait(dve, y_full, i - 1)
                    ve.tensor_copy(h_t[:, k % 2, :, :].rearrange("p a f -> p (a f)"), ps_h[:]).then_inc(ht_done, 1)

                steps(dve, lambda i, k, o: hidden(i, k))


def finish(nc, R, pair_d, x2_d, out, T):
    N, D = T // 512, 3
    with ExitStack() as ctx:
        def sb(name, shape, dt=F32):
            return ctx.enter_context(nc.sbuf_tensor("f_" + name, shape, dt))

        def sem(name):
            return ctx.enter_context(nc.semaphore("f_" + name))

        acc, xs = sb("acc", [P, D, KE, 4, 256]), sb("xs", [P, D, 4, 256])
        s, o = sb("s", [P, 2, 4, 256]), sb("o", [P, 2, 4, 256])
        raw, st, rs = sb("raw", [P, 2, 4, 6]), sb("st", [P, 2, 4, 2]), sb("rs", [P, 2, 4])
        nb = sb("nb", [P, 2, 4])
        acc_in, xs_in = [sem(f"acc_in{k}") for k in range(D)], [sem(f"xs_in{k}") for k in range(D)]
        out_done = [sem(f"out_done{k}") for k in range(2)]
        added, bn, agg, rstd, shift = sem("added"), sem("bn"), sem("agg"), sem("rstd"), sem("shift")
        normed, summed = sem("normed"), sem("summed")

        def rows(dram, i):
            return dram[i * 512:(i + 1) * 512, :].rearrange("(t p) h -> p t h", p=P)

        with nc.Block() as block:
            @block.sync
            def _(sp):
                for i in range(N):
                    if i >= D:
                        sp.wait_ge(added, i - D + 1)
                    for k in range(KE):
                        sp.dma_start(acc[:, i % D, k], rows(pair_d[k * T:(k + 1) * T, :], i)).then_inc(acc_in[i % D], 16)
                    if i >= D:
                        sp.wait_ge(summed, i - D + 1)
                    sp.dma_start(xs[:, i % D], rows(x2_d, i)).then_inc(xs_in[i % D], 16)

            @block.gpsimd
            def _(pool):
                def rstd_of(i):
                    r_ = rs[:, i % 2, :]
                    pool.wait_ge(agg, 4 * (i + 1))
                    if i >= 2:
                        pool.wait_ge(normed, 4 * (i - 1))
                    nc.gpsimd.tensor_scalar(r_, st[:, i % 2, :, 1], R["y_scale2"][:], EPS, ALU.mult, ALU.add).then_inc(rstd, 1)
                    pool.wait_ge(rstd, 3 * i + 1)
                    nc.gpsimd.tensor_tensor(r_, r_, R["neg_half"][:], ALU.pow).then_inc(rstd, 1)
                    pool.wait_ge(rstd, 3 * i + 2)
                    nc.gpsimd.tensor_scalar(r_, r_, R["y_scale"][:], None, ALU.mult).then_inc(rstd, 1)

                def total(i):
                    pool.wait_ge(normed, 4 * (i + 1))
                    pool.wait_ge(xs_in[i % D], 16 * (i // D + 1))
                    if i >= 2:
                        pool.wait_ge(out_done[i % 2], 16 * (i // 2))
                    nc.gpsimd.tensor_tensor(o[:, i % 2], s[:, i % 2], xs[:, i % D], ALU.add).then_inc(summed, 1)

                for i in range(N):
                    rstd_of(i)
                    if i >= 1:
                        total(i - 1)
                total(N - 1)

            @block.vector
            def _(dve):
                def shifts(i):
                    dve.wait_ge(rstd, 3 * (i + 1))
                    nc.vector.scalar_tensor_tensor(out=nb[:, i % 2, :], in0=st[:, i % 2, :, 0], scalar=-1.0, in1=rs[:, i % 2, :],
                                                   op0=ALU.mult, op1=ALU.mult).then_inc(shift, 1)

                for i in range(N):
                    dve.wait_ge(acc_in[i % D], 16 * KE * (i // D + 1))
                    if i >= 2:
                        dve.wait_ge(summed, i - 1)
                    nc.vector.tensor_tensor(s[:, i % 2], acc[:, i % D, 0], acc[:, i % D, 1], ALU.add).then_inc(added, 1)
                    dve.wait_ge(added, i + 1)
                    for t in range(4):
                        nc.vector.bn_stats(raw[:, i % 2, t, :], s[:, i % 2, t, :]).then_inc(bn, 1)
                    for t in range(4):
                        dve.wait_ge(bn, 4 * i + t + 1)
                        nc.vector.bn_aggr(st[:, i % 2, t, :], raw[:, i % 2, t, :]).then_inc(agg, 1)
                    if i >= 1:
                        shifts(i - 1)
                shifts(N - 1)

            @block.scalar
            def _(act):
                def store(i):
                    act.wait_ge(summed, i + 1)
                    act.dma_start(rows(out, i), o[:, i % 2]).then_inc(out_done[i % 2], 16)

                for i in range(N):
                    act.wait_ge(shift, i + 1)
                    for t in range(4):
                        nc.scalar.activation(s[:, i % 2, t, :], s[:, i % 2, t, :], ACT.Identity,
                                             bias=nb[:, i % 2, t:t + 1], scale=rs[:, i % 2, t:t + 1]).then_inc(normed, 1)
                    if i >= 1:
                        store(i - 1)
                store(N - 1)
                for k in range(2):
                    act.wait_ge(out_done[k], 16 * len(range(k, N, 2)))


def build(nc, x, gamma, beta, w_qkv, b_qkv, w_out, b_out, router, w_gate, w_up, w_down, out):
    B, S, H = x.shape
    T = B * S
    RT = region(T)

    def dram(name, shape, dt=F32):
        return nc.dram_tensor(name, shape, dt).ap()

    y_d, x2_d = dram("y_d", [T, H]), dram("x2_d", [T, H])
    xn2_d = dram("xn2_d", [T + P, 2 * H], F16)
    pair_d = dram("pair_d", [KE * T + E * 512, H])
    lg_d = dram("lg_d", [E, T])
    qk_d, mt_d = dram("qk_d", [4, H, S]), dram("mt_d", [2, HG * S])
    table_d = dram("table_d", [E * RT, 4], I32)

    with ExitStack() as outer:
        def sb(name, shape, dt=F32):
            return outer.enter_context(nc.sbuf_tensor(name, shape, dt))
        ident, neg_half = sb("ident", [P, P]), sb("neg_half", [P, 4])
        w_max = sb("w_max", [P, 12])
        w_src = [[w[e].rearrange("(c p) f -> p c f", p=P) for e in range(E)] for w in (w_gate, w_up, w_down)]
        cleared = outer.enter_context(nc.semaphore("cleared"))
        with ExitStack() as ctx:
            W = shared(nc, ctx)
            W["ident"], W["neg_half"] = ident, neg_half
            prepare_weights(nc, W, w_qkv, b_qkv, w_out, b_out, gamma, beta, xn2_d, table_d, cleared)
            attention(nc, W, x, y_d, x2_d, xn2_d, lg_d, qk_d, mt_d, router, w_src, w_max)
        with ExitStack() as ctx:
            def sc(name, shape, dt=F32):
                return ctx.enter_context(nc.sbuf_tensor(name, shape, dt))
            R = {"ident": ident, "neg_half": neg_half, "w_max": w_max,
                 "w_scale": sc("w_scale", [P, 3]), "g_scale": sc("g_scale", [P, 1]), "u_scale": sc("u_scale", [P, 1]),
                 "y_scale": sc("y_scale", [P, 1]), "y_scale2": sc("y_scale2", [P, 1]),
                 "hi": sc("we_hi", [P, E * WE], F16), "lo": sc("we_lo", [P, E * WE], F16),
                 "tile_e": sc("tile_e", [P, tiles_of(T)], I32), "tile_off": sc("tile_off", [P, tiles_of(T)], I32)}
            with ExitStack() as inner:
                raw = inner.enter_context(nc.sbuf_tensor("we_raw", [P, 3, 1024], F32))
                route(nc, R, lg_d, table_d, T, (w_src, raw), (cleared, clears(T) * 16))
            experts(nc, R, table_d, xn2_d, pair_d, T)
            finish(nc, R, pair_d, x2_d, out, T)


_INS = ["hidden_states", "ln_gamma", "ln_beta", "W_qkv", "b_qkv", "W_out", "b_out"]
_NAMES = ["L0_attn_" + n for n in _INS] + ["L0_ffn_router_kernel_DE", "L0_ffn_kernel_gating_EDF",
                                          "L0_ffn_kernel_up_EDF", "L0_ffn_kernel_down_EFD"]


def kernel(**inputs):
    import numpy as _np
    import concourse.bacc as _bacc
    from concourse import mybir as _mybir
    from concourse.bass_utils import run_bass_kernel_spmd as _run

    nc = _bacc.Bacc("TRN2", target_bir_lowering=False, num_devices=1)
    arrays, args = {}, []
    for name in _NAMES:
        a = _np.ascontiguousarray(inputs[name])
        arrays[f"in_{name}"] = a
        args.append(nc.dram_tensor(f"in_{name}", a.shape, _mybir.dt.from_np(a.dtype), kind="ExternalInput").ap())
    x = args[0]
    out = nc.dram_tensor("out", [x.shape[0] * x.shape[1], x.shape[2]], _mybir.dt.float32, kind="ExternalOutput").ap()
    x, gamma, beta, w_qkv, b_qkv, w_out, b_out, router, w_gate, w_up, w_down = args
    build(nc, x, gamma, beta, w_qkv, b_qkv, w_out, b_out, router, w_gate, w_up, w_down, out)
    r = _run(nc, [arrays], core_ids=[0])
    return r.results[0]["out"].reshape(inputs[_NAMES[0]].shape)
```

```python
from contextlib import ExitStack

import concourse.bass as bass
from concourse import mybir

F32 = mybir.dt.float32
F32R = mybir.dt.float32r
F16 = mybir.dt.float16
I32 = mybir.dt.int32
ALU = mybir.AluOpType
ACT = mybir.ActivationFunctionType
AX_X = mybir.AxisListType.X

P = 128
NH = 16
HD = 16
EPS = 1e-5
G = 4
HG = NH // G
VW = 32
KR = 96
KM = KR + 2


def split3(pe, out, stat_hi, stat_lo, mov_hi, mov_lo):
    n = len(stat_hi)
    for c in range(n):
        pe.matmul(out, stat_hi[c], mov_hi[c], start=(c == 0), stop=False)
        pe.matmul(out, stat_hi[c], mov_lo[c], start=False, stop=False)
        last = pe.matmul(out, stat_lo[c], mov_hi[c], start=False, stop=(c == n - 1))
    return last


def carry(eng, passed):
    eng.sem_inc(passed, 1)


def clears(T):
    return 1 + -(-(E * region(T) // P) // (5 * P))


def prepare_weights(nc, W, x, w_qkv, b_qkv, w_out, b_out, gamma, beta, xn2_d, table_d, cleared):
    with ExitStack() as ctx:
        def sb(name, shape, dt=F32):
            return ctx.enter_context(nc.sbuf_tensor(name, shape, dt))

        def sem(name):
            return ctx.enter_context(nc.semaphore(name))

        wq_in = sb("wq_in", [P, 6, 256])
        wo_in = sb("wo_in", [P, 2, 256])
        wo_t = sb("wo_t", [P, 2, 256])
        beta_rows = sb("beta_rows", [P, 256])
        bo_rows = sb("bo_rows", [P, 256])
        gamma_col = sb("gamma_col", [P, 2])
        bq_col = sb("bq_col", [P, 6])
        wbeta = sb("wbeta", [P, 6, 256])
        wb_col = sb("wb_col", [P, 6])
        bv_wide = sb("bv_wide", [P, 2, P])
        bank = [ctx.enter_context(nc.psum_tensor(f"prep_bank{i}", [P, 512], F32)) for i in range(2)]
        loaded = sem("w_loaded")
        ident0 = sem("w_ident0")
        ident_ready = sem("w_ident_ready")
        turned = sem("w_turned")
        hi_done = sem("w_hi_done")
        raw_done = sem("w_raw_done")
        lo_done = sem("w_lo_done")
        bias_step = sem("w_bias_step")
        bo_ready = sem("w_bo_ready")
        bo_done = sem("w_bo_done")
        ones_done, stacks_set = sem("w_ones_done"), sem("w_stacks_set")

        T = xn2_d.shape[0] - P
        rows = table_d.shape[0] // P
        zeros = sb("zeros", [P, 512], F16)
        filler = sb("filler", [P, 5, P, 4], I32)
        dest_base, dest_first = sb("dest_base", [P, 1], I32), sb("dest_first", [P, 1])
        iota_i = sb("iota_i", [P, 32], I32)
        router_const = sem("w_router_const")
        zeros_ready, filler_step = sem("w_zeros"), sem("w_filler")
        jobs = [("q", o, c) for c in range(2) for o in (range(4), range(4, 6))] + [("o", range(2), c) for c in range(2)]
        with nc.Block() as block:
            @block.sync
            def _(sp):
                sp.dma_start(W["xa"][:], x[0].rearrange("(t p) h -> p t h", p=P)).then_inc(W["x_first"], 16)
                with nc.allow_non_contiguous_dma(reason="bias and gamma columns, once"):
                    sp.dma_start(wq_in[:], w_qkv.rearrange("(t p) h -> p t h", p=P)).then_inc(loaded, 16)
                    sp.dma_start(wo_in[:], w_out.rearrange("(t p) h -> p t h", p=P)).then_inc(loaded, 16)
                    sp.dma_start(beta_rows[:], beta.unsqueeze(0).to_broadcast([P, 256])).then_inc(loaded, 16)
                    sp.dma_start(bo_rows[:], b_out.unsqueeze(0).to_broadcast([P, 256])).then_inc(loaded, 16)
                    sp.dma_start(gamma_col[:], gamma.rearrange("(c p) -> p c", p=P)).then_inc(loaded, 16)
                    sp.dma_start(bq_col[:], b_qkv.rearrange("(c p) -> p c", p=P)).then_inc(loaded, 16)

                sp.wait_ge(zeros_ready, 1)
                sp.dma_start(xn2_d[T:, :], zeros[:]).then_inc(cleared, 16)
                table = table_d.rearrange("(p r) c -> p (r c)", p=P)
                sp.wait_ge(filler_step, 13)
                for n in range(0, rows, 5 * P):
                    m = min(5 * P, rows - n)
                    sp.dma_start(table[:, 4 * n:4 * (n + m)], filler[:].rearrange("p a q c -> p (a q c)")[:, 0:4 * m]).then_inc(cleared, 16)
                sp.wait_ge(cleared, 16 * clears(T))

            @block.gpsimd
            def _(pool):
                nc.gpsimd.memset(filler[:], 0).then_inc(filler_step, 1)
                pool.wait_ge(filler_step, 1)
                for n in range(5):
                    nc.gpsimd.iota(filler[:, n, :, 0], pattern=[[1, P]], base=T, channel_multiplier=0).then_inc(filler_step, 1)
                    pool.wait_ge(filler_step, n + 2)
                nc.gpsimd.iota(filler[:, :, :, 2], pattern=[[P, 5], [1, P]], base=0, channel_multiplier=rows).then_inc(filler_step, 1)
                pool.wait_ge(filler_step, 7)
                nc.gpsimd.iota(dest_base[:], pattern=[[0, 1]], base=0, channel_multiplier=1).then_inc(filler_step, 1)
                pool.wait_ge(filler_step, 8)
                nc.gpsimd.memset(W["ident"][:], 0.0).then_inc(ident0, 1)
                pool.wait_ge(ident0, 1)
                nc.gpsimd.affine_select(out=W["ident"][:], in_=W["ident"][:], compare_op=ALU.not_equal, fill=1.0,
                                        base=0, pattern=[[-1, P]], channel_multiplier=1).then_inc(ident_ready, 1)
                n = 0

                def step(ins):
                    nonlocal n
                    n += 1
                    ins.then_inc(router_const, 1)
                    pool.wait_ge(router_const, n)
                step(nc.gpsimd.memset(W["before"][:], 1.0))
                step(nc.gpsimd.affine_select(out=W["before"][:], in_=W["before"][:], compare_op=ALU.is_gt, fill=0.0,
                                             base=0, pattern=[[1, P]], channel_multiplier=-1))
                step(nc.gpsimd.memset(W["ones"][:], 1.0))
                step(nc.gpsimd.memset(W["block"][:], 512.0))
                step(nc.gpsimd.memset(W["pay"][:], 0))
                step(nc.gpsimd.iota(iota_i[:, 0:32], pattern=[[0, 4], [-1, E]], base=E, channel_multiplier=0))
                step(nc.gpsimd.tensor_copy(W["first"][:].rearrange("p t e -> p (t e)"), iota_i[:, 0:32]))
                step(nc.gpsimd.iota(iota_i[:, 0:E], pattern=[[region(T), E]], base=0, channel_multiplier=0))
                step(nc.gpsimd.tensor_copy(W["place"][:], iota_i[:, 0:E]))
                for k in range(KE):
                    for c in range(2):
                        step(nc.gpsimd.iota(iota_i[:, 0:4], pattern=[[P, 4]], base=c * k * T - 512, channel_multiplier=1))
                        step(nc.gpsimd.tensor_copy(W["where"][:, :, k, c], iota_i[:, 0:4]))
                nc.gpsimd.memset(W["v_aug"][:], 0.0).then_inc(ones_done, 1)
                nc.gpsimd.memset(W["k_st"][0:KR].bitcast(F32), 0.0).then_inc(ones_done, 1)
                nc.gpsimd.memset(W["neg_half"][:], -0.5).then_inc(ones_done, 1)
                pool.wait_ge(ones_done, 3)
                nc.gpsimd.memset(W["v_aug"][:, :, :, HD:HD + 1], 1.0).then_inc(ones_done, 1)
                pool.wait_ge(ones_done, 4)

            @block.tensor
            def _(pe):
                pe.wait_ge(loaded, 96)
                pe.wait_ge(ident_ready, 1)
                for n, (kind, o, c) in enumerate(jobs):
                    if n >= 2:
                        pe.wait_ge(lo_done, n - 1)
                    src = wq_in if kind == "q" else wo_in
                    for m, tile in enumerate(o):
                        last = nc.tensor.transpose(bank[n % 2][:, m * P:(m + 1) * P], src[:, tile, c * P:(c + 1) * P], W["ident"][:])
                    last.then_inc(turned, 1)
                pe.wait_ge(bias_step, 4)
                pe.wait_ge(raw_done, 2)
                pe.wait_ge(lo_done, len(jobs))
                for c in range(2):
                    last = nc.tensor.matmul(bank[0][:, 0:256], bv_wide[:, c, :], wo_t[:, c, :], start=(c == 0), stop=(c == 1))
                last.then_inc(bo_ready, 1)

            @block.scalar
            def _(act):
                act.wait_ge(zeros_ready, 1)
                nc.scalar.activation(W["k_st"][KR:KM].rearrange("p g h n -> p (g h n)"), zeros[KR:KM, 0:1].to_broadcast([2, G * HG * 512]),
                                     ACT.Copy, bias=1.0).then_inc(stacks_set, 1)
                act.wait_ge(loaded, 96)
                for n, (kind, o, c) in enumerate(jobs):
                    act.wait_ge(turned, n + 1)
                    cols, got = slice(o[0] * P, (o[-1] + 1) * P), slice(0, len(o) * P)
                    if kind == "q":
                        nc.scalar.activation(W["wq_hi"][:, c, cols], bank[n % 2][:, got], ACT.Copy,
                                             scale=gamma_col[:, c:c + 1]).then_inc(hi_done, 1)
                    else:
                        nc.scalar.activation(wo_t[:, c, cols], bank[n % 2][:, got], ACT.Copy).then_inc(raw_done, 1)
                        nc.scalar.activation(W["wo_hi"][:, c, cols], bank[n % 2][:, got], ACT.Copy).then_inc(hi_done, 1)

            @block.vector
            def _(dve):
                nc.vector.memset(zeros[:], 0.0).then_inc(zeros_ready, 1)
                nc.vector.memset(W["q_st"][0:KR].bitcast(F32), 0.0).then_inc(stacks_set, 1)
                dve.wait_ge(filler_step, 8)
                nc.vector.tensor_scalar(filler[:, :, :, 2], filler[:, :, :, 2], 511, None, ALU.bitwise_and).then_inc(filler_step, 1)
                nc.vector.tensor_scalar(dest_base[:], dest_base[:], 4, None, ALU.arith_shift_right).then_inc(filler_step, 1)
                dve.wait_ge(filler_step, 10)
                nc.vector.tensor_copy(dest_first[:], dest_base[:]).then_inc(filler_step, 1)
                dve.wait_ge(filler_step, 11)
                nc.vector.tensor_scalar(dest_first[:], dest_first[:], 512.0, float(KE * T), ALU.mult, ALU.add).then_inc(filler_step, 1)
                dve.wait_ge(filler_step, 12)
                nc.vector.tensor_scalar(filler[:, :, :, 2], filler[:, :, :, 2], dest_first[:], None, ALU.add).then_inc(filler_step, 1)
                dve.wait_ge(loaded, 96)
                nc.vector.tensor_tensor(wbeta[:], wq_in[:], beta_rows[:].unsqueeze(1).to_broadcast([P, 6, 256]), ALU.mult).then_inc(bias_step, 1)
                dve.wait_ge(bias_step, 1)
                nc.vector.reduce_sum(wb_col[:], wbeta[:], AX_X).then_inc(bias_step, 1)
                dve.wait_ge(bias_step, 2)
                nc.vector.tensor_tensor(W["b_col"][:], wb_col[:], bq_col[:], ALU.add).then_inc(bias_step, 1)
                dve.wait_ge(bias_step, 3)
                nc.vector.tensor_copy(bv_wide[:], W["b_col"][:, 4:6].unsqueeze(2).to_broadcast([P, 2, P])).then_inc(bias_step, 1)
                for n, (kind, o, c) in enumerate(jobs):
                    dve.wait_ge(hi_done, n + 1)
                    cols, got = slice(o[0] * P, (o[-1] + 1) * P), slice(0, len(o) * P)
                    if kind == "q":
                        nc.vector.scalar_tensor_tensor(out=W["wq_lo"][:, c, cols], in0=bank[n % 2][:, got],
                                                       scalar=gamma_col[:, c:c + 1], in1=W["wq_hi"][:, c, cols].bitcast(F32),
                                                       op0=ALU.mult, op1=ALU.subtract).then_inc(lo_done, 1)
                    else:
                        nc.vector.tensor_tensor(W["wo_lo"][:, c, cols], bank[n % 2][:, got],
                                                W["wo_hi"][:, c, cols].bitcast(F32), ALU.subtract).then_inc(lo_done, 1)
                dve.wait_ge(bo_ready, 1)
                nc.vector.tensor_tensor(W["bo"][:], bank[0][:, 0:256], bo_rows[:], ALU.add).then_inc(bo_done, 1)
                dve.wait_ge(bo_done, 1)


USES = [
    (0, "mt", 1, 0), (0, "v", 1, 0),
    (1, "cx", 3, -1), (1, "zt", 0, 1),
    (2, "zt", 1, 1),
    (3, "qk", 0, 1), (3, "cn", 0, -1),
    (4, "mt", 2, 0), (4, "qk", 1, 1), (4, "cn", 1, -1),
    (5, "cx", 0, 0), (5, "xt", 0, -2),
    (6, "out", 0, -1),
    (7, "out", 1, -1),
    (8, "mt", 3, 0), (8, "xt", 1, -2),
    (9, "cx", 1, 0),
    (10, "qk", 2, 1),
    (11, "qk", 3, 1),
    (12, "mt", 0, 1), (12, "lg", 0, -2),
    (13, "cx", 2, 0), (13, "ct", 0, -3),
    (14, "v", 0, 1),
]
PER = {"mt": 4, "v": 2, "cx": 4, "zt": 2, "cn": 2, "qk": 4, "xt": 2, "out": 2, "lg": 1, "ct": 1}
RS = 19
RP = 19
NB = 3
BY_TILE = ("stats1", "stats3", "stats4", "y", "lna", "xn2")
SPREAD = ("stats1", "stats3", "lna")
CONTEXT_AT = 1
TURN = {"pe": (3, 3, 3), "act": (1, 1, 1), "dve": (1, 2, 3)}


def turn_of(engine, kind, n):
    return 0 if kind == "ctx" else TURN[engine][n]


BANK = {(kind, i): n % NB for n, (_, kind, i, _) in enumerate(USES)}


def attention(nc, W, x, y_d, x2_d, xn2_d, table_d, qk_d, mt_d, router, w_src, w_max, cleared):
    B = x.shape[0]
    with ExitStack() as ctx:
        def sb(name, shape, dt=F32):
            return ctx.enter_context(nc.sbuf_tensor("a_" + name, shape, dt))

        def sem(name):
            return ctx.enter_context(nc.semaphore("a_" + name))

        v_aug, q_st, k_st, ident = W["v_aug"], W["q_st"], W["k_st"], W["ident"]
        xa = W["xa"]
        y = sb("y", [P, 4, 256])
        z = sb("z", [P, 4, 256])
        z_hi = sb("z_hi", [P, 2, 512], F32R)
        z_lo = sb("z_lo", [P, 2, 512], F32R)
        qk_hi = sb("qk_hi", [P, 4, 512], F32R)
        qk_lo = sb("qk_lo", [P, 4, 512], F32R)
        probs = sb("probs", [P, 2, HG, 512])
        mx = sb("mx", [P, 2, 16])
        mt = sb("mt", [16, 2, 2, P], F32R)
        ctx_t = sb("ctx_t", [P, 2, 512])
        rsum = sb("rsum", [P, 16])
        cn = sb("cn", [P, 4, 256])
        c_hi = sb("c_hi", [P, 2, 512], F32R)
        c_lo = sb("c_lo", [P, 2, 512], F32R)
        xp = sb("xp", [P, 4, 256])
        yp = sb("yp", [P, 4, 256])
        a = sb("a", [P, 4, 256])
        x2 = sb("x2", [P, 4, 256])
        xn2 = sb("xn2", [P, 4, 256])
        xn_s = sb("xn_s", [P, 4, 2, 256], F16)
        w_raw = sb("w_raw", [P, 2, 2048])
        x_t = sb("x_t", [P, 2, 512])
        pick = sb("pick", [P, 4, E])
        lgs, work, prob, both = (sb(n, [P, 4, E]) for n in ("lgs", "work", "prob", "both"))
        hot = [sb(f"hot{k}", [P, 4, E]) for k in range(KE)]
        rank, chosen = sb("rank", [P, 4, E]), sb("chosen", [P, 4, E])
        half, quarter = sb("half", [P, 4, 4]), sb("quarter", [P, 4, 2])
        top, total = sb("top", [P, 4]), sb("total", [P, 4])
        best = [sb(f"best{k}", [P, 4]) for k in range(KE)]
        less, exp_less = sb("less", [P, 4]), sb("exp_less", [P, 4])
        ct = sb("ct", [P, 2, 4, E])
        row = sb("row", [P, 4, KE])
        row_i = sb("row_i", [P, 4, KE], I32)
        wr = sb("wr", [P, 2, 8])
        st = {k: sb(f"st{k}", [P, 4, 2]) for k in (1, 3, 4)}
        bst = {k: sb(f"bst{k}", [P, 4, 6]) for k in (1, 3, 4)}
        rs = {k: sb(f"rs{k}", [P, 4]) for k in (1, 3, 4)}
        r2 = sb("r2", [P, 4])
        t2 = sb("t2", [P, 4])

        misc = [ctx.enter_context(nc.psum_tensor(f"misc{i}", [P, 512], F32)) for i in range(NB)]
        sm = [ctx.enter_context(nc.psum_tensor(f"sm{i}", [P, 512], F32)) for i in range(2)]
        stp = [ctx.enter_context(nc.psum_tensor(f"stp{i}", [P, 512], F32)) for i in range(2)]
        cacc = ctx.enter_context(nc.psum_tensor("cacc", [P, 512], F32))

        wr_in = sem("wr_in")
        sp_passed, pool_passed, dve_passed = sem("sp_passed"), sem("pool_passed"), sem("dve_passed")
        x_in, xp_in, yp_in = sem("x_in"), sem("xp_in"), sem("yp_in")
        y_out, x2_out, xn2_out, entered = sem("y_out"), sem("x2_out"), sem("xn2_out"), sem("entered")
        centred, routed, route_exp, ranked = sem("centred"), sem("routed"), sem("route_exp"), sem("ranked")
        qk_w = [sem(f"qk_w{c}") for c in range(2)]
        stack_in = [sem(f"stack_in{g}") for g in range(G)]
        mt_w = sem("mt_w")
        m_in = [sem(f"m_in{g}") for g in range(G)]
        full = {k: sem(f"{k}_full") for k in PER}
        zt_hi, qkh, cnh, mth = sem("zt_hi"), sem("qk_hi"), sem("cn_hi"), sem("mt_hi")
        free = {k: sem(f"{k}_free") for k in PER}
        sm_full = sem("sm_full")
        max_done = [sem(f"max_done{k}") for k in range(2)]
        st_full, exp_done = sem("st_full"), sem("exp_done")
        pv_done, ctx_full, ctx_evac = sem("pv_done"), sem("ctx_full"), sem("ctx_evac")
        bn = {k: sem(f"bn{k}") for k in (1, 3, 4)}
        agg = {k: sem(f"agg{k}") for k in (1, 3, 4)}
        rstd = {k: sem(f"rstd{k}") for k in (1, 3, 4)}
        y_done, z_done = sem("y_done"), sem("z_done")
        xn_hi, xn_lo = sem("xn_hi"), sem("xn_lo")
        w_in, w_red = [sem(f"w_in{k}") for k in range(2)], sem("w_red")
        recip = sem("recip")
        yp_done, lna_done, x2_done, xn2_done = sem("yp_done"), sem("lna_done"), sem("x2_done"), sem("xn2_done")

        def wait(eng, s, value):
            if not (isinstance(value, int) and value <= 0):
                eng.wait_ge(s, value)

        def there(b, lag):
            return not isinstance(b, int) or 0 <= b + lag < B

        def before(b, kind, i):
            at = [(k, j) for _, k, j, _ in USES].index((kind, i))
            for back in range(1, 4 * len(USES)):
                pos = at - back
                _, k, j, lag = USES[pos % len(USES)]
                it = b + pos // len(USES)
                if BANK[k, j] == BANK[kind, i] and there(it, lag):
                    return k, (it + lag) * PER[k] + j + 1
            return None

        w_loads = {(-2, 0): (0, 1), (-1, 4): (2, 3), (0, 7): (4, 5), (0, 12): (6, 7), (1, 5): (8, 9), (1, 12): (10, 11)}
        w_reduces = {(-1, 2): (0,), (-1, 4): (1,), (-1, 8): (2, 3), (0, 9): (4,), (0, 10): (5,), (0, 14): (6,),
                     (0, 15): (7,), (1, 7): (8,), (1, 8): (9,), (1, 14): (10,), (1, 15): (11,)}

        def iterations(eng, body):
            for b in range(-2, 4):
                body(b)
            if B > 6:
                with eng.Fori(4, B - 2) as b:
                    body(b)
            for b in range(max(B - 2, 4), B + 3):
                body(b)

        with nc.Block() as block:
            @block.sync
            def _(sp):
                sp.dma_start(wr[:], router.rearrange("(c p) e -> p c e", p=P)).then_inc(wr_in, 16)

                def write_qk(i, c):
                    wait(sp, free["qk"], 4 * i + 2 * c + 2)
                    carry(sp, sp_passed)
                    wait(sp, stack_in[2 * c], 96 * i)
                    wait(sp, stack_in[2 * c + 1], 96 * i)
                    for part, src in enumerate((qk_hi, qk_lo)):
                        for k in range(2):
                            sp.dma_start(qk_d[2 * k + part, c * P:(c + 1) * P, :], src[:, 2 * c + k, :].bitcast(F32)).then_inc(qk_w[c], 16)

                def stack(i, g, old):
                    c = g // 2
                    wait(sp, qk_w[c], 64 * (i + 1))
                    carry(sp, sp_passed)
                    wait(sp, st_full, old)
                    for st_, parts in ((q_st, (0, 0, 1)), (k_st, (2, 3, 2))):
                        for r, part in enumerate(parts):
                            src = qk_d[part, g * 64:(g + 1) * 64, :].rearrange("(h d) n -> d h n", d=HD)
                            sp.dma_start(st_[r * HD:(r + 1) * HD, g, :, :].bitcast(F32), src).then_inc(stack_in[g], 16)

                def max_rows(i, g, n):
                    wait(sp, free["mt"], n + 1)
                    wait(sp, m_in[(g - 1) % 4], 16 * (i + (g > 0)))
                    sp.dma_start(mt_d.rearrange("r (k n) -> k r n", n=P), mt[:, g % 2, :, :].bitcast(F32)).then_inc(mt_w, 16)
                    wait(sp, mt_w, 16 * (n + 1))
                    sp.dma_start(q_st[KR:KM, g, :, :].rearrange("r h n -> r (h n)").bitcast(F32), mt_d).then_inc(m_in[g], 16)

                def body(b):
                    n = 4 * b
                    if there(b, 0):
                        max_rows(b, 1, n + 1)
                        stack(b, 3, 64 * b)
                        max_rows(b, 2, n + 2)
                    if there(b, 1):
                        write_qk(b + 1, 0)
                        stack(b + 1, 0, 16 * (n + 1))
                        stack(b + 1, 1, 16 * (n + 2))
                    if there(b, 0):
                        max_rows(b, 3, n + 3)
                    if there(b, 1):
                        write_qk(b + 1, 1)
                        stack(b + 1, 2, 16 * (n + 3))
                        max_rows(b + 1, 0, n + 4)
                iterations(sp, body)

            @block.gpsimd
            def _(pool):
                def rsqrt(k, i, steps, first, src, dst):
                    carry(pool, pool_passed)
                    nc.gpsimd.tensor_scalar(dst, src, EPS, None, ALU.add).then_inc(rstd[k], 1)
                    wait(pool, rstd[k], steps * i + first + 1)
                    nc.gpsimd.tensor_tensor(dst, dst, W["neg_half"][:, 0:4], ALU.pow).then_inc(rstd[k], 1)
                    wait(pool, rstd[k], steps * i + first + 2)

                def rows(dram, i):
                    return dram[bass.ts(i, 512), :].rearrange("(t p) h -> p t h", p=P)

                number = [0]

                def step(i, out, a, b=None, op=None):
                    number[0] += 1
                    ins = nc.gpsimd.tensor_copy(out, a) if op is None else nc.gpsimd.tensor_tensor(out, a, b, op)
                    ins.then_inc(ranked, 1)
                    wait(pool, ranked, RP * i + number[0])

                def enter(i):
                    number[0] = 0
                    pay = W["pay"]
                    wait(pool, routed, RS * (i + 1))
                    wait(pool, free["ct"], i + 1)
                    wait(pool, entered, 128 * i)
                    for t in range(4):
                        step(i, rank[:, t, :], ct[:, 0, t, :], W["place"][:], ALU.add)
                        step(i, W["place"][:], W["place"][:], ct[:, 1, t, :], ALU.add)
                    for k in range(KE):
                        step(i, chosen[:], rank[:], hot[k][:], ALU.mult)
                        step(i, half[:], chosen[:, :, 0:4], chosen[:, :, 4:8], ALU.add)
                        step(i, quarter[:], half[:, :, 0:2], half[:, :, 2:4], ALU.add)
                        step(i, row[:, :, k], quarter[:, :, 0], quarter[:, :, 1], ALU.add)
                    step(i, W["where"][:], W["where"][:], W["block"][:], ALU.add)
                    carry(pool, pool_passed)
                    step(i, row_i[:], row[:])
                    carry(pool, pool_passed)
                    step(i, pay[:, :, :, 0:4:2], W["where"][:])
                    carry(pool, pool_passed)
                    for t in range(4):
                        for k in range(KE):
                            pool.indirect_dma_start(table_d, bass.IndirectOffsetOnAxis(ap=row_i[:, t, k:k + 1], axis=0),
                                                    pay[:, t, k, :], None).then_inc(entered, 16)

                def body(b):
                    if there(b, 2) and not (isinstance(b, int) and b == -2):
                        i = b + 2
                        wait(pool, y_done, 4 * i)
                        carry(pool, pool_passed)
                        pool.dma_start(xa[:], rows(x.rearrange("b s h -> (b s) h"), i)).then_inc(x_in, 16)
                    if there(b, -2):
                        i = b - 2
                        wait(pool, xn_lo, i + 1)
                        carry(pool, pool_passed)
                        pool.dma_start(rows(xn2_d, i), xn_s[:].rearrange("p t a h -> p t (a h)")).then_inc(xn2_out, 16)
                    if there(b, -1):
                        i = b - 1
                        wait(pool, x2_done, i)
                        carry(pool, pool_passed)
                        pool.dma_start(xp[:], rows(x.rearrange("b s h -> (b s) h"), i)).then_inc(xp_in, 16)
                        wait(pool, free["out"], 2 * i)
                        wait(pool, y_out, 16 * (i + 1))
                        carry(pool, pool_passed)
                        pool.dma_start(yp[:], rows(y_d, i)).then_inc(yp_in, 16)
                        wait(pool, yp_in, 16 * (i + 1))
                        nc.gpsimd.tensor_tensor(yp[:], yp[:], W["bo"][:].unsqueeze(1).to_broadcast([P, 4, 256]), ALU.add).then_inc(yp_done, 1)
                    if there(b, 2):
                        i = b + 2
                        wait(pool, agg[1], 4 * (i + 1))
                        rsqrt(1, i, 6, 0, st[1][:, :, 1], rs[1][:])
                        nc.gpsimd.tensor_tensor(t2[:], rs[1][:], rs[1][:], ALU.mult).then_inc(rstd[1], 1)
                        wait(pool, rstd[1], 6 * i + 3)
                        nc.gpsimd.tensor_tensor(t2[:], t2[:], st[1][:, :, 1], ALU.mult).then_inc(rstd[1], 1)
                        wait(pool, rstd[1], 6 * i + 4)
                        wait(pool, z_done, 4 * i)
                        rsqrt(1, i, 6, 4, t2[:], r2[:])
                    if there(b, -1):
                        i = b - 1
                        wait(pool, agg[3], 4 * (i + 1))
                        rsqrt(3, i, 2, 0, st[3][:, :, 1], rs[3][:])
                    if there(b, -1):
                        i = b - 1
                        wait(pool, lna_done, 4 * (i + 1))
                        wait(pool, xp_in, 16 * (i + 1))
                        wait(pool, x2_out, 16 * i)
                        wait(pool, xn2_done, 4 * i)
                        nc.gpsimd.tensor_tensor(x2[:], xp[:], a[:], ALU.add).then_inc(x2_done, 1)
                        wait(pool, agg[4], 4 * (i + 1))
                        rsqrt(4, i, 2, 0, st[4][:, :, 1], rs[4][:])
                        wait(pool, x2_done, i + 1)
                        carry(pool, pool_passed)
                        pool.dma_start(rows(x2_d, i), x2[:]).then_inc(x2_out, 16)
                    if there(b, 2):
                        i = b + 2
                        wait(pool, y_done, 4 * (i + 1))
                        carry(pool, pool_passed)
                        pool.dma_start(rows(y_d, i), y[:]).then_inc(y_out, 16)
                    if there(b, -3):
                        enter(b - 3)
                pool.wait_ge(cleared[0], cleared[1])
                iterations(pool, body)
                for s in (y_out, x2_out, xn2_out):
                    pool.wait_ge(s, 16 * B)
                pool.wait_ge(entered, 128 * B)

            @block.tensor
            def _(pe):
                te = nc.tensor

                def bank_for(b, kind, i):
                    prev = before(b, kind, i)
                    if prev is not None:
                        wait(pe, free[prev[0]], prev[1])
                    return misc[BANK[kind, i]]

                def turn(bank, src, c):
                    for t in range(4):
                        last = te.transpose(bank[:, t * P:(t + 1) * P], src[:, t, c * P:(c + 1) * P], ident[:])
                    return last

                def use(b, kind, i, d):
                    bank = bank_for(b, kind, i)
                    if kind == "zt":
                        wait(pe, z_done, 4 * (d + 1))
                        last = turn(bank, z, i)
                    elif kind == "qk":
                        wait(pe, free["zt"], 2 * (d + 1))
                        col = (i % 2) * 256 + (i // 2) * P
                        last = split3(te, bank[:], [W["wq_hi"][:, c, col:col + P] for c in range(2)],
                                      [W["wq_lo"][:, c, col:col + P] for c in range(2)],
                                      [z_hi[:, c, :] for c in range(2)], [z_lo[:, c, :] for c in range(2)])
                    elif kind == "v":
                        wait(pe, free["zt"], 2 * (d + 1))
                        for half in range(2):
                            tk = slice((2 * i + half) * P, (2 * i + half + 1) * P)
                            last = split3(te, bank[:, half * 256:(half + 1) * 256],
                                          [z_hi[:, c, tk] for c in range(2)], [z_lo[:, c, tk] for c in range(2)],
                                          [W["wq_hi"][:, c, 512:768] for c in range(2)],
                                          [W["wq_lo"][:, c, 512:768] for c in range(2)])
                    elif kind == "mt":
                        wait(pe, max_done[1], 8 * (4 * d + i + 1))
                        last = te.transpose(bank[0:16, 0:P], mx[:, i % 2, :], ident[:])
                    elif kind == "cx":
                        wait(pe, ctx_evac, 4 * d + i + 1)
                        for t in range(4):
                            last = te.transpose(bank[:, t * P:(t + 1) * P], ctx_t[:, i % 2, t * P:(t + 1) * P], ident[:])
                    elif kind == "cn":
                        wait(pe, free["cx"], 4 * (d + 1))
                        last = turn(bank, cn, i)
                    elif kind == "out":
                        wait(pe, free["cn"], 2 * (d + 1))
                        for half in range(2):
                            tk = slice((2 * i + half) * P, (2 * i + half + 1) * P)
                            last = split3(te, bank[:, half * 256:(half + 1) * 256],
                                          [c_hi[:, c, tk] for c in range(2)], [c_lo[:, c, tk] for c in range(2)],
                                          [W["wo_hi"][:, c, :] for c in range(2)], [W["wo_lo"][:, c, :] for c in range(2)])
                    elif kind == "xt":
                        wait(pe, xn2_done, 4 * (d + 1))
                        last = turn(bank, xn2, i)
                    elif kind == "lg":
                        wait(pe, free["xt"], 2 * (d + 1))
                        for t in range(4):
                            for c in range(2):
                                last = te.matmul(bank[:, t * E:(t + 1) * E], x_t[:, c, t * P:(t + 1) * P], wr[:, c, :],
                                                 start=(c == 0), stop=(c == 1))
                    else:
                        wait(pe, routed, RS * d + 16)
                        pairs = both[:].rearrange("p t e -> p (t e)")
                        te.matmul(bank[:, 0:32], W["before"][:], pairs, start=True, stop=True)
                        last = te.matmul(bank[:, 32:64], W["ones"][:], pairs, start=True, stop=True)
                    last.then_inc(full[kind], 1)

                def context_part(b, s):
                    lag = -1 if s == 0 else 0
                    if there(b, lag):
                        q = 16 * b + s - 1
                        gq, jq = (s - 1) % 16 // 4, (s - 1) % 4
                        wait(pe, exp_done, 4 * (q + 1))
                        if jq % 2 == 0:
                            wait(pe, free["v"], 2 * (b + lag) + jq // 2 + 1)
                        if jq == 0:
                            wait(pe, ctx_evac, 4 * b + gq)
                        for h in range(HG):
                            last = te.matmul(cacc[32 * h:32 * h + 32, :], v_aug[:, jq, HG * gq + h, :],
                                             probs[:, jq % 2, h, :], start=(jq == 0), stop=(jq == 3),
                                             skip_group_check=True)
                        last.then_inc(pv_done, 1)

                def beside(b, s, r):
                    uses = [u for u in USES if u[0] == s]
                    for n, (_, kind, i, lag) in enumerate(uses):
                        if r == turn_of("pe", kind, n) and there(b, lag):
                            use(b, kind, i, b + lag)

                def body(b):
                    for s in range(16):
                        g, j = s // 4, s % 4
                        da, ga = b + (g >= 2), (g + 2) % 4
                        for r in range(4):
                            if there(b, int(g >= 2)):
                                if j == 0 and r == 0:
                                    wait(pe, stack_in[ga], 96 * (da + 1))
                                wait(pe, max_done[r % 2], 32 * da + 8 * ga + 2 * j + r // 2)
                                te.matmul(sm[r % 2][:], q_st[0:KR, ga, j, r * P:(r + 1) * P], k_st[0:KR, ga, j, :],
                                          start=True, stop=True).then_inc(sm_full, 1)
                            if there(b, 0):
                                if j == 0 and r == 0:
                                    wait(pe, m_in[g], 16 * (b + 1))
                                wait(pe, exp_done, 64 * b + 4 * s + r - 1)
                                te.matmul(stp[r % 2][:], k_st[0:KM, g, r, j * P:(j + 1) * P], q_st[0:KM, g, r, :],
                                          start=True, stop=True).then_inc(st_full, 1)
                            if r == CONTEXT_AT:
                                context_part(b, s)
                            beside(b, s, r)
                pe.wait_ge(wr_in, 16)
                iterations(pe, body)

            @block.scalar
            def _(act):
                sc = nc.scalar

                def extra(b, kind, i, lag):
                    if not there(b, lag):
                        return
                    d = b + lag
                    bank = misc[BANK[kind, i]] if (kind, i) in BANK else None
                    if kind in PER:
                        wait(act, full[kind], PER[kind] * d + i + 1)
                    if kind == "zt":
                        wait(act, full["v"], 2 * d)
                        sc.activation(z_hi[:, i, :], bank[:], ACT.Copy).then_inc(zt_hi, 1)
                    elif kind == "qk":
                        wait(act, qk_w[i // 2], 64 * d)
                        sc.activation(qk_hi[:, i, :], bank[:], ACT.Identity,
                                      bias=W["b_col"][:, (i % 2) * 2 + i // 2:(i % 2) * 2 + i // 2 + 1]).then_inc(qkh, 1)
                    elif kind == "v":
                        wait(act, pv_done, 16 * d + (0 if i else -2))
                        sc.activation(v_aug[:, 2 * i:2 * i + 2, :, 0:HD],
                                      bank[:].rearrange("p (t h d) -> p t h d", t=2, h=NH), ACT.Copy).then_inc(free["v"], 1)
                    elif kind == "ctx":
                        n = 4 * d + i
                        wait(act, pv_done, 4 * (n + 1))
                        wait(act, full["cx"], n - 1)
                        sc.activation(ctx_t[:, i % 2, :], cacc[:], ACT.Copy).then_inc(ctx_evac, 1)
                    elif kind == "cn":
                        wait(act, full["out"], 2 * d)
                        sc.activation(c_hi[:, i, :], bank[:], ACT.Copy).then_inc(cnh, 1)
                    elif kind == "xt":
                        wait(act, full["lg"], d)
                        sc.activation(x_t[:, i, :], bank[:], ACT.Copy).then_inc(free["xt"], 1)
                    elif kind == "lg":
                        wait(act, centred, 2 * d)
                        sc.activation(lgs[:].rearrange("p t e -> p (t e)"), bank[:, 0:32], ACT.Copy).then_inc(free["lg"], 1)
                    elif kind == "probs":
                        wait(act, centred, 2 * (d + 1))
                        sc.activation(prob[:], work[:], ACT.Exp).then_inc(route_exp, 1)
                    elif kind == "less":
                        wait(act, routed, RS * d + 16)
                        sc.activation(exp_less[:], less[:], ACT.Exp).then_inc(route_exp, 1)
                    elif kind == "ct":
                        wait(act, ranked, RP * d)
                        sc.activation(ct[:].rearrange("p a t e -> p (a t e)"), bank[:, 0:64], ACT.Copy).then_inc(free["ct"], 1)
                    elif kind == "xn_hi":
                        wait(act, xn2_done, 4 * (d + 1))
                        wait(act, xn2_out, 16 * d)
                        sc.activation(xn_s[:, :, 0, :], xn2[:], ACT.Copy, scale=XS).then_inc(xn_hi, 1)
                    elif kind == "z":
                        wait(act, y_done, 4 * (d + 1))
                        wait(act, rstd[1], 6 * (d + 1))
                        wait(act, full["zt"], 2 * d)
                        for t in range(4):
                            sc.activation(z[:, t, :], y[:, t, :], ACT.Copy, scale=r2[:, t:t + 1]).then_inc(z_done, 1)

                def load_w(n):
                    if n >= 2:
                        act.wait_ge(w_red, n - 1)
                    for e in range(2):
                        act.dma_start(w_raw[:, n % 2, e * 1024:(e + 1) * 1024].rearrange("p (c f) -> p c f", c=2 if n < 8 else 4),
                                      w_src[n // 4][n % 4 * 2 + e]).then_inc(w_in[n % 2], 16)

                extras = {
                    0: [("v", 0, 0), ("probs", 0, -3)], 1: [("ctx", 3, -1), ("v", 1, 0)], 2: [("zt", 0, 1), ("xn_hi", 0, -2)],
                    3: [("zt", 1, 1)], 4: [("qk", 0, 1), ("cn", 0, -1)], 5: [("ctx", 0, 0), ("qk", 1, 1), ("cn", 1, -1)],
                    6: [("xt", 0, -2)], 9: [("ctx", 1, 0), ("xt", 1, -2)], 10: [("less", 0, -3)], 11: [("qk", 2, 1)],
                    12: [("qk", 3, 1)], 13: [("ctx", 2, 0), ("lg", 0, -2)], 14: [("ct", 0, -3), ("z", 0, 2)],
                }

                def body(b):
                    for s in range(16):
                        j = s % 4
                        if isinstance(b, int) and (b, s) in w_loads:
                            for n in w_loads[b, s]:
                                load_w(n)
                        for r in range(4):
                            if there(b, 0):
                                q = 16 * b + s
                                if r == 0:
                                    wait(act, pv_done, q - 1)
                                wait(act, st_full, 4 * q + r + 1)
                                sc.activation(probs[:, j % 2, r, :], stp[r % 2][:], ACT.Exp, scale=HD ** -0.5).then_inc(exp_done, 1)
                            for n, (kind, i, lag) in enumerate(extras.get(s, [])):
                                if r == turn_of("act", kind, n):
                                    extra(b, kind, i, lag)
                iterations(act, body)

            @block.vector
            def _(dve):
                ve = nc.vector

                def stats(k, src, i, t):
                    ve.bn_stats(bst[k][:, t, :], src[:, t, :]).then_inc(bn[k], 1)
                    if t == 3:
                        for u in range(4):
                            wait(dve, bn[k], 4 * i + u + 1)
                            carry(dve, dve_passed)
                            ve.bn_aggr(st[k][:, u, :], bst[k][:, u, :]).then_inc(agg[k], 1)

                def normal(k, dst, src, done, t):
                    ve.tensor_scalar(dst[:, t, :], src[:, t, :], st[k][:, t, 0:1], rs[k][:, t:t + 1],
                                     ALU.subtract, ALU.mult).then_inc(done, 1)

                def extra(b, kind, i, lag, t=0):
                    if not there(b, lag):
                        return
                    d = b + lag
                    bank = misc[BANK[kind, i]] if (kind, i) in BANK else None
                    n = 4 * d + i
                    if kind == "mt":
                        wait(dve, full["mt"], n + 1)
                        wait(dve, mt_w, 16 * (n - 1))
                        ve.tensor_scalar(mt[:, i % 2, 0, :], bank[0:16, 0:P], -1.0, None, ALU.mult).then_inc(mth, 1)
                        wait(dve, mth, n + 1)
                        ve.scalar_tensor_tensor(out=mt[:, i % 2, 1, :], in0=bank[0:16, 0:P], scalar=-1.0,
                                                in1=mt[:, i % 2, 0, :].bitcast(F32), op0=ALU.mult,
                                                op1=ALU.subtract).then_inc(free["mt"], 1)
                    elif kind == "cx":
                        wait(dve, full["cx"], n + 1)
                        wait(dve, full["cn"], 2 * d)
                        wait(dve, free["cx"], n)
                        v = bank[:].rearrange("p (t h d) -> p t h d", t=4, h=HG)
                        ve.reciprocal(rsum[:].rearrange("p (t h) -> p t h", t=4), v[:, :, :, HD]).then_inc(recip, 1)
                        wait(dve, recip, n + 1)
                        ve.tensor_tensor(cn[:, :, i * 64:(i + 1) * 64].rearrange("p t (h d) -> p t h d", h=HG),
                                         v[:, :, :, 0:HD],
                                         rsum[:].rearrange("p (t h) -> p t h", t=4).unsqueeze(3).to_broadcast([P, 4, HG, HD]),
                                         ALU.mult).then_inc(free["cx"], 1)
                    elif kind == "zt":
                        wait(dve, zt_hi, 2 * d + i + 1)
                        ve.tensor_tensor(z_lo[:, i, :], bank[:], z_hi[:, i, :].bitcast(F32), ALU.subtract).then_inc(free["zt"], 1)
                    elif kind == "cn":
                        wait(dve, cnh, 2 * d + i + 1)
                        ve.tensor_tensor(c_lo[:, i, :], bank[:], c_hi[:, i, :].bitcast(F32), ALU.subtract).then_inc(free["cn"], 1)
                    elif kind == "qk":
                        wait(dve, qkh, n + 1)
                        col = (i % 2) * 2 + i // 2
                        ve.scalar_tensor_tensor(out=qk_lo[:, i, :], in0=bank[:], scalar=W["b_col"][:, col:col + 1],
                                                in1=qk_hi[:, i, :].bitcast(F32), op0=ALU.add,
                                                op1=ALU.subtract).then_inc(free["qk"], 1)
                    elif kind == "out":
                        wait(dve, full["out"], 2 * d + i + 1)
                        wait(dve, yp_done, d + 1)
                        wait(dve, x2_done, d)
                        ve.tensor_tensor(a[:, 2 * i:2 * i + 2, :], bank[:].rearrange("p (t h) -> p t h", t=2),
                                         yp[:, 2 * i:2 * i + 2, :], ALU.add).then_inc(free["out"], 1)
                    elif kind == "stats3":
                        if t == 0:
                            wait(dve, free["out"], 2 * (d + 1))
                        stats(3, a, d, t)
                    elif kind == "lna":
                        if t == 0:
                            wait(dve, rstd[3], 2 * (d + 1))
                        normal(3, a, a, lna_done, t)
                    elif kind == "stats4":
                        if t == 0:
                            wait(dve, x2_done, d + 1)
                        stats(4, x2, d, t)
                    elif kind == "xn2":
                        if t == 0:
                            wait(dve, rstd[4], 2 * (d + 1))
                            wait(dve, full["xt"], 2 * d)
                            wait(dve, xn_lo, d)
                        normal(4, xn2, x2, xn2_done, t)
                    elif kind == "stats1":
                        if t == 0:
                            if isinstance(d, int) and d == 0:
                                dve.wait_ge(W["x_first"], 16)
                            wait(dve, x_in, 16 * d)
                            wait(dve, rstd[1], 6 * d)
                        stats(1, xa, d, t)
                    elif kind == "y":
                        if t == 0:
                            wait(dve, rstd[1], 6 * d + 2)
                            wait(dve, z_done, 4 * d)
                            wait(dve, y_out, 16 * d)
                        normal(1, y, xa, y_done, t)
                    elif kind == "xn_lo":
                        wait(dve, xn_hi, d + 1)
                        ve.scalar_tensor_tensor(out=xn_s[:, :, 1, :], in0=xn2[:], scalar=XS, in1=xn_s[:, :, 0, :],
                                                op0=ALU.mult, op1=ALU.subtract).then_inc(xn_lo, 1)

                def wide(v):
                    return v.unsqueeze(2).to_broadcast([P, 4, E])

                def route_step(n, d):
                    if n in (1, 3, 19):
                        wait(dve, *{1: (free["lg"], d + 1), 3: (route_exp, 2 * d + 1), 19: (route_exp, 2 * d + 2)}[n])
                    if n == 10:
                        wait(dve, ranked, RP * d)
                    if n == 20:
                        wait(dve, entered, 128 * d)
                    wait(dve, *((centred, 2 * d + n - 1) if n < 3 else (routed, RS * d + n - 3)))
                    carry(dve, dve_passed)
                    if n == 1:
                        ins = ve.reduce_max(top[:], lgs[:], AX_X)
                    elif n == 2:
                        ins = ve.tensor_tensor(work[:], lgs[:], wide(top[:]), ALU.subtract)
                    elif n == 3:
                        ins = ve.reduce_sum(total[:], prob[:], AX_X)
                    elif n == 4:
                        ins = ve.reciprocal(total[:], total[:])
                    elif n == 5:
                        ins = ve.tensor_tensor(prob[:], prob[:], wide(total[:]), ALU.mult)
                    elif n in (6, 12):
                        ins = ve.reduce_max(best[n // 12][:], prob[:], AX_X)
                    elif n in (7, 13):
                        ins = ve.tensor_tensor(pick[:], prob[:], wide(best[n // 12][:]), ALU.is_equal)
                    elif n in (8, 14):
                        ins = ve.tensor_tensor(pick[:], pick[:], W["first"][:], ALU.mult)
                    elif n in (9, 15):
                        ins = ve.reduce_max(total[:], pick[:], AX_X)
                    elif n in (10, 16):
                        ins = ve.tensor_tensor(hot[n // 12][:], pick[:], wide(total[:]), ALU.is_equal)
                    elif n == 11:
                        ins = ve.scalar_tensor_tensor(out=prob[:], in0=hot[0][:], scalar=-2.0, in1=prob[:], op0=ALU.mult, op1=ALU.add)
                    elif n == 17:
                        ins = ve.tensor_tensor(less[:], best[1][:], best[0][:], ALU.subtract)
                    elif n == 18:
                        ins = ve.tensor_tensor(both[:], hot[0][:], hot[1][:], ALU.add)
                    elif n == 19:
                        ins = ve.tensor_scalar(total[:], exp_less[:], 1.0, None, ALU.add)
                    elif n == 20:
                        ins = ve.reciprocal(W["pay"][:, :, 0, 1].bitcast(F32), total[:])
                    elif n == 21:
                        ins = ve.tensor_tensor(W["pay"][:, :, 1, 1].bitcast(F32), exp_less[:], W["pay"][:, :, 0, 1].bitcast(F32), ALU.mult)
                    ins.then_inc(centred if n < 3 else routed, 1)

                route_at = {(14, 2): (1, -2), (15, 2): (2, -2), (11, 3): (19, -3), (12, 3): (20, -3), (13, 3): (21, -3)}
                for n in range(16):
                    route_at[1 + n // 2, 2 * (n % 2)] = (3 + n, -3)

                extras = {
                    0: [("xn2", 0, -2)], 1: [("mt", 1, 0)], 2: [("cx", 3, -1), ("zt", 0, 1)],
                    3: [("zt", 1, 1), ("xn_lo", 0, -2)], 4: [("qk", 0, 1), ("cn", 0, -1)],
                    5: [("mt", 2, 0), ("qk", 1, 1), ("cn", 1, -1)], 6: [("cx", 0, 0)],
                    7: [("out", 0, -1), ("stats1", 0, 2)], 8: [("out", 1, -1)], 9: [("mt", 3, 0), ("stats3", 0, -1)],
                    10: [("cx", 1, 0)], 11: [("qk", 2, 1), ("lna", 0, -1)], 12: [("qk", 3, 1), ("y", 0, 2)],
                    13: [("mt", 0, 1), ("stats4", 0, -1)], 14: [("cx", 2, 0)],
                }

                def body(b):
                    for s in range(16):
                        g, j = s // 4, s % 4
                        da, ga = b + (g >= 2), (g + 2) % 4
                        if isinstance(b, int) and (b, s) in w_reduces:
                            for n in w_reduces[b, s]:
                                dve.wait_ge(w_in[n % 2], 32 * (n // 2 + 1))
                                ve.reduce_max(w_max[:, n:n + 1], w_raw[:, n % 2, :], AX_X, apply_absolute_value=True).then_inc(w_red, 1)
                        for r in range(4):
                            if there(b, int(g >= 2)):
                                if j == 0 and r == 0:
                                    wait(dve, full["mt"], 4 * da + ga - 1)
                                wait(dve, sm_full, 64 * da + 16 * ga + 4 * j + r + 1)
                                ve.reduce_max(mx[:, ga % 2, 4 * j + r:4 * j + r + 1], sm[r % 2][:], AX_X).then_inc(max_done[r % 2], 1)
                            for n, (kind, i, lag) in enumerate(extras.get(s, [])):
                                if kind in SPREAD:
                                    extra(b, kind, i, lag, r)
                                elif r == turn_of("dve", kind, n):
                                    for t in range(4 if kind in BY_TILE else 1):
                                        extra(b, kind, i, lag, t)
                            if (s, r) in route_at and there(b, route_at[s, r][1]):
                                route_step(route_at[s, r][0], b + route_at[s, r][1])
                iterations(dve, body)


def shared(nc, ctx):
    def sb(name, shape, dt=F32):
        return ctx.enter_context(nc.sbuf_tensor(name, shape, dt))
    return {
        "wq_hi": sb("wq_hi", [P, 2, 768], F32R), "wq_lo": sb("wq_lo", [P, 2, 768], F32R),
        "wo_hi": sb("wo_hi", [P, 2, 256], F32R), "wo_lo": sb("wo_lo", [P, 2, 256], F32R),
        "b_col": sb("b_col", [P, 6]), "bo": sb("bo", [P, 256]),
        "before": sb("before", [P, P]), "ones": sb("ones", [P, P]), "first": sb("first", [P, 4, E]),
        "block": sb("block", [P, 4, KE, 2]), "pay": sb("pay", [P, 4, KE, 4], I32), "where": sb("where", [P, 4, KE, 2]),
        "xa": sb("xa", [P, 4, 256]), "x_first": ctx.enter_context(nc.semaphore("x_first")),
        "v_aug": sb("v_aug", [P, 4, NH, VW]),
        "q_st": sb("q_st", [KM, G, HG, 512], F32R), "k_st": sb("k_st", [KM, G, HG, 512], F32R),
    }


E = 8
F = 512
KE = 2
WE = 3 * 1024
XS = 1024.0
U = 8
RB = 4
UP = 8


def tiles_of(T):
    n = KE * T // P + E - 1
    return -(-n // U) * U


def region(T):
    return -(-(T // P + E) // 16) * 16 * P


def route(nc, R, T, w_loader):
    NT = T // P
    RT = region(T)
    with ExitStack() as ctx:
        def sb(name, shape, dt=F32):
            return ctx.enter_context(nc.sbuf_tensor("r_" + name, shape, dt))

        def sem(name):
            return ctx.enter_context(nc.semaphore("r_" + name))

        iota_i = sb("iota_i", [P, E + tiles_of(T)], I32)
        iota = sb("iota", [P, E + tiles_of(T)])
        count = sb("count", [P, E])
        cnt_i = sb("cnt_i", [P, E], I32)
        ntile = sb("ntile", [P, E])
        tb = sb("tb", [P, E])
        jump = sb("jump", [P, E])
        e_f, off_f, tmp_f = (sb(n, [P, tiles_of(T)]) for n in ("e_f", "off_f", "tmp_f"))
        const = sem("const")
        step = sem("step")
        w_in, w_hi, w_lo = [sem(f"w_in{k}") for k in range(RB)], sem("w_hi"), sem("w_lo")
        wm_turned, wm_diag, wm_wide, scaled = sem("wm_turned"), sem("wm_diag"), sem("wm_wide"), sem("scaled")
        wm = sb("wm", [P, 3])
        ones = sb("ones", [3, P])
        wm_col = sb("wm_col", [3, 1])
        diag = sb("diag", [3, 3])
        sbank = ctx.enter_context(nc.psum_tensor("r_sbank", [P, 512], F32))

        w_src, raw = w_loader
        parts = [(e, k) for e in range(E) for k in range(3)]

        def part_of(which, e, k):
            return R[which][:, e * WE + k * 1024:e * WE + (k + 1) * 1024]

        with nc.Block() as block:
            @block.sync
            def _(sp):
                for n, (e, k) in enumerate(parts):
                    if n >= RB:
                        sp.wait_ge(w_lo, n - RB + 1)
                    sp.dma_start(raw[:, n % RB, :].rearrange("p (c f) -> p c f", c=2 if k < 2 else 4), w_src[k][e]).then_inc(w_in[n % RB], 16)

            @block.gpsimd
            def _(pool):
                nc.gpsimd.memset(ones[:], 1.0).then_inc(const, 1)
                pool.wait_ge(const, 1)
                nc.gpsimd.iota(iota_i[:, 0:E], pattern=[[RT, E]], base=0, channel_multiplier=0).then_inc(const, 1)
                pool.wait_ge(const, 2)
                nc.gpsimd.iota(iota_i[:, E:], pattern=[[1, tiles_of(T)]], base=0, channel_multiplier=0).then_inc(const, 1)

            @block.tensor
            def _(pe):
                pe.wait_ge(wm_diag, 1)
                nc.tensor.transpose(sbank[0:3, 0:P], wm[:], R["ident"][:]).then_inc(wm_turned, 1)
                pe.wait_ge(wm_diag, 2)
                pe.wait_ge(const, 1)
                nc.tensor.matmul(sbank[:, P:P + 3], ones[:], diag[:], start=True, stop=True).then_inc(wm_wide, 1)

            @block.scalar
            def _(act):
                def split_hi(n):
                    e, k = parts[n]
                    act.wait_ge(w_in[n % RB], 16 * (n // RB + 1))
                    nc.scalar.activation(part_of("hi", e, k), raw[:, n % RB, :], ACT.Copy, scale=R["w_scale"][:, k:k + 1]).then_inc(w_hi, 1)
                act.wait_ge(scaled, 1)
                for n in range(len(parts)):
                    split_hi(n)

            @block.vector
            def _(dve):
                ve = nc.vector
                done = [0]

                def chain(ins):
                    done[0] += 1
                    ins.then_inc(step, 1)
                    dve.wait_ge(step, done[0])

                def split_lo(n):
                    e, k = parts[n]
                    dve.wait_ge(w_hi, n + 1)
                    ve.scalar_tensor_tensor(out=part_of("lo", e, k), in0=raw[:, n % RB, :], scalar=R["w_scale"][:, k:k + 1],
                                            in1=part_of("hi", e, k), op0=ALU.mult, op1=ALU.subtract).then_inc(w_lo, 1)

                chain(ve.reduce_max(wm[:], R["w_max"][:].rearrange("p (k n) -> p k n", k=3), AX_X))
                ve.tensor_scalar(wm[:], wm[:], 2.0 ** -100, None, ALU.max).then_inc(wm_diag, 1)
                dve.wait_ge(wm_turned, 1)
                chain(ve.reduce_max(wm_col[:], sbank[0:3, 0:P], AX_X))
                ve.tensor_scalar(diag[:], R["ident"][0:3, 0:3], wm_col[:], None, ALU.mult).then_inc(wm_diag, 1)
                dve.wait_ge(wm_wide, 1)
                chain(ve.tensor_copy(wm[:], sbank[:, P:P + 3]))
                chain(ve.tensor_scalar(wm[:].bitcast(I32), wm[:].bitcast(I32), 23, None, ALU.arith_shift_right))
                chain(ve.tensor_scalar(wm[:].bitcast(I32), wm[:].bitcast(I32), 23, None, ALU.logical_shift_left))
                chain(ve.reciprocal(R["w_scale"][:], wm[:]))
                inv = R["w_scale"]
                chain(ve.tensor_scalar(R["g_scale"][:], wm[:, 0:1], 2.0 ** -13 / XS, None, ALU.mult))
                chain(ve.tensor_scalar(R["u_scale"][:], inv[:, 0:1], 2.0 ** -16 / XS, None, ALU.mult))
                chain(ve.tensor_scalar(R["y_scale"][:], wm[:, 0:1], wm[:, 1:2], 2.0 ** -10, ALU.mult, ALU.mult))
                chain(ve.tensor_scalar(R["y_scale"][:], R["y_scale"][:], wm[:, 2:3], None, ALU.mult))
                chain(ve.tensor_tensor(R["y_scale2"][:], R["y_scale"][:], R["y_scale"][:], ALU.mult))
                ve.tensor_scalar(inv[:], inv[:], 2.0 ** 13, None, ALU.mult).then_inc(scaled, 1)
                dve.wait_ge(const, 3)
                chain(ve.tensor_copy(iota[:], iota_i[:]))
                chain(ve.tensor_tensor(count[:], R["place"][:], iota[:, 0:E], ALU.subtract))
                chain(ve.tensor_scalar(ntile[:], count[:], float(P - 1), None, ALU.add))
                chain(ve.tensor_copy(cnt_i[:], ntile[:]))
                chain(ve.tensor_scalar(cnt_i[:], cnt_i[:], 7, None, ALU.arith_shift_right))
                chain(ve.tensor_copy(ntile[:], cnt_i[:]))
                chain(ve.memset(tb[:, 0:1], 0.0))
                it = iota[:, E:]
                chain(ve.memset(e_f[:], 0.0))
                chain(ve.tensor_scalar(off_f[:], it, float(P), None, ALU.mult))
                for n in range(len(parts)):
                    split_lo(n)
                    e = n % E
                    if 0 < n < E:
                        chain(ve.tensor_tensor(tb[:, e:e + 1], tb[:, e - 1:e], ntile[:, e - 1:e], ALU.add))
                    elif n == E:
                        chain(ve.tensor_scalar(jump[:], ntile[:], float(-P), float(RT), ALU.mult, ALU.add))
                    elif E < n < 2 * E:
                        chain(ve.scalar_tensor_tensor(out=e_f[:], in0=it, scalar=tb[:, e:e + 1], in1=e_f[:], op0=ALU.is_ge, op1=ALU.add))
                        chain(ve.tensor_scalar(tmp_f[:], it, tb[:, e:e + 1], jump[:, e - 1:e], ALU.is_ge, ALU.mult))
                        chain(ve.tensor_tensor(off_f[:], off_f[:], tmp_f[:], ALU.add))
                chain(ve.tensor_scalar(R["tile_e"][:], e_f[:], float(WE), None, ALU.mult))
                chain(ve.tensor_copy(R["tile_off"][:], off_f[:]))
                dve.wait_ge(w_lo, len(parts))


def experts(nc, R, table_d, xn2_d, pair_d, x2_d, T):
    NTL = tiles_of(T)
    RT = region(T)
    with ExitStack() as ctx:
        def sb(name, shape, dt=F32):
            return ctx.enter_context(nc.sbuf_tensor("e_" + name, shape, dt))

        def sem(name):
            return ctx.enter_context(nc.semaphore("e_" + name))

        pair = sb("pair", [P, U, 4], I32)
        xg = sb("xg", [P, 4, 512], F16)
        x_t = sb("x_t", [P, 2, 512], F16)
        sg = sb("sg", [P, 2, F])
        h = sb("h", [P, 2, F])
        h_s = sb("h_s", [P, 2, 2, F], F16)
        h_t = sb("h_t", [P, 2, 2, F], F16)
        yw = sb("yw", [P, 4, 256])
        ident16 = sb("ident16", [P, P], F16)
        ps_x = ctx.enter_context(nc.psum_tensor("ps_x", [P, 2, 512], F16))
        ps_h = ctx.enter_context(nc.psum_tensor("ps_h", [P, 2 * F], F16))
        ps_g = [ctx.enter_context(nc.psum_tensor(f"ps_g{i}", [P, 512], F32)) for i in range(2)]
        ps_u = [ctx.enter_context(nc.psum_tensor(f"ps_u{i}", [P, 512], F32)) for i in range(2)]
        ps_y = [ctx.enter_context(nc.psum_tensor(f"ps_y{i}", [P, 512], F32)) for i in range(2)]

        pair_in = [sem(f"pair_in{k}") for k in range(U)]
        x_in, stored = [sem(f"x_in{k}") for k in range(4)], [sem(f"stored{k}") for k in range(4)]
        xt_full, xt_free = sem("xt_full"), sem("xt_free")
        g_full, u_full, sg_done, h_done = sem("g_full"), sem("u_full"), sem("sg_done"), sem("h_done")
        passed, ident_done = sem("passed"), sem("ident_done")
        h_hi, h_lo, ht_full, ht_done = sem("h_hi"), sem("h_lo"), sem("ht_full"), sem("ht_done")
        y_full, yw_done = sem("y_full"), sem("yw_done")

        def wait(eng, s, value):
            if not (isinstance(value, int) and value <= 0):
                eng.wait_ge(s, value)

        def steps(eng, body, once=None):
            for k in range(U):
                body(k, k, 0)
            if once:
                once()
            with eng.Fori(1, NTL // U - 1) as o:
                for k in range(U):
                    body(o * U + k, k, o)
            for k in range(U):
                body(NTL - U + k, k, NTL // U - 1)

        def no(i, past):
            return isinstance(i, int) and not 0 <= past < NTL

        with nc.Block() as block:
            @block.sync
            def _(sp):
                def body(i, k, o):
                    off = sp.value_load(R["tile_off"][0:1, bass.ds(i, 1)], min_val=0, max_val=E * RT - P)
                    wait(sp, stored[k % 4], 16 * (2 * o + k // 4 - 1))
                    sp.dma_start(pair[:, k, :], table_d[bass.ds(off, P), :]).then_inc(pair_in[k], 16)
                def rows_ahead():
                    for n in range(ahead(T)):
                        sp.dma_start(R["x2_ahead"][:, n], x2_d[n * 512:(n + 1) * 512, :].rearrange("(t p) h -> p t h", p=P)).then_inc(R["x2_ahead_in"], 16)

                steps(sp, body, rows_ahead)

            @block.gpsimd
            def _(pool):
                def gather(i, k, o):
                    pool.wait_ge(pair_in[k], 16 * (o + 1))
                    wait(pool, xt_full, i - 3)
                    carry(pool, passed)
                    pool.indirect_dma_start(xg[:, k % 4, :], None, xn2_d,
                                            bass.IndirectOffsetOnAxis(ap=pair[:, k, 0:1], axis=0)).then_inc(x_in[k % 4], 16)

                def body(o):
                    i = o * U
                    for k in range(U):
                        if not no(i, i + k + 3 if isinstance(i, int) else 0):
                            gather(i + k + 3, (k + 3) % U, o + (k + 3) // U)
                        pool.wait_ge(yw_done, i + k + 1)
                        carry(pool, passed)
                        pool.indirect_dma_start(pair_d, bass.IndirectOffsetOnAxis(ap=pair[:, k, 2:3], axis=0),
                                                yw[:, k % 4, :], None).then_inc(stored[k % 4], 16)
                for k in range(3):
                    gather(k, k, 0)
                body(0)
                with pool.Fori(1, NTL // U - 1) as o:
                    body(o)
                body(NTL // U - 1)
                for k in range(4):
                    pool.wait_ge(stored[k], 16 * NTL // 4)

            @block.tensor
            def _(pe):
                te = nc.tensor

                def x_turn(i, k, o):
                    pe.wait_ge(x_in[k % 4], 16 * (o * (UP // 4) + k // 4 + 1))
                    wait(pe, xt_free, i)
                    for c in range(4):
                        last = te.transpose(ps_x[:, k % 2, c * P:(c + 1) * P], xg[:, k % 4, c * P:(c + 1) * P], ident16[:])
                    last.then_inc(xt_full, 1)

                def weight(part, e, which, cols):
                    return R[part][:, bass.ds(e + (which * 1024 + cols.start), cols.stop - cols.start)]

                def project(i, k, e, which, ps, full, used):
                    wait(pe, used, i - 1)
                    out = ps[k % 2][:]
                    for c in range(2):
                        x_hi, x_lo = (x_t[:, k % 2, (2 * a + c) * P:(2 * a + c + 1) * P] for a in range(2))
                        cols = slice(c * F, (c + 1) * F)
                        te.matmul(out, x_hi, weight("hi", e, which, cols), start=(c == 0), stop=False)
                        te.matmul(out, x_lo, weight("hi", e, which, cols), start=False, stop=False)
                        last = te.matmul(out, x_hi, weight("lo", e, which, cols), start=False, stop=(c == 1))
                    last.then_inc(full, 1)

                def h_turn(i, k):
                    pe.wait_ge(h_lo, i + 1)
                    wait(pe, ht_done, i)
                    for a in range(2):
                        for c in range(4):
                            last = te.transpose(ps_h[:, a * F + c * P:a * F + (c + 1) * P], h_s[:, k % 2, a, c * P:(c + 1) * P], ident16[:])
                    last.then_inc(ht_full, 1)

                def first_weight(i):
                    return pe.value_load(R["tile_e"][0:1, bass.ds(i, 1)], min_val=0, max_val=(E - 1) * WE)

                def down(i, k, e):
                    pe.wait_ge(ht_done, i + 1)
                    wait(pe, yw_done, i - 1)
                    out = ps_y[k % 2][:, 0:256]
                    for c in range(4):
                        hh_, hl_ = (h_t[:, k % 2, a, c * P:(c + 1) * P] for a in range(2))
                        cols = slice(c * 256, (c + 1) * 256)
                        te.matmul(out, hh_, weight("hi", e, 2, cols), start=(c == 0), stop=False)
                        te.matmul(out, hl_, weight("hi", e, 2, cols), start=False, stop=False)
                        last = te.matmul(out, hh_, weight("lo", e, 2, cols), start=False, stop=(c == 3))
                    last.then_inc(y_full, 1)

                def body(o):
                    i = o * UP
                    e = first_weight(i)
                    last_e = None if no(i, i - 1 if isinstance(i, int) else 0) else first_weight(i - 1)
                    for k in range(UP):
                        past = not no(i, i + k - 1 if isinstance(i, int) else 0)
                        if not no(i, i + k + 1 if isinstance(i, int) else 0):
                            x_turn(i + k + 1, (k + 1) % UP, o + (k + 1) // UP)
                        pe.wait_ge(xt_free, i + k + 1)
                        project(i + k, k, e, 0, ps_g, g_full, sg_done)
                        if past:
                            h_turn(i + k - 1, (k - 1) % UP)
                        project(i + k, k, e, 1, ps_u, u_full, h_done)
                        next_e = first_weight(i + k + 1) if k < UP - 1 else None
                        if past:
                            down(i + k - 1, (k - 1) % UP, last_e)
                        last_e, e = e, next_e
                pe.wait_ge(ident_done, 1)
                x_turn(0, 0, 0)
                body(0)
                with pe.Fori(1, NTL // UP - 1) as o:
                    body(o)
                body(NTL // UP - 1)
                h_turn(NTL - 1, UP - 1)
                down(NTL - 1, UP - 1, first_weight(NTL - 1))

            @block.scalar
            def _(act):
                sc = nc.scalar

                def x_copy(i, k):
                    act.wait_ge(xt_full, i + 1)
                    wait(act, u_full, i - 1)
                    sc.activation(x_t[:, k % 2, :], ps_x[:, k % 2, :], ACT.Copy).then_inc(xt_free, 1)

                def weighted(i, k, o):
                    act.wait_ge(y_full, i + 1)
                    wait(act, stored[k % 4], 16 * (2 * o + k // 4))
                    sc.activation(yw[:, k % 4, :], ps_y[k % 2][:, 0:256], ACT.Copy,
                                  scale=pair[:, k, 1:2].bitcast(F32)).then_inc(yw_done, 1)

                def high(i, k):
                    act.wait_ge(h_done, i + 1)
                    wait(act, ht_full, i - 1)
                    sc.activation(h_s[:, k % 2, 0, :], h[:, k % 2, :], ACT.Copy).then_inc(h_hi, 1)

                def body(i, k, o):
                    if not no(i, i - 1 if isinstance(i, int) else 0):
                        high(i - 1, (k - 1) % U)
                    if not no(i, i - 2 if isinstance(i, int) else 0):
                        weighted(i - 2, (k - 2) % U, o if k >= 2 else o - 1)
                    if not no(i, i + 1 if isinstance(i, int) else 0):
                        x_copy(i + 1, (k + 1) % U)
                    act.wait_ge(g_full, i + 1)
                    wait(act, h_done, i - 1)
                    sc.activation(sg[:, k % 2, :], ps_g[k % 2][:], ACT.Silu, scale=R["g_scale"][:]).then_inc(sg_done, 1)
                x_copy(0, 0)
                steps(act, body)
                high(NTL - 1, U - 1)
                for k in (U - 2, U - 1):
                    weighted(NTL - U + k, k, NTL // U - 1)

            @block.vector
            def _(dve):
                ve = nc.vector
                ve.tensor_copy(ident16[:], R["ident"][:]).then_inc(ident_done, 1)

                def hidden(i, k):
                    dve.wait_ge(u_full, i + 1)
                    dve.wait_ge(sg_done, i + 1)
                    wait(dve, h_lo, i - 1)
                    ve.scalar_tensor_tensor(out=h[:, k % 2, :], in0=ps_u[k % 2][:], scalar=R["u_scale"][:], in1=sg[:, k % 2, :],
                                            op0=ALU.mult, op1=ALU.mult).then_inc(h_done, 1)
                    dve.wait_ge(h_hi, i + 1)
                    ve.tensor_tensor(h_s[:, k % 2, 1, :], h[:, k % 2, :], h_s[:, k % 2, 0, :], ALU.subtract).then_inc(h_lo, 1)
                    dve.wait_ge(ht_full, i + 1)
                    wait(dve, y_full, i - 1)
                    ve.tensor_copy(h_t[:, k % 2, :, :].rearrange("p a f -> p (a f)"), ps_h[:]).then_inc(ht_done, 1)

                steps(dve, lambda i, k, o: hidden(i, k))


def ahead(T):
    return min(T // 512, 12)


def finish(nc, R, pair_d, x2_d, out, T):
    N, D = T // 512, 3
    with ExitStack() as ctx:
        def sb(name, shape, dt=F32):
            return ctx.enter_context(nc.sbuf_tensor("f_" + name, shape, dt))

        def sem(name):
            return ctx.enter_context(nc.semaphore("f_" + name))

        acc, xs = sb("acc", [P, D, KE, 4, 256]), sb("xs", [P, D, 4, 256])
        s, o = sb("s", [P, D, 4, 256]), sb("o", [P, D, 4, 256])
        raw, st, rs = sb("raw", [P, D, 4, 6]), sb("st", [P, D, 4, 2]), sb("rs", [P, D, 4])
        nb = sb("nb", [P, D, 4])
        acc_in, xs_in = [sem(f"acc_in{k}") for k in range(D)], [sem(f"xs_in{k}") for k in range(D)]
        out_done = [sem(f"out_done{k}") for k in range(D)]
        added, bn, agg, rstd, shift = sem("added"), sem("bn"), sem("agg"), sem("rstd"), sem("shift")
        normed, summed = sem("normed"), sem("summed")

        def rows(dram, i):
            return dram[i * 512:(i + 1) * 512, :].rearrange("(t p) h -> p t h", p=P)

        with nc.Block() as block:
            @block.sync
            def _(sp):
                for i in range(N):
                    if i >= D:
                        sp.wait_ge(added, i - D + 1)
                    for k in range(KE):
                        sp.dma_start(acc[:, i % D, k], rows(pair_d[k * T:(k + 1) * T, :], i)).then_inc(acc_in[i % D], 16)
                    if i >= ahead(T):
                        if i >= D:
                            sp.wait_ge(summed, i - D + 1)
                        sp.dma_start(xs[:, i % D], rows(x2_d, i)).then_inc(xs_in[i % D], 16)

            @block.gpsimd
            def _(pool):
                def rstd_of(i):
                    r_ = rs[:, i % D, :]
                    pool.wait_ge(agg, 4 * (i + 1))
                    if i >= D:
                        pool.wait_ge(normed, 4 * (i - D + 1))
                    nc.gpsimd.tensor_scalar(r_, st[:, i % D, :, 1], R["y_scale2"][:], EPS, ALU.mult, ALU.add).then_inc(rstd, 1)
                    pool.wait_ge(rstd, 3 * i + 1)
                    nc.gpsimd.tensor_tensor(r_, r_, R["neg_half"][:], ALU.pow).then_inc(rstd, 1)
                    pool.wait_ge(rstd, 3 * i + 2)
                    nc.gpsimd.tensor_scalar(r_, r_, R["y_scale"][:], None, ALU.mult).then_inc(rstd, 1)

                def total(i):
                    pool.wait_ge(normed, 4 * (i + 1))
                    if i < ahead(T):
                        pool.wait_ge(R["x2_ahead_in"], 16 * ahead(T))
                        x2 = R["x2_ahead"][:, i]
                    else:
                        pool.wait_ge(xs_in[i % D], 16 * len([n for n in range(ahead(T), i + 1) if n % D == i % D]))
                        x2 = xs[:, i % D]
                    if i >= D:
                        pool.wait_ge(out_done[i % D], 16 * (i // D))
                    nc.gpsimd.tensor_tensor(o[:, i % D], s[:, i % D], x2, ALU.add).then_inc(summed, 1)

                for i in range(N):
                    rstd_of(i)
                    if i >= 1:
                        total(i - 1)
                total(N - 1)

            @block.vector
            def _(dve):
                def shifts(i):
                    dve.wait_ge(rstd, 3 * (i + 1))
                    nc.vector.scalar_tensor_tensor(out=nb[:, i % D, :], in0=st[:, i % D, :, 0], scalar=-1.0, in1=rs[:, i % D, :],
                                                   op0=ALU.mult, op1=ALU.mult).then_inc(shift, 1)

                for i in range(N):
                    dve.wait_ge(acc_in[i % D], 16 * KE * (i // D + 1))
                    if i >= D:
                        dve.wait_ge(summed, i - D + 1)
                    nc.vector.tensor_tensor(s[:, i % D], acc[:, i % D, 0], acc[:, i % D, 1], ALU.add).then_inc(added, 1)
                    dve.wait_ge(added, i + 1)
                    for t in range(4):
                        nc.vector.bn_stats(raw[:, i % D, t, :], s[:, i % D, t, :]).then_inc(bn, 1)
                    for t in range(4):
                        dve.wait_ge(bn, 4 * i + t + 1)
                        nc.vector.bn_aggr(st[:, i % D, t, :], raw[:, i % D, t, :]).then_inc(agg, 1)
                    if i >= 1:
                        shifts(i - 1)
                shifts(N - 1)

            @block.scalar
            def _(act):
                def store(i):
                    act.wait_ge(summed, i + 1)
                    act.dma_start(rows(out, i), o[:, i % D]).then_inc(out_done[i % D], 16)

                for i in range(N):
                    act.wait_ge(shift, i + 1)
                    for t in range(4):
                        nc.scalar.activation(s[:, i % D, t, :], s[:, i % D, t, :], ACT.Identity,
                                             bias=nb[:, i % D, t:t + 1], scale=rs[:, i % D, t:t + 1]).then_inc(normed, 1)
                    if i >= 1:
                        store(i - 1)
                store(N - 1)
                for k in range(D):
                    act.wait_ge(out_done[k], 16 * len(range(k, N, D)))


def build(nc, x, gamma, beta, w_qkv, b_qkv, w_out, b_out, router, w_gate, w_up, w_down, out):
    B, S, H = x.shape
    T = B * S
    RT = region(T)

    def dram(name, shape, dt=F32):
        return nc.dram_tensor(name, shape, dt).ap()

    y_d, x2_d = dram("y_d", [T, H]), dram("x2_d", [T, H])
    xn2_d = dram("xn2_d", [T + P, 2 * H], F16)
    pair_d = dram("pair_d", [KE * T + E * 512, H])
    qk_d, mt_d = dram("qk_d", [4, H, S]), dram("mt_d", [2, HG * S])
    table_d = dram("table_d", [E * RT, 4], I32)

    with ExitStack() as outer:
        def sb(name, shape, dt=F32):
            return outer.enter_context(nc.sbuf_tensor(name, shape, dt))
        ident, neg_half = sb("ident", [P, P]), sb("neg_half", [P, 4])
        w_max = sb("w_max", [P, 12])
        place = sb("place", [P, E])
        w_src = [[w[e].rearrange("(c p) f -> p c f", p=P) for e in range(E)] for w in (w_gate, w_up, w_down)]
        cleared = outer.enter_context(nc.semaphore("cleared"))
        with ExitStack() as ctx:
            W = shared(nc, ctx)
            W["ident"], W["neg_half"], W["place"] = ident, neg_half, place
            prepare_weights(nc, W, x, w_qkv, b_qkv, w_out, b_out, gamma, beta, xn2_d, table_d, cleared)
            attention(nc, W, x, y_d, x2_d, xn2_d, table_d, qk_d, mt_d, router, w_src, w_max, (cleared, 16 * clears(T)))
        with ExitStack() as ctx:
            def sc(name, shape, dt=F32):
                return ctx.enter_context(nc.sbuf_tensor(name, shape, dt))
            R = {"ident": ident, "neg_half": neg_half, "w_max": w_max, "place": place,
                 "w_scale": sc("w_scale", [P, 3]), "g_scale": sc("g_scale", [P, 1]), "u_scale": sc("u_scale", [P, 1]),
                 "y_scale": sc("y_scale", [P, 1]), "y_scale2": sc("y_scale2", [P, 1]),
                 "x2_ahead": sc("x2_ahead", [P, ahead(T), 4, 256]), "x2_ahead_in": ctx.enter_context(nc.semaphore("x2_ahead_in")),
                 "tile_e": sc("tile_e", [P, tiles_of(T)], I32), "tile_off": sc("tile_off", [P, tiles_of(T)], I32)}
            with ExitStack() as weights:
                for part in ("hi", "lo"):
                    R[part] = weights.enter_context(nc.sbuf_tensor(f"we_{part}", [P, E * WE], F16))
                with ExitStack() as inner:
                    raw = inner.enter_context(nc.sbuf_tensor("we_raw", [P, RB, 1024], F32))
                    route(nc, R, T, (w_src, raw))
                experts(nc, R, table_d, xn2_d, pair_d, x2_d, T)
            finish(nc, R, pair_d, x2_d, out, T)


_INS = ["hidden_states", "ln_gamma", "ln_beta", "W_qkv", "b_qkv", "W_out", "b_out"]
_NAMES = ["L0_attn_" + n for n in _INS] + ["L0_ffn_router_kernel_DE", "L0_ffn_kernel_gating_EDF",
                                          "L0_ffn_kernel_up_EDF", "L0_ffn_kernel_down_EFD"]


def kernel(**inputs):
    import numpy as _np
    import concourse.bacc as _bacc
    from concourse import mybir as _mybir
    from concourse.bass_utils import run_bass_kernel_spmd as _run

    nc = _bacc.Bacc("TRN2", target_bir_lowering=False, num_devices=1)
    arrays, args = {}, []
    for name in _NAMES:
        a = _np.ascontiguousarray(inputs[name])
        arrays[f"in_{name}"] = a
        args.append(nc.dram_tensor(f"in_{name}", a.shape, _mybir.dt.from_np(a.dtype), kind="ExternalInput").ap())
    x = args[0]
    out = nc.dram_tensor("out", [x.shape[0] * x.shape[1], x.shape[2]], _mybir.dt.float32, kind="ExternalOutput").ap()
    x, gamma, beta, w_qkv, b_qkv, w_out, b_out, router, w_gate, w_up, w_down = args
    build(nc, x, gamma, beta, w_qkv, b_qkv, w_out, b_out, router, w_gate, w_up, w_down, out)
    r = _run(nc, [arrays], core_ids=[0])
    return r.results[0]["out"].reshape(inputs[_NAMES[0]].shape)
```
